# Optimizing a Trainium2 kernel written in Bass

```python
import numpy as np
import jax
import jax.numpy as jnp

def _softmax(x, axis=-1):
    return jax.nn.softmax(x, axis=axis)

def _gelu(x):
    return jax.nn.gelu(x, approximate=True)

def _silu(x):
    return jax.nn.silu(x)

def _sigmoid(x):
    return jax.nn.sigmoid(x)

def _layernorm(x, axis=-1, eps=1e-05):
    m = jnp.mean(x, axis=axis, keepdims=True)
    v = jnp.var(x, axis=axis, keepdims=True)
    return (x - m) / jnp.sqrt(v + eps)

def _scatter_add(tgt, idx, src, axis=0):
    return tgt.at[idx].add(src)

def _segment_sum(src, seg, n):
    return jax.ops.segment_sum(src, seg, n)
kernel_name = 'mk_cond_seq_d2_seqx_r4_76353a'

def setup_inputs(seed: int=0):
    np.random.seed(seed)
    _w = jnp.asarray

    def _rec_inputs():
        import jax
        import jax.numpy as jnp
        _rk = jax.random.key(seed)
        x = -0.0003929 + 0.9999 * jax.random.normal(jax.random.fold_in(_rk, 1), (64, 64, 512), jnp.float32)
        _lenS = 64 - jax.random.randint(jax.random.fold_in(_rk, 7), (64,), 0, max(1, 64 // 4) + 1, jnp.int32)
        _lenS2 = 64 - jax.random.randint(jax.random.fold_in(_rk, 8), (64,), 0, max(1, 64 // 4) + 1, jnp.int32)
        pos_BxS = jnp.broadcast_to(jnp.arange(64, dtype=jnp.int32), (64, 64))
        cond_2048 = 0.00782532 + 1.00527 * jax.random.normal(jax.random.fold_in(_rk, 12), (64, 512), jnp.float32)
        _validS = jnp.arange(64)[None, :] < _lenS[:, None]
        _validS2 = jnp.arange(64)[None, :] < _lenS2[:, None]
        _causal = jnp.tril(jnp.ones((64, 64), dtype=bool))
        mask_1x1xSxS_ff0 = jnp.where(jnp.ones((1, 1, 64, 64), dtype=bool), 0.0, -1000000000.0).astype(jnp.float32)
        return (x, pos_BxS, cond_2048, mask_1x1xSxS_ff0)
    x, pos_BxS, cond_2048, mask_1x1xSxS_ff0 = _rec_inputs()

    def _L0_cond_setup():
        import jax, jax.numpy as jnp
        import numpy as np
        HIDDEN, NQ, NKV, HD, INTER = (512, 8, 1, 64, 2048)
        B, S = (4, 512)
        EPS = 1e-06
        ROPE_BASE = 10000.0

        def ada_rms(x, t, w, tw):
            n = x * jax.lax.rsqrt(jnp.mean(jnp.square(x), axis=-1, keepdims=True) + EPS)
            scale = t @ tw.T
            return n * (w * (1.0 + scale))[:, None, :]

        def apply_rope(x, pos_ids):
            half = HD // 2
            inv_freq = 1.0 / ROPE_BASE ** (jnp.arange(0, HD, 2, dtype=jnp.float32) / HD)
            ang = pos_ids.astype(jnp.float32)[:, :, None] * inv_freq
            cos = jnp.concatenate([jnp.cos(ang), jnp.cos(ang)], axis=-1)[:, None]
            sin = jnp.concatenate([jnp.sin(ang), jnp.sin(ang)], axis=-1)[:, None]
            x1, x2 = (x[..., :half], x[..., half:])
            rot = jnp.concatenate([-x2, x1], axis=-1)
            return x * cos + rot * sin
        key = jax.random.key(seed)
        ks = jax.random.split(key, 12)
        f32 = jnp.float32
        inp = {'x': jax.random.normal(ks[0], (B, S, HIDDEN), f32), 'pos_ids': jnp.broadcast_to(jnp.arange(S, dtype=jnp.int32), (B, S)), 'time_emb': jax.random.normal(ks[1], (B, HIDDEN), f32), 'ln1_w': jnp.ones((HIDDEN,), f32), 'ln1_tw': jax.random.normal(ks[2], (HIDDEN, HIDDEN), f32) * 0.02, 'ln2_w': jnp.ones((HIDDEN,), f32), 'ln2_tw': jax.random.normal(ks[3], (HIDDEN, HIDDEN), f32) * 0.02, 'Wq': jax.random.normal(ks[4], (NQ * HD, HIDDEN), f32) * 0.02, 'Wk': jax.random.normal(ks[5], (NKV * HD, HIDDEN), f32) * 0.02, 'Wv': jax.random.normal(ks[6], (NKV * HD, HIDDEN), f32) * 0.02, 'Wo': jax.random.normal(ks[7], (HIDDEN, NQ * HD), f32) * 0.02, 'Wg': jax.random.normal(ks[8], (INTER, HIDDEN), f32) * 0.02, 'Wu': jax.random.normal(ks[9], (INTER, HIDDEN), f32) * 0.02, 'Wd': jax.random.normal(ks[10], (HIDDEN, INTER), f32) * 0.02}
        return inp
    _L0_cond_all = _L0_cond_setup()
    _L0_cond_in = {k: v for k, v in _L0_cond_all.items() if k in ('ln1_w', 'ln1_tw', 'ln2_w', 'ln2_tw', 'Wq', 'Wk', 'Wv', 'Wo', 'Wg', 'Wu', 'Wd')}
    del _L0_cond_all

    def _L1_cond_setup():
        import jax, jax.numpy as jnp
        import numpy as np
        B, L, C, H = (2, 512, 512, 16)
        COND = 512
        HID = 4 * C
        LN_EPS = 1e-06

        def _ln(x):
            m = jnp.mean(x, axis=-1, keepdims=True)
            v = jnp.mean((x - m) ** 2, axis=-1, keepdims=True)
            return (x - m) / jnp.sqrt(v + LN_EPS)

        def _gelu_tanh(u):
            c = np.sqrt(2.0 / np.pi).astype(np.float32)
            return 0.5 * u * (1.0 + jnp.tanh(c * (u + 0.044715 * u ** 3)))
        key = jax.random.key(seed)
        ks = jax.random.split(key, 8)
        s = 0.02
        return {'x': jax.random.normal(ks[0], (B, L, C), jnp.float32), 'cond_BD': jax.random.normal(ks[1], (B, COND), jnp.float32), 'attn_bias': jnp.zeros((1, 1, L, L), jnp.float32), 'Wqkv': jax.random.normal(ks[2], (3 * C, C), jnp.float32) * s, 'q_bias': jnp.zeros((C,), jnp.float32), 'v_bias': jnp.zeros((C,), jnp.float32), 'scale_mul_log': jnp.full((1, H, 1, 1), np.log(4.0), jnp.float32), 'Wproj': jax.random.normal(ks[3], (C, C), jnp.float32) * s, 'bproj': jnp.zeros((C,), jnp.float32), 'Wada': jax.random.normal(ks[4], (6 * C, COND), jnp.float32) * s, 'bada': jnp.zeros((6 * C,), jnp.float32), 'Wfc1': jax.random.normal(ks[5], (HID, C), jnp.float32) * s, 'bfc1': jnp.zeros((HID,), jnp.float32), 'Wfc2': jax.random.normal(ks[6], (C, HID), jnp.float32) * s, 'bfc2': jnp.zeros((C,), jnp.float32)}
    _L1_cond_all = _L1_cond_setup()
    _L1_cond_in = {k: v for k, v in _L1_cond_all.items() if k in ('Wqkv', 'q_bias', 'v_bias', 'scale_mul_log', 'Wproj', 'bproj', 'Wada', 'bada', 'Wfc1', 'bfc1', 'Wfc2', 'bfc2')}
    del _L1_cond_all
    return {'x': x, 'pos_BxS': pos_BxS, 'cond_2048': cond_2048, 'mask_1x1xSxS_ff0': mask_1x1xSxS_ff0, 'L0_cond_ln1_w': _L0_cond_in['ln1_w'], 'L0_cond_ln1_tw': _L0_cond_in['ln1_tw'], 'L0_cond_ln2_w': _L0_cond_in['ln2_w'], 'L0_cond_ln2_tw': _L0_cond_in['ln2_tw'], 'L0_cond_Wq': _L0_cond_in['Wq'], 'L0_cond_Wk': _L0_cond_in['Wk'], 'L0_cond_Wv': _L0_cond_in['Wv'], 'L0_cond_Wo': _L0_cond_in['Wo'], 'L0_cond_Wg': _L0_cond_in['Wg'], 'L0_cond_Wu': _L0_cond_in['Wu'], 'L0_cond_Wd': _L0_cond_in['Wd'], 'L1_cond_Wqkv': _L1_cond_in['Wqkv'], 'L1_cond_q_bias': _L1_cond_in['q_bias'], 'L1_cond_v_bias': _L1_cond_in['v_bias'], 'L1_cond_scale_mul_log': _L1_cond_in['scale_mul_log'], 'L1_cond_Wproj': _L1_cond_in['Wproj'], 'L1_cond_bproj': _L1_cond_in['bproj'], 'L1_cond_Wada': _L1_cond_in['Wada'], 'L1_cond_bada': _L1_cond_in['bada'], 'L1_cond_Wfc1': _L1_cond_in['Wfc1'], 'L1_cond_bfc1': _L1_cond_in['bfc1'], 'L1_cond_Wfc2': _L1_cond_in['Wfc2'], 'L1_cond_bfc2': _L1_cond_in['bfc2']}

def reference(x, pos_BxS, cond_2048, mask_1x1xSxS_ff0, L0_cond_ln1_w, L0_cond_ln1_tw, L0_cond_ln2_w, L0_cond_ln2_tw, L0_cond_Wq, L0_cond_Wk, L0_cond_Wv, L0_cond_Wo, L0_cond_Wg, L0_cond_Wu, L0_cond_Wd, L1_cond_Wqkv, L1_cond_q_bias, L1_cond_v_bias, L1_cond_scale_mul_log, L1_cond_Wproj, L1_cond_bproj, L1_cond_Wada, L1_cond_bada, L1_cond_Wfc1, L1_cond_bfc1, L1_cond_Wfc2, L1_cond_bfc2):
    import jax
    import jax.numpy as jnp

    def _L0_cond_ref(x, pos_ids, time_emb, ln1_w, ln1_tw, ln2_w, ln2_tw, Wq, Wk, Wv, Wo, Wg, Wu, Wd):
        import jax, jax.numpy as jnp
        import numpy as np
        HIDDEN, NQ, NKV, HD, INTER = (512, 8, 1, 64, 2048)
        B, S = (4, 512)
        EPS = 1e-06
        ROPE_BASE = 10000.0

        def ada_rms(x, t, w, tw):
            n = x * jax.lax.rsqrt(jnp.mean(jnp.square(x), axis=-1, keepdims=True) + EPS)
            scale = t @ tw.T
            return n * (w * (1.0 + scale))[:, None, :]

        def apply_rope(x, pos_ids):
            half = HD // 2
            inv_freq = 1.0 / ROPE_BASE ** (jnp.arange(0, HD, 2, dtype=jnp.float32) / HD)
            ang = pos_ids.astype(jnp.float32)[:, :, None] * inv_freq
            cos = jnp.concatenate([jnp.cos(ang), jnp.cos(ang)], axis=-1)[:, None]
            sin = jnp.concatenate([jnp.sin(ang), jnp.sin(ang)], axis=-1)[:, None]
            x1, x2 = (x[..., :half], x[..., half:])
            rot = jnp.concatenate([-x2, x1], axis=-1)
            return x * cos + rot * sin
        b, s, _ = x.shape
        g = NQ // NKV
        res = x
        h = ada_rms(x, time_emb, ln1_w, ln1_tw)
        q = (h @ Wq.T).reshape(b, s, NQ, HD).transpose(0, 2, 1, 3)
        k = (h @ Wk.T).reshape(b, s, NKV, HD).transpose(0, 2, 1, 3)
        v = (h @ Wv.T).reshape(b, s, NKV, HD).transpose(0, 2, 1, 3)
        q = apply_rope(q, pos_ids)
        k = apply_rope(k, pos_ids)
        qg = q.reshape(b, NKV, g, s, HD)
        scores = jnp.einsum('bkgsd,bktd->bkgst', qg, k) / jnp.sqrt(jnp.float32(HD))
        attn = jax.nn.softmax(scores, axis=-1)
        ctx = jnp.einsum('bkgst,bktd->bkgsd', attn, v)
        ctx = ctx.reshape(b, NQ, s, HD).transpose(0, 2, 1, 3).reshape(b, s, NQ * HD)
        x = res + ctx @ Wo.T
        res = x
        h = ada_rms(x, time_emb, ln2_w, ln2_tw)
        mlp = jax.nn.silu(h @ Wg.T) * (h @ Wu.T) @ Wd.T
        return res + mlp

    def _L1_cond_ref(x, cond_BD, attn_bias, Wqkv, q_bias, v_bias, scale_mul_log, Wproj, bproj, Wada, bada, Wfc1, bfc1, Wfc2, bfc2):
        import jax, jax.numpy as jnp
        import numpy as np
        B, L, C, H = (2, 512, 512, 16)
        COND = 512
        HID = 4 * C
        LN_EPS = 1e-06

        def _ln(x):
            m = jnp.mean(x, axis=-1, keepdims=True)
            v = jnp.mean((x - m) ** 2, axis=-1, keepdims=True)
            return (x - m) / jnp.sqrt(v + LN_EPS)

        def _gelu_tanh(u):
            c = np.sqrt(2.0 / np.pi).astype(np.float32)
            return 0.5 * u * (1.0 + jnp.tanh(c * (u + 0.044715 * u ** 3)))
        Bs, Lx, Cx = x.shape
        D = Cx // H
        ada = (jax.nn.silu(cond_BD) @ Wada.T + bada).reshape(Bs, 1, 6, Cx)
        gamma1, gamma2, scale1, scale2, shift1, shift2 = [ada[:, :, i, :] for i in range(6)]

        def attn(xin):
            qkv_bias = jnp.concatenate([q_bias, jnp.zeros_like(q_bias), v_bias])
            qkv = (xin @ Wqkv.T + qkv_bias).reshape(Bs, Lx, 3, H, D)
            qkv = jnp.transpose(qkv, (2, 0, 3, 1, 4))
            q, k, v = (qkv[0], qkv[1], qkv[2])
            sm = jnp.exp(jnp.minimum(scale_mul_log, jnp.log(jnp.float32(100.0))))
            qn = q / jnp.maximum(jnp.linalg.norm(q, axis=-1, keepdims=True), 1e-12) * sm
            kn = k / jnp.maximum(jnp.linalg.norm(k, axis=-1, keepdims=True), 1e-12)
            scores = jnp.einsum('bhqd,bhkd->bhqk', qn, kn) + attn_bias
            p = jax.nn.softmax(scores, axis=-1)
            o = jnp.einsum('bhqk,bhkd->bhqd', p, v)
            o = jnp.transpose(o, (0, 2, 1, 3)).reshape(Bs, Lx, Cx)
            return o @ Wproj.T + bproj
        x = x + attn(_ln(x) * (scale1 + 1.0) + shift1) * gamma1
        h = _gelu_tanh((_ln(x) * (scale2 + 1.0) + shift2) @ Wfc1.T + bfc1)
        x = x + (h @ Wfc2.T + bfc2) * gamma2
        return x
    x = _L0_cond_ref(x, pos_BxS, cond_2048, L0_cond_ln1_w, L0_cond_ln1_tw, L0_cond_ln2_w, L0_cond_ln2_tw, L0_cond_Wq, L0_cond_Wk, L0_cond_Wv, L0_cond_Wo, L0_cond_Wg, L0_cond_Wu, L0_cond_Wd)
    x = _L1_cond_ref(x, cond_2048, mask_1x1xSxS_ff0, L1_cond_Wqkv, L1_cond_q_bias, L1_cond_v_bias, L1_cond_scale_mul_log, L1_cond_Wproj, L1_cond_bproj, L1_cond_Wada, L1_cond_bada, L1_cond_Wfc1, L1_cond_bfc1, L1_cond_Wfc2, L1_cond_bfc2)
    return x

_drawn_inputs = setup_inputs


def setup_inputs(seed=0):
    import zlib

    import numpy as np

    out = dict(_drawn_inputs(seed))
    spreads = {'L0_cond_ln1_w': (1.0, 0.6),
     'L0_cond_ln2_w': (1.0, 0.2),
     'L1_cond_q_bias': (0.0, 0.8),
     'L1_cond_v_bias': (0.0, 0.6),
     'L1_cond_scale_mul_log': (1.3862943649291992, 0.6),
     'L1_cond_bproj': (0.0, 0.274),
     'L1_cond_bada': (0.0, 0.1),
     'L1_cond_bfc1': (0.0, 0.519),
     'L1_cond_bfc2': (0.0, 0.285)}
    factors = {'L0_cond_ln1_tw': 3.989, 'L0_cond_Wq': 6.369, 'L0_cond_Wk': 6.37, 'L1_cond_Wqkv': 2.689}
    for name, (base, spread) in spreads.items():
        noise = np.random.default_rng([zlib.crc32(name.encode()), seed]).standard_normal(out[name].shape)
        drawn = base * np.exp(spread * noise) if base else spread * noise
        out[name] = jnp.asarray(drawn.astype(out[name].dtype))
    for name, factor in factors.items():
        out[name] = (out[name] * factor).astype(out[name].dtype)
    return out
```

```python
from contextlib import ExitStack

import concourse.bass as bass
from concourse import mybir

ALU = mybir.AluOpType
ACT = mybir.ActivationFunctionType
F32 = mybir.dt.float32
F16 = mybir.dt.float16
I32 = mybir.dt.int32
AX_X = mybir.AxisListType.X

P = 128
D = 512
KC = D // P
SEQ = 64
NSEQ = 64
BLOCK = 512
TILES = BLOCK // P
NBLK = NSEQ * SEQ // BLOCK
INTER = 2048
IC = INTER // P
HEADS0, HD0 = 8, 64
HEADS1, HD1 = 16, 32
HALF = HEADS1 // 2
QKV0 = D + 2 * HD0
EPS = 1e-6
WS = 16.0
INV = 1.0 / WS
TWO_PI = 6.283185307179586
PI_HIGH = 6.28125
PI_LOW = TWO_PI - PI_HIGH
ROUND = 12582912.0
PI_IN = 3.1415925

SLOTS0 = 24
SLOTS1 = 32


def slot_table(slots, stages, starts, second_norm):
    table = [[] for _ in range(slots)]
    for t, first in enumerate(starts):
        for n, stage in enumerate(stages):
            table[first + n].append((stage, t))
    for t, s in enumerate(second_norm):
        table[s].append(("norm2", t))
    return table


TABLE0 = slot_table(SLOTS0, ["norm1", "proj", "turn", "scores", "turn_p", "mix", "out"],
                    [1, 5, 9, 13], [17, 18, 19, 21])
TABLE1 = slot_table(SLOTS1, ["norm1", "proj", "wait", "turn0", "turn1_scores0", "scores1_turn_p0",
                             "mix0_turn_p1", "mix1", "out"],
                    [0, 7, 14, 21], [16, 17, 23, 30])


def order_of(table, stages):
    return [(s, t) for slot in table for s, t in slot if s in stages]


NORMS0 = order_of(TABLE0, ("norm1", "norm2"))
NORMS1 = order_of(TABLE1, ("norm1", "norm2"))


def layers_kernel(nc, x, pos, cond_t, mask, ln_w, tw_t, wqkv0_t, wo0_t, wg_t, wu_t, wd_t,
                  wqkv1_t, q_bias, v_bias, scale_log, wproj_t, b_proj, wada_t, b_ada, b_ada_row,
                  wfc1_t, b_fc1, wfc2_t, b_fc2, out):
    with ExitStack() as ctx:
        def sb(name, shape, dt):
            return ctx.enter_context(nc.sbuf_tensor(name, shape, dt))

        def sem(name):
            return ctx.enter_context(nc.semaphore(name))

        x_mid = nc.dram_tensor("x_mid", (NSEQ * SEQ, D), F32, kind="Internal").ap()
        rope_dram = nc.dram_tensor("rope_tables", (P, NBLK * TILES, 2, 32), F32, kind="Internal").ap()
        gain0_dram = nc.dram_tensor("gain0", (NBLK, P, 2, KC, 8), F32, kind="Internal").ap()
        mod1_dram = nc.dram_tensor("mod1", (NBLK, P, 4, KC, 8), F32, kind="Internal").ap()
        gamma_dram = nc.dram_tensor("gamma", (2, NSEQ, D), F32, kind="Internal").ap()

        weights = sb("weights", [P, 58368], F16)
        region_a, region_b, region_c = weights[:, 0:32768], weights[:, 32768:49152], weights[:, 49152:58368]

        def cut(ap, k):
            return ap.rearrange("p (h k n) -> p h k n", h=2, k=k)

        gate_w, up_w = cut(region_a[:, 0:16384], KC), cut(region_a[:, 16384:32768], KC)
        down_w = cut(region_b, IC)
        qkv0_w, wo0_w = cut(region_c[:, 0:5120], KC), cut(region_c[:, 5120:9216], KC)
        qkv1_w, proj1_w = cut(region_a[:, 0:12288], KC), cut(region_a[:, 12288:16384], KC)
        fc1_w, fc2_w = cut(region_a[:, 16384:32768], KC), cut(region_b, IC)

        xa = sb("x_attn", [P, TILES, D], F32)
        xm = sb("x_mlp", [P, TILES, D], F32)
        h_attn = sb("h_attn", [P, 2, 2, KC, P], F16)
        h_mlp = sb("h_mlp", [P, 2, KC, BLOCK], F16)
        inner = sb("inner", [P, 2, IC, BLOCK], F16)
        ident32 = sb("ident32", [P, P], F32)
        ident16 = sb("ident16", [P, P], F16)
        scratch = sb("scratch", [P, 8300], F32)

        taken = {"scratch": 0, "c": 0}

        def carve(n32, where="scratch"):
            at = taken[where]
            taken[where] = at + n32
            if where == "c":
                return region_c[:, 2 * at:2 * (at + n32)].bitcast(F32)
            assert at + n32 <= 8300, at + n32
            return scratch[:, at:at + n32]

        xn = carve(512)
        small = carve(256)
        stats = small[:, 0:8]
        moments = small[:, 8:10]
        rstd = small[:, 10:11]
        var_eps = small[:, 11:12]
        minus_half = small[:, 12:44]
        row_max = small[:, 44:52]
        row_sum = small[:, 52:60]
        row_inv = small[:, 60:68]
        norm_sq = small[:, 68:100]
        norm_inv = small[:, 100:132]
        sm_scale = small[:, 132:148]
        v_bias_t = small[:, 148:152]
        b_fc1_t = small[:, 152:168]
        mask_t = small[:, 168:232]
        spare = small[:, 232:233]
        eps_t = small[:, 233:234]
        eps_t0 = small[:, 234:235]
        gains = carve(128)
        base = taken["scratch"]
        act0 = carve(1024).rearrange("p (a n) -> p a n", a=2)
        qk0 = carve(8 * 2 * 64 // 2).bitcast(F16).rearrange("p (g h d) -> p g h d", g=HEADS0, h=2)
        kk0 = carve(128).bitcast(F16).rearrange("p (h r d) -> p h r d", h=2, r=2)
        rot = carve(576)
        rot2 = carve(576)
        qf0 = carve(512).bitcast(F16).rearrange("p (b g q) -> p b g q", b=2, g=HEADS0)
        kf0 = carve(128).bitcast(F16).rearrange("p (h n) -> p h n", h=2)
        v0 = carve(64).bitcast(F16).rearrange("p (h d) -> p h d", h=2)
        vv0 = carve(128).bitcast(F16).rearrange("p (b h d) -> p b h d", b=2, h=2)
        e0 = carve(512).rearrange("p (g t) -> p g t", g=8)
        p0 = carve(512).bitcast(F16).rearrange("p (g h t) -> p g h t", g=8, h=2)
        pt0 = carve(512).bitcast(F16).rearrange("p (g n) -> p g n", g=8)
        ctx0 = carve(512).bitcast(F16).rearrange("p (h c n) -> p h c n", h=2, c=KC)
        rope = carve(TILES * 64).rearrange("p (t s f) -> p t s f", t=TILES, s=2)
        cond32 = carve(256).rearrange("p (k b) -> p k b", k=KC)
        cond_cut = carve(256).bitcast(F16).rearrange("p (h k b) -> p h k b", h=2, k=KC)
        silu_cut = carve(256).bitcast(F16).rearrange("p (h k b) -> p h k b", h=2, k=KC)
        taken["scratch"] = base
        u1 = carve(1024).rearrange("p (a n) -> p a n", a=2)
        g1 = carve(1024).rearrange("p (a n) -> p a n", a=2)
        q16 = carve(512).bitcast(F16).rearrange("p (g r d) -> p g r d", g=HALF, r=4)
        k16 = carve(512).bitcast(F16).rearrange("p (g r d) -> p g r d", g=HALF, r=4)
        qf1 = carve(512).bitcast(F16).rearrange("p (g n) -> p g n", g=HALF)
        kf1 = carve(512).bitcast(F16).rearrange("p (g n) -> p g n", g=HALF)
        sq1 = carve(1024)
        e1 = sq1[:, 0:512].rearrange("p (g t) -> p g t", g=HALF)
        ctx32 = sq1[:, 512:1024]
        vv1 = carve(1024).bitcast(F16).rearrange("p (b h n) -> p b h n", b=2, h=2)
        v1 = carve(512).bitcast(F16).rearrange("p (h n) -> p h n", h=2)
        p1 = carve(512).bitcast(F16).rearrange("p (g h t) -> p g h t", g=HALF, h=2)
        qk1 = carve(1024, "c")
        pt1 = carve(512, "c").bitcast(F16).rearrange("p (g n) -> p g n", g=HALF)
        ctx1 = carve(512, "c").bitcast(F16).rearrange("p (h c n) -> p h c n", h=2, c=KC)
        gamma_a = carve(512, "c")
        gamma_m = carve(512, "c")
        q_bias_t = carve(512, "c")
        b_proj_t = carve(512, "c")
        b_fc2_t = carve(512, "c")
        stage_inner = [inner[:].rearrange("p h c n -> p (h c n)")[:, 4096 * n:4096 * (n + 1)].bitcast(F32)
                       for n in range(4)]
        stage_c = [region_c[:, 4096 * n:4096 * (n + 1)].bitcast(F32) for n in range(2)]
        ada_cut = xm[:].rearrange("p t n -> p (t n)").bitcast(F16).rearrange("p (h k n) -> p h k n", h=2, k=KC)
        ada_out = act0.rearrange("p a n -> p (a n)")
        hm_words = h_mlp[:].rearrange("p h k n -> p (h k n)").bitcast(F32)
        xm_words = xm[:].rearrange("p t n -> p (t n)")
        ang, turns = hm_words[:, 0:1024], hm_words[:, 1024:2048]
        cos_t, sin_t = xm_words[:, 0:1024], xm_words[:, 1024:2048]
        freq = act0[:, 0, 0:32]
        pos_i = act0[:, 0, 64:96].bitcast(I32)
        pos_f = act0[:, 0, 96:128]
        ln_w_t = act0[:, 0, 128:136]
        b_ada_t = act0[:, 0, 136:160]
        ada_f32 = act0[:, 0, 256:512].rearrange("p (c b) -> p c b", c=KC)
        gamma_row = act0[:, 1, :]
        b_ada_bc = [hm_words[0:NSEQ, 512 * n:512 * (n + 1)] for n in range(2)]

        ps_m = [ctx.enter_context(nc.psum_tensor(f"ps_m{n}", [P, 512], F32)) for n in range(4)]
        ps_pq = ctx.enter_context(nc.psum_tensor("ps_pq", [P, 1024], F32))
        ps_c = ctx.enter_context(nc.psum_tensor("ps_c", [P, 512], F32))
        ps_d = ctx.enter_context(nc.psum_tensor("ps_d", [P, 512], F32))

        def as16(ap, g):
            return ap.bitcast(F16).rearrange("p (g n) -> p g n", g=g)

        s_const = sem("constants_ready")
        s_setup_dma = sem("setup_loads")
        s_setup = sem("setup_chain")
        s_setup_act = sem("setup_chain_act")
        s_cond = sem("cond_cut_ready")
        s_rope_st = sem("rope_stored")
        s_stage = [sem(f"weights_landed{n}") for n in range(6)]
        s_whi = sem("weights_hi_cut")
        s_wlo = sem("weights_lo_cut")
        s_ada = sem("ada_products")
        s_ada_out = sem("ada_out_ready")
        s_ada_st = sem("ada_stored")
        s_l1c = sem("layer1_constants_loaded")
        s_l1s = sem("layer1_scale_ready")

        class Layer:

            def __init__(self, n):
                def s(name):
                    return sem(f"l{n}_{name}")
                self.x_in = s("x_loaded")
                self.tables = s("tables_loaded")
                self.stat = s("stat_ready")
                self.var = s("var_eps_ready")
                self.rstd = s("rstd_ready")
                self.xn = s("xn_ready")
                self.nt = s("norm_transposed")
                self.h32 = s("h32_ready")
                self.h_hi = s("h_hi_ready")
                self.h_lo = s("h_lo_ready")
                self.proj = s("projected")
                self.rot = s("rotated")
                self.qk32 = s("qk32_ready")
                self.v_hi = s("v_hi_ready")
                self.v16 = s("v_cut")
                self.vv = s("v_spread")
                self.q_hi = s("q_hi_ready")
                self.k_hi = s("k_hi_ready")
                self.q_lo = s("q_lo_ready")
                self.kk = s("k_lo_ready")
                self.turned = s("qk_transposed")
                self.qf = s("q_feature_major")
                self.kf = s("k_feature_major")
                self.scores = s("scores_ready")
                self.mx = s("row_max_ready")
                self.shift = s("scores_shifted")
                self.e = s("exp_ready")
                self.sum = s("row_sum_ready")
                self.inv = s("row_inverse_ready")
                self.prob = s("probs_ready")
                self.p_hi = s("p_hi_ready")
                self.p_lo = s("p_lo_ready")
                self.p_turned = s("p_transposed")
                self.pt = s("p_key_major")
                self.mixed = s("mixed")
                self.c_hi = s("ctx_hi_ready")
                self.c_lo = s("ctx_lo_ready")
                self.o = s("out_projected")
                self.x1 = s("x_after_attention")
                self.hand = s("x_handed_over")
                self.up = s("up_done")
                self.act = s("act_done")
                self.m32 = s("inner32_ready")
                self.m_hi = s("inner_hi_ready")
                self.m_lo = s("inner_lo_ready")
                self.down = s("down_done")
                self.y = s("y_ready")
                self.y_out = s("y_stored")
                self.sq = s("qk_squared")
                if n == 0:
                    self.gated = s("act_times_gate")
                else:
                    self.stat0 = s("stat_partial")
                    self.h_scaled = s("h_scaled")
                    self.projv = s("v_projected")
                    self.mx0 = s("masked_ready")
                    self.c32 = s("ctx32_ready")
                    self.o_b = s("out_biased")
                    self.o_g = s("out_gated")
                    self.u = s("u_ready")
                    self.usq = s("u_squared")
                    self.poly = s("poly_ready")
                    self.arg = s("tanh_arg_ready")
                    self.d_b = s("down_biased")
                    self.d_g = s("down_gated")
                    self.gam_a = s("gamma_attn_loaded")
                    self.gam_m = s("gamma_mlp_loaded")
                    self.normed = s("qk_normalised")
                    self.nsum = s("qk_norms_summed")
                    self.nmax = s("qk_norms_floored")
                    self.npow = s("qk_norms_inverted")
                    self.ninv = s("qk_norms_ready")

        L0, L1 = Layer(0), Layer(1)

        def first_block(it):
            return isinstance(it, int) and it == 0

        def rows(w, k, c0, n):
            return w[k * P * KC:(k + 1) * P * KC, c0:c0 + n].rearrange("(k p) n -> p k n", p=P)

        groups = [("ada", 0, rows(tw_t[0], 0, 0, D)),
                  ("w", qkv0_w[:, :, :, 0:512], rows(wqkv0_t, 0, 0, 512)),
                  ("w", qkv0_w[:, :, :, 512:640], rows(wqkv0_t, 0, 512, 128)),
                  ("w", wo0_w, rows(wo0_t, 0, 0, D)),
                  ("ada", 1, rows(tw_t[1], 0, 0, D))]
        FIRST = len(groups)
        groups += [("ada", 2 + n, rows(wada_t, 0, n * D, D)) for n in range(6)]
        for n in range(4):
            groups.append(("w", gate_w[:, :, :, 512 * n:512 * (n + 1)], rows(wg_t, 0, 512 * n, 512)))
            groups.append(("w", up_w[:, :, :, 512 * n:512 * (n + 1)], rows(wu_t, 0, 512 * n, 512)))
        groups += [("w", down_w[:, :, 4 * n:4 * (n + 1), :], rows(wd_t, n, 0, D)) for n in range(4)]
        SETUP = len(groups)
        groups += [("w", qkv1_w[:, :, :, 512 * n:512 * (n + 1)], rows(wqkv1_t, 0, 512 * n, 512)) for n in range(3)]
        groups.append(("w", proj1_w, rows(wproj_t, 0, 0, D)))
        groups += [("w", fc1_w[:, :, :, 512 * n:512 * (n + 1)], rows(wfc1_t, 0, 512 * n, 512)) for n in range(4)]
        SWAP = len(groups)
        groups += [("w", fc2_w[:, :, 4 * n:4 * (n + 1), :], rows(wfc2_t, n, 0, D)) for n in range(4)]

        def place(g):
            if g < SETUP:
                n, k = g % 4, g // 4
                return s_stage[n], 16 * (k + 1), stage_inner[n], g - 4
            if g < SWAP:
                n, k = (g - SETUP) % 2, (g - SETUP) // 2
                return s_stage[4 + n], 16 * (k + 1), stage_c[n], g - 2 if g - 2 >= SETUP else -1
            n = g - SWAP
            before = sum(1 for q in range(SETUP) if q % 4 == n)
            return s_stage[n], 16 * (before + 1), stage_inner[n], -1

        def staged(g):
            n = groups[g][2].shape[2]
            return place(g)[2][:, 0:KC * n].rearrange("p (k n) -> p k n", k=KC)

        def dest(g, hl):
            if groups[g][0] == "ada":
                return ada_cut[:, hl]
            return groups[g][1][:, hl]

        def ada_before(g):
            return sum(1 for q in groups[:g] if q[0] == "ada")

        def tile(it, t):
            return it * TILES + t

        def norm_no(norms, it, kind, t):
            return it * len(norms) + norms.index((kind, t))

        block = ctx.enter_context(nc.Block())

        @block.sync
        def _(sp):
            count_registers = [sp.alloc_register("count_first"), sp.alloc_register("count_second")]

            def counts(*values):
                for n, r in zip(values, count_registers):
                    if not isinstance(n, int):
                        sp.reg_mov(r, n)
                return [n if isinstance(n, int) else r for n, r in zip(values, count_registers)]

            def by_block(ap, it, t):
                return ap.rearrange("(n t p) d -> n t p d", n=NBLK, t=TILES)[bass.ds(it, 1), t].rearrange("o p d -> (o p) d")

            def load_group(g):
                s, _, words, reuse = place(g)
                if reuse >= 0:
                    sp.wait_ge(s_wlo, reuse + 1)
                sp.dma_start(staged(g), groups[g][2]).then_inc(s, 16)

            def load_x(L, src, it, t):
                sp.dma_start(xa[:, t, :], by_block(src, it, t)).then_inc(L.x_in, 16)

            def spread(L, v, vv, it, t):
                cut_done, mixed = counts(tile(it, t) + 1, tile(it, t) if L is L0 else 2 * tile(it, t))
                sp.wait_ge(L.v16, cut_done)
                sp.wait_ge(L.mixed, mixed)
                for b in range(2):
                    for half in range(2):
                        sp.dma_start(vv[SEQ * half:SEQ * (half + 1), b], v[SEQ * b:SEQ * (b + 1)]).then_inc(L.vv, 16)

            def store_y(L, dst, it, t):
                sp.wait_ge(L.y, tile(it, t) + 1)
                sp.dma_start(by_block(dst, it, t), xm[:, t, :]).then_inc(L.y_out, 16)

            def hand_over(L, norms, it, t):
                if first_block(it):
                    sp.wait_ge(L.x1, tile(it, t) + 1)
                else:
                    attended, left = counts(tile(it, t) + 1, 16 * (tile(it, t) - TILES + 1))
                    sp.wait_ge(L.x1, attended)
                    sp.wait_ge(L.y_out, left)
                sp.dma_start(xm[:, t, :], xa[:, t, :]).then_inc(L.hand, 16)

            def next_x(L, norms, src, it, t):
                handed, normed = counts(16 * (tile(it, t) + 1), norm_no(norms, it, "norm2", t) + 1)
                sp.wait_ge(L.hand, handed)
                sp.wait_ge(L.xn, normed)
                load_x(L, src, it + 1, t)

            def move_on(L, norms, src, it, t, more):
                hand_over(L, norms, it, t)
                if more:
                    next_x(L, norms, src, it, t)

            def tables0(it):
                sp.dma_start(gains[:, 0:64], gain0_dram[bass.ds(it, 1)].rearrange("o p k c b -> p (o k c b)")).then_inc(L0.tables, 16)
                sp.dma_start(rope.rearrange("p t s f -> p (t s f)"), rope_dram.rearrange("p (n t) s f -> p n t s f", n=NBLK)[:, bass.ds(it, 1)].rearrange("p o t s f -> p (o t s f)")).then_inc(L0.tables, 16)

            def tables1(it):
                sp.dma_start(gains[:, 0:128], mod1_dram[bass.ds(it, 1)].rearrange("o p k c b -> p (o k c b)")).then_inc(L1.tables, 16)

            def gamma(L, which, dst, s, it, t):
                for b in range(2):
                    row = gamma_dram[which].rearrange("(n s) d -> n s d", n=NBLK)[bass.ds(it, 1), 2 * t + b, :]
                    sp.dma_start(dst[SEQ * b:SEQ * (b + 1), :], row.to_broadcast([SEQ, D])).then_inc(s, 16)

            sp.dma_start(pos_i, pos).then_inc(s_setup_dma, 16)
            sp.dma_start(ln_w_t, ln_w).then_inc(s_setup_dma, 16)
            sp.dma_start(b_ada_t, b_ada).then_inc(s_setup_dma, 16)
            sp.dma_start(cond32, cond_t).then_inc(s_setup_dma, 16)
            for g in range(2):
                load_group(g)
            for t in range(TILES):
                load_x(L0, x, 0, t)
            for g in range(2, FIRST - 1):
                load_group(g)
            sp.wait_ge(s_setup, 13)
            sp.dma_start(rope_dram[:, :, 0, :], cos_t.rearrange("p (t f) -> p t f", f=32)).then_inc(s_rope_st, 16)
            sp.dma_start(rope_dram[:, :, 1, :], sin_t.rearrange("p (t f) -> p t f", f=32)).then_inc(s_rope_st, 16)
            sp.wait_ge(s_rope_st, 32)
            load_group(FIRST - 1)
            for n in range(2):
                sp.dma_start(b_ada_bc[n], b_ada_row[n:n + 1, :].to_broadcast([NSEQ, D])).then_inc(s_setup_dma, 16)

            def store_ada(n):
                sp.wait_ge(s_ada_out, n + 1)
                if n < 2:
                    for blk in range(NBLK):
                        sp.dma_start(gain0_dram[blk, :, n], ada_f32[:, :, 8 * blk:8 * (blk + 1)]).then_inc(s_ada_st, 16)
                elif n < 4:
                    for c in range(NBLK):
                        sp.dma_start(gamma_dram[n - 2, 8 * c:8 * (c + 1), :], gamma_row[8 * c:8 * (c + 1), :]).then_inc(s_ada_st, 16)
                else:
                    for blk in range(NBLK):
                        sp.dma_start(mod1_dram[blk, :, n - 4], ada_f32[:, :, 8 * blk:8 * (blk + 1)]).then_inc(s_ada_st, 16)

            load_group(FIRST)
            store_ada(0)
            load_group(FIRST + 1)
            store_ada(1)
            sp.wait_ge(s_ada_st, 16 * NBLK * 2)
            tables0(0)
            for s in range(SLOTS0):
                g = FIRST + s
                if g + 2 < SETUP:
                    load_group(g + 2)
                if g < SETUP and groups[g][0] == "ada":
                    store_ada(groups[g][1])
                for stage, t in TABLE0[s]:
                    if stage == "turn":
                        spread(L0, v0, vv0, 0, t)
            for t in range(TILES):
                hand_over(L0, NORMS0, 0, t)
                next_x(L0, NORMS0, x, 0, t)

            def last_gain0(it):
                normed, rotated = counts((it + 1) * len(NORMS0), tile(it + 1, 0))
                sp.wait_ge(L0.h32, normed)
                sp.wait_ge(L0.rot, rotated)
                tables0(it + 1)

            def slots0(it, more):
                last_gain0(it)
                for s in range(SLOTS0):
                    for stage, t in TABLE0[s]:
                        if stage == "turn":
                            spread(L0, v0, vv0, it + 1, t)
                    if s >= IC and (s - IC) % 2 == 1:
                        store_y(L0, x_mid, it, (s - IC) // 2)
                    if s > IC and (s - IC) % 2 == 0:
                        move_on(L0, NORMS0, x, it + 1, (s - IC) // 2 - 1, more)
                move_on(L0, NORMS0, x, it + 1, TILES - 1, more)

            with sp.Fori(0, NBLK - 2) as i:
                slots0(i, True)
            slots0(NBLK - 2, False)
            def load_const1():
                for dst, src, n in ((mask_t, mask, 2), (q_bias_t, q_bias, 1), (b_proj_t, b_proj, 1), (b_fc2_t, b_fc2, 1),
                                    (sm_scale, scale_log, 1)):
                    if n == 2:
                        for b in range(2):
                            sp.dma_start(dst[SEQ * b:SEQ * (b + 1), :], src).then_inc(s_l1c, 16)
                    else:
                        sp.dma_start(dst, src.to_broadcast([P, src.shape[1]])).then_inc(s_l1c, 16)
                sp.dma_start(v_bias_t, v_bias).then_inc(s_l1c, 16)
                sp.dma_start(b_fc1_t, b_fc1).then_inc(s_l1c, 16)

            sp.wait_ge(L0.x1, TILES * NBLK)
            for g in range(SETUP, SETUP + 2):
                load_group(g)
            for s in range(IC, SLOTS0):
                g = SETUP + s - IC + 2
                if g < SWAP:
                    load_group(g)
                if (s - IC) % 2 == 1:
                    store_y(L0, x_mid, NBLK - 1, (s - IC) // 2)
            sp.wait_ge(s_wlo, SWAP)
            load_const1()
            sp.wait_ge(s_ada_st, 16 * NBLK * 8)
            tables1(0)
            sp.wait_ge(L0.y_out, 16 * TILES * NBLK)
            for t in range(TILES):
                load_x(L1, x_mid, 0, t)
            sp.wait_ge(L0.down, 8 * NBLK)
            for g in range(SWAP, len(groups)):
                load_group(g)

            def attn1(stage, it, t):
                if stage == "norm1":
                    sp.wait_ge(L1.o_g, tile(it, t))
                    gamma(L1, 0, gamma_a, L1.gam_a, it, t)
                if stage == "wait":
                    spread(L1, v1, vv1, it, t)

            for s in range(SLOTS1):
                for stage, t in TABLE1[s]:
                    attn1(stage, 0, t)
            for t in range(TILES):
                hand_over(L1, NORMS1, 0, t)
                next_x(L1, NORMS1, x_mid, 0, t)

            def slots1(it, both, more):
                if both:
                    sp.wait_ge(L1.h32, (it + 1) * len(NORMS1))
                    tables1(it + 1)
                for s in range(SLOTS1):
                    if both:
                        for stage, t in TABLE1[s]:
                            attn1(stage, it + 1, t)
                    if s >= IC and (s - IC) % 4 == 0:
                        t = (s - IC) // 4
                        sp.wait_ge(L1.d_g, tile(it, t))
                        gamma(L1, 1, gamma_m, L1.gam_m, it, t)
                    if s >= IC and (s - IC) % 4 == 3:
                        store_y(L1, out, it, (s - IC) // 4)
                    if both and s > IC and (s - IC) % 4 == 0:
                        move_on(L1, NORMS1, x_mid, it + 1, (s - IC) // 4 - 1, more)
                if both:
                    move_on(L1, NORMS1, x_mid, it + 1, TILES - 1, more)

            with sp.Fori(0, NBLK - 2) as i:
                slots1(i, True, True)
            slots1(NBLK - 2, True, False)
            slots1(NBLK - 1, False, False)
            sp.wait_ge(L1.y_out, 16 * TILES * NBLK)

        @block.gpsimd
        def _(pool):
            for n, m in enumerate((ident32, ident16)):
                nc.gpsimd.memset(m[:], 0.0).then_inc(s_const, 1)
                pool.wait_ge(s_const, 2 * n + 1)
                nc.gpsimd.affine_select(out=m[:], in_=m[:], compare_op=ALU.not_equal, fill=1.0, base=0,
                                        pattern=[[-1, P]], channel_multiplier=1).then_inc(s_const, 1)
            nc.gpsimd.memset(minus_half, -0.5).then_inc(s_const, 1)
            nc.gpsimd.memset(eps_t, EPS).then_inc(s_const, 1)
            nc.gpsimd.memset(eps_t0, D * EPS).then_inc(s_const, 1)
            for n in range(32):
                inv_freq = float(1.0 / 10000.0 ** (2.0 * n / HD0))
                nc.gpsimd.memset(freq[:, n:n + 1], inv_freq).then_inc(s_const, 1)

            def norm(L, norms, it, kind, t):
                n = norm_no(norms, it, kind, t)
                pool.wait_ge(L.stat, n + 1)
                value = stats[:, 0:1] if L is L0 else moments[:, 1:2]
                nc.gpsimd.tensor_tensor(var_eps, value, eps_t[:, 0:1] if L is L1 else eps_t0, ALU.add).then_inc(L.var, 1)
                pool.wait_ge(L.var, n + 1)
                nc.gpsimd.tensor_tensor(rstd, var_eps, minus_half[:, 0:1], ALU.pow).then_inc(L.rstd, 1)

            def norm_lo(L, norms, it, kind, t):
                n = norm_no(norms, it, kind, t)
                pool.wait_ge(L.h_hi, n + 1)
                dst = h_attn[:, t % 2, 1] if kind == "norm1" else h_mlp[:, 1, :, t * P:(t + 1) * P]
                hi = h_attn[:, t % 2, 0] if kind == "norm1" else h_mlp[:, 0, :, t * P:(t + 1) * P]
                nc.gpsimd.tensor_tensor(dst, xn.rearrange("p (c n) -> p c n", c=KC), hi, ALU.subtract).then_inc(L.h_lo, 1)

            def attn0(stage, it, t):
                n = tile(it, t)
                if stage in ("norm1", "norm2"):
                    norm(L0, NORMS0, it, stage, t)
                    norm_lo(L0, NORMS0, it, stage, t)
                if stage == "proj":
                    pool.wait_ge(L0.q_hi, n + 1)
                    nc.gpsimd.tensor_tensor(qk0[:, :, 1, :], rot[:, 0:512].rearrange("p (g d) -> p g d", g=HEADS0),
                                            qk0[:, :, 0, :], ALU.subtract).then_inc(L0.q_lo, 1)
                    pool.wait_ge(L0.k_hi, n + 1)
                    nc.gpsimd.tensor_tensor(kk0[:, 1], rot[:, 512:576].unsqueeze(1).to_broadcast([P, 2, HD0]), kk0[:, 0],
                                            ALU.subtract).then_inc(L0.kk, 1)
                if stage == "scores":
                    pool.wait_ge(L0.p_hi, n + 1)
                    nc.gpsimd.tensor_tensor(p0[:, :, 1, :], e0, p0[:, :, 0, :], ALU.subtract).then_inc(L0.p_lo, 1)

            def mlp_lo(L, src, it, j):
                pool.wait_ge(L.m_hi, it * IC + j + 1)
                nc.gpsimd.tensor_tensor(inner[:, 1, j, :], src[:, j % 2, :], inner[:, 0, j, :],
                                        ALU.subtract).then_inc(L.m_lo, 1)

            pool.wait_ge(s_const, 39)
            for s in range(SLOTS0):
                for stage, t in TABLE0[s]:
                    attn0(stage, 0, t)

            def slots0(it, both):
                for s in range(SLOTS0):
                    if 1 <= s <= IC:
                        mlp_lo(L0, act0, it, s - 1)
                    if both:
                        for stage, t in TABLE0[s]:
                            attn0(stage, it + 1, t)

            with pool.Fori(0, NBLK - 1) as i:
                slots0(i, True)
            slots0(NBLK - 1, False)

            def attn1(stage, it, t):
                n = tile(it, t)
                if stage in ("norm1", "norm2"):
                    norm(L1, NORMS1, it, stage, t)
                    norm_lo(L1, NORMS1, it, stage, t)
                if stage == "proj":
                    pool.wait_ge(L1.nmax, n + 1)
                    nc.gpsimd.tensor_tensor(norm_inv, norm_sq, minus_half, ALU.pow).then_inc(L1.npow, 1)
                    pool.wait_ge(L1.npow, n + 1)
                    pool.wait_ge(s_l1s, 3)
                    nc.gpsimd.tensor_tensor(norm_inv[:, 0:HEADS1], norm_inv[:, 0:HEADS1], sm_scale,
                                            ALU.mult).then_inc(L1.ninv, 1)
                for h in range(2):
                    if stage == ("wait", "turn0")[h]:
                        for which, dst, hi_done, lo_done, a, b in ((0, q16, L1.q_hi, L1.q_lo, 0, 1), (1, k16, L1.k_hi, L1.kk, 0, 2)):
                            src = qk1[:, 512 * which + 256 * h:512 * which + 256 * (h + 1)].rearrange("p (g d) -> p g d", g=HALF)
                            pool.wait_ge(hi_done, 4 * n + 2 * h + 2)
                            for r in range(2):
                                lo = dst[:, :, (1 + 2 * r) if which == 0 else (2 + r), :]
                                nc.gpsimd.tensor_tensor(lo, src, dst[:, :, 0, :], ALU.subtract).then_inc(lo_done, 1)
                    if stage == ("turn1_scores0", "scores1_turn_p0")[h]:
                        pool.wait_ge(L1.p_hi, 2 * n + h + 1)
                        nc.gpsimd.tensor_tensor(p1[:, :, 1, :], e1, p1[:, :, 0, :], ALU.subtract).then_inc(L1.p_lo, 1)
                if stage == "out":
                    pool.wait_ge(L1.o_g, n + 1)
                    nc.gpsimd.tensor_tensor(xa[:, t, :], xa[:, t, :], ctx32, ALU.add).then_inc(L1.x1, 1)

            def mlp1(it, j):
                pool.wait_ge(L1.poly, it * IC + j + 1)
                nc.gpsimd.tensor_tensor(g1[:, j % 2, :], g1[:, j % 2, :], u1[:, j % 2, :], ALU.mult).then_inc(L1.arg, 1)

            for s in range(SLOTS1):
                for stage, t in TABLE1[s]:
                    attn1(stage, 0, t)

            def slots1(it, both):
                for s in range(SLOTS1):
                    if s < IC:
                        mlp1(it, s)
                    if 1 <= s <= IC:
                        mlp_lo(L1, u1, it, s - 1)
                    if both:
                        for stage, t in TABLE1[s]:
                            attn1(stage, it + 1, t)

            with pool.Fori(0, NBLK - 1) as i:
                slots1(i, True)
            slots1(NBLK - 1, False)

        @block.scalar
        def _(act):
            act.wait_ge(s_setup_dma, 64)
            act.wait_ge(s_setup, 7)
            nc.scalar.activation(sin_t, ang, ACT.Sin).then_inc(s_setup_act, 1)
            act.wait_ge(s_setup, 11)
            nc.scalar.activation(cos_t, turns, ACT.Sin).then_inc(s_setup_act, 1)
            nc.scalar.copy(cond_cut[:, 0], cond32).then_inc(s_setup_act, 1)
            nc.scalar.activation(xn[:, 0:256].rearrange("p (k b) -> p k b", k=KC), cond32, ACT.Tanh, scale=0.5).then_inc(s_setup_act, 1)

            def cut_hi(g):
                s, n, _, _ = place(g)
                act.wait_ge(s, n)
                if groups[g][0] == "ada":
                    act.wait_ge(s_rope_st, 32)
                    act.wait_ge(s_ada, ada_before(g))
                if SETUP <= g < SWAP:
                    act.wait_ge(L0.up, NBLK * IC)
                if g >= SWAP:
                    act.wait_ge(L0.down, NBLK * 8)
                nc.scalar.mul(dest(g, 0), staged(g), WS).then_inc(s_whi, 1)

            for g in range(FIRST):
                cut_hi(g)

            def norm_square(it, kind, t):
                n = norm_no(NORMS0, it, kind, t)
                act.wait_ge(L0.h_lo, n)
                if kind == "norm1":
                    act.wait_ge(L0.x_in, 16 * (tile(it, t) + 1))
                else:
                    act.wait_ge(L0.x1, tile(it, t) + 1)
                nc.scalar.activation(xn, xa[:, t, :], ACT.Square, accum_out=stats[:, 0:1]).then_inc(L0.stat, 1)

            def norm_hi(L, norms, it, kind, t):
                n = norm_no(norms, it, kind, t)
                act.wait_ge(L.h32, n + 1)
                if kind == "norm1":
                    if t > 0 or not first_block(it):
                        act.wait_ge(L.proj if L is L0 else L.projv, tile(it, t) - 1)
                    dst = h_attn[:, t % 2, 0]
                else:
                    act.wait_ge(L.up, it * IC)
                    dst = h_mlp[:, 0, :, t * P:(t + 1) * P]
                nc.scalar.copy(dst, xn.rearrange("p (c n) -> p c n", c=KC)).then_inc(L.h_hi, 1)

            def attn0(stage, it, t):
                n = tile(it, t)
                if stage in ("norm1", "norm2"):
                    norm_square(it, stage, t)
                    norm_hi(L0, NORMS0, it, stage, t)
                if stage == "proj":
                    act.wait_ge(L0.rot, n + 1)
                    act.wait_ge(L0.turned, n)
                    nc.scalar.copy(qk0[:, :, 0, :], rot[:, 0:512].rearrange("p (g d) -> p g d", g=HEADS0)).then_inc(L0.q_hi, 1)
                    nc.scalar.copy(kk0[:, 0], rot[:, 512:576].unsqueeze(1).to_broadcast([P, 2, HD0])).then_inc(L0.k_hi, 1)
                if stage == "turn":
                    act.wait_ge(L0.turned, n + 1)
                    act.wait_ge(L0.scores, n)
                    nc.scalar.copy(kf0, as16(ps_pq[:, 0:128], 2)).then_inc(L0.kf, 1)
                if stage == "scores":
                    act.wait_ge(L0.shift, n + 1)
                    nc.scalar.activation(e0, e0, ACT.Exp, scale=float(HD0) ** -0.5).then_inc(L0.e, 1)
                    act.wait_ge(L0.prob, n + 1)
                    act.wait_ge(L0.p_turned, n)
                    nc.scalar.copy(p0[:, :, 0, :], e0).then_inc(L0.p_hi, 1)
                if stage == "turn_p":
                    act.wait_ge(L0.p_turned, n + 1)
                    act.wait_ge(L0.mixed, n)
                    nc.scalar.copy(pt0, as16(ps_d[:], 8)).then_inc(L0.pt, 1)
                if stage == "mix":
                    act.wait_ge(L0.mixed, n + 1)
                    act.wait_ge(L0.o, n)
                    nc.scalar.copy(ctx0[:, 0], ps_d[:].rearrange("p (c n) -> p c n", c=KC)).then_inc(L0.c_hi, 1)

            for s in range(SLOTS0):
                if FIRST + s < SETUP:
                    cut_hi(FIRST + s)
                for stage, t in TABLE0[s]:
                    attn0(stage, 0, t)

            def mlp_hi(L, src, it, j):
                act.wait_ge(L.m32, it * IC + j + 1)
                act.wait_ge(L.down, it * (8 if L is L0 else 16))
                nc.scalar.copy(inner[:, 0, j, :], src[:, j % 2, :]).then_inc(L.m_hi, 1)

            def slots0(it, both):
                for s in range(SLOTS0):
                    if s < IC:
                        act.wait_ge(L0.up, it * IC + s + 1)
                        act.wait_ge(L0.m_lo, it * IC + (s - 1 if s > 1 else 0))
                        nc.scalar.activation(act0[:, s % 2, :], ps_m[2 * (s % 2)][:], ACT.Tanh,
                                             scale=0.5 * INV).then_inc(L0.act, 1)
                    if 1 <= s <= IC:
                        mlp_hi(L0, act0, it, s - 1)
                    if both:
                        for stage, t in TABLE0[s]:
                            attn0(stage, it + 1, t)
                    elif s >= IC:
                        cut_hi(SETUP + s - IC)

            with act.Fori(0, NBLK - 1) as i:
                slots0(i, True)
            slots0(NBLK - 1, False)

            act.wait_ge(s_l1s, 1)
            nc.scalar.activation(sm_scale, sm_scale, ACT.Exp).then_inc(s_l1s, 2)

            def attn1(stage, it, t):
                n = tile(it, t)
                if stage in ("norm1", "norm2"):
                    norm_hi(L1, NORMS1, it, stage, t)
                if stage == "proj":
                    act.wait_ge(L1.proj, n + 1)
                    act.wait_ge(L1.k_hi, 4 * n)
                    act.wait_ge(L1.kk, 4 * n)
                    nc.scalar.mul(qk1[:, 512:1024], ps_pq[:, 512:1024], INV).then_inc(L1.rot, 1)
                    act.wait_ge(L1.qk32, n + 1)
                    act.wait_ge(L1.rot, n + 1)
                    act.wait_ge(L1.x1, n)
                    nc.scalar.activation(sq1, qk1, ACT.Square).then_inc(L1.sq, 1)
                    act.wait_ge(L1.projv, n + 1)
                    act.wait_ge(L1.vv, 64 * n)
                    nc.scalar.mul(v1[:, 0], ps_d[:], INV).then_inc(L1.v_hi, 1)
                for h in range(2):
                    if stage == ("wait", "turn0")[h]:
                        act.wait_ge(L1.normed, n + 1)
                        act.wait_ge(L1.turned, 2 * n + h)
                        for r in range(2):
                            nc.scalar.copy(q16[:, :, 2 * r, :], qk1[:, 256 * h:256 * (h + 1)].rearrange("p (g d) -> p g d", g=HALF)).then_inc(L1.q_hi, 1)
                        for r in range(2):
                            nc.scalar.copy(k16[:, :, r, :], qk1[:, 512 + 256 * h:512 + 256 * (h + 1)].rearrange("p (g d) -> p g d", g=HALF)).then_inc(L1.k_hi, 1)
                    if stage == ("turn0", "turn1_scores0")[h]:
                        act.wait_ge(L1.turned, 2 * n + h + 1)
                        act.wait_ge(L1.scores, 2 * n + h)
                        nc.scalar.copy(kf1, as16(ps_pq[:, 0:512], HALF)).then_inc(L1.kf, 1)
                    if stage == ("turn1_scores0", "scores1_turn_p0")[h]:
                        act.wait_ge(L1.shift, 2 * n + h + 1)
                        nc.scalar.activation(e1, e1, ACT.Exp).then_inc(L1.e, 1)
                        act.wait_ge(L1.prob, 2 * n + h + 1)
                        act.wait_ge(L1.p_turned, 2 * n + h)
                        nc.scalar.copy(p1[:, :, 0, :], e1).then_inc(L1.p_hi, 1)
                    if stage == ("scores1_turn_p0", "mix0_turn_p1")[h]:
                        act.wait_ge(L1.p_turned, 2 * n + h + 1)
                        act.wait_ge(L1.mixed, 2 * n + h)
                        bank = ps_d[:] if h == 0 else ps_pq[:, 512:1024]
                        nc.scalar.copy(pt1, as16(bank, HALF)).then_inc(L1.pt, 1)
                if stage == "mix1":
                    act.wait_ge(L1.c32, n + 1)
                    act.wait_ge(L1.o, n)
                    nc.scalar.copy(ctx1[:, 0], ctx32.rearrange("p (c n) -> p c n", c=KC)).then_inc(L1.c_hi, 1)

            for s in range(SLOTS1):
                if SWAP + s < len(groups):
                    cut_hi(SWAP + s)
                for stage, t in TABLE1[s]:
                    attn1(stage, 0, t)

            def slots1(it, both):
                for s in range(SLOTS1):
                    if s < IC:
                        j = s
                        act.wait_ge(L1.up, it * IC + j + 1)
                        act.wait_ge(L1.m_lo, it * IC + (j - 1 if j > 1 else 0))
                        if j == 0:
                            act.wait_ge(L1.y, tile(it, 0))
                        nc.scalar.activation(u1[:, j % 2, :], ps_m[j % 4][:], ACT.Identity, bias=b_fc1_t[:, j:j + 1],
                                             scale=INV).then_inc(L1.u, 1)
                        act.wait_ge(L1.u, it * IC + j + 1)
                        nc.scalar.activation(g1[:, j % 2, :], u1[:, j % 2, :], ACT.Square).then_inc(L1.usq, 1)
                    if 1 <= s <= IC:
                        mlp_hi(L1, u1, it, s - 1)
                    if s < IC:
                        act.wait_ge(L1.arg, it * IC + j + 1)
                        nc.scalar.activation(g1[:, j % 2, :], g1[:, j % 2, :], ACT.Tanh).then_inc(L1.act, 1)
                    if both:
                        for stage, t in TABLE1[s]:
                            attn1(stage, it + 1, t)

            with act.Fori(0, NBLK - 1) as i:
                slots1(i, True)
            slots1(NBLK - 1, False)

        @block.vector
        def _(dve):
            steps = [0]

            def link(ins):
                steps[0] += 1
                ins.then_inc(s_setup, 1)
                dve.wait_ge(s_setup, steps[0])

            dve.wait_ge(s_setup_dma, 64)
            dve.wait_ge(s_const, 39)
            a3, t3 = ang.rearrange("p (t f) -> p t f", f=32), turns.rearrange("p (t f) -> p t f", f=32)
            link(nc.vector.tensor_copy(pos_f, pos_i))
            link(nc.vector.tensor_tensor(a3, pos_f.unsqueeze(2).to_broadcast([P, 32, 32]),
                                         freq.unsqueeze(1).to_broadcast([P, 32, 32]), ALU.mult))
            link(nc.vector.tensor_scalar(turns, ang, 1.0 / TWO_PI, ROUND, ALU.mult, ALU.add))
            link(nc.vector.tensor_scalar(turns, turns, ROUND, None, ALU.subtract))
            link(nc.vector.scalar_tensor_tensor(ang, turns, -PI_HIGH, ang, ALU.mult, ALU.add))
            link(nc.vector.scalar_tensor_tensor(ang, turns, -PI_LOW, ang, ALU.mult, ALU.add))
            link(nc.vector.tensor_scalar(ang, ang, PI_IN, -PI_IN, ALU.min, ALU.max))
            link(nc.vector.tensor_scalar(turns, ang, TWO_PI / 4, PI_IN, ALU.add, ALU.is_gt))
            link(nc.vector.scalar_tensor_tensor(turns, turns, -TWO_PI, ang, ALU.mult, ALU.add))
            link(nc.vector.tensor_scalar(turns, turns, TWO_PI / 4, PI_IN, ALU.add, ALU.min))
            link(nc.vector.tensor_scalar(turns, turns, -PI_IN, None, ALU.max))
            dve.wait_ge(s_setup_act, 2)
            link(nc.vector.tensor_scalar(sin_t, sin_t, INV, None, ALU.mult))
            link(nc.vector.tensor_scalar(cos_t, cos_t, INV, None, ALU.mult))
            dve.wait_ge(s_setup_act, 4)
            half_silu = xn[:, 0:256].rearrange("p (k b) -> p k b", k=KC)
            link(nc.vector.tensor_tensor(cond_cut[:, 1], cond32, cond_cut[:, 0], ALU.subtract))
            link(nc.vector.scalar_tensor_tensor(half_silu, half_silu, 1.0, cond32, ALU.add, ALU.mult))
            link(nc.vector.tensor_scalar(half_silu, half_silu, 0.5, None, ALU.mult))
            link(nc.vector.tensor_copy(silu_cut[:, 0], half_silu))
            nc.vector.tensor_tensor(silu_cut[:, 1], half_silu, silu_cut[:, 0], ALU.subtract).then_inc(s_cond, 1)

            def cut_lo(g):
                dve.wait_ge(s_whi, g + 1)
                nc.vector.scalar_tensor_tensor(dest(g, 1), staged(g), WS, dest(g, 0), ALU.mult,
                                               ALU.subtract).then_inc(s_wlo, 1)
                if groups[g][0] == "ada":
                    ada(groups[g][1])

            def ada(n):
                dve.wait_ge(s_ada, n + 1)
                dve.wait_ge(s_ada_st, 16 * NBLK * n)
                bank = ps_m[n % 2]
                feat = bank[:, 0:256].rearrange("p (c b) -> p c b", c=KC)
                if n < 2:
                    link(nc.vector.tensor_scalar(ada_f32, feat, INV, 1.0, ALU.mult, ALU.add))
                    w = ln_w_t[:, 4 * n:4 * (n + 1)].unsqueeze(2).to_broadcast([P, KC, NSEQ])
                    nc.vector.tensor_tensor(ada_f32, ada_f32, w, ALU.mult).then_inc(s_ada_out, 1)
                elif n < 4:
                    dve.wait_ge(s_setup_dma, 64 + 32)
                    nc.vector.scalar_tensor_tensor(gamma_row[0:NSEQ, :], bank[0:NSEQ, :], INV, b_ada_bc[n - 2], ALU.mult,
                                                   ALU.add).then_inc(s_ada_out, 1)
                else:
                    b = b_ada_t[:, 4 * (n - 2):4 * (n - 1)].unsqueeze(2).to_broadcast([P, KC, NSEQ])
                    ins = nc.vector.scalar_tensor_tensor(ada_f32, feat, INV, b, ALU.mult, ALU.add)
                    if n < 6:
                        link(ins)
                        ins = nc.vector.tensor_scalar(ada_f32, ada_f32, 1.0, None, ALU.add)
                    ins.then_inc(s_ada_out, 1)

            for g in range(FIRST):
                cut_lo(g)

            def gain(kind, t, shift=0):
                k = 0 if kind == "norm1" else 1
                g = gains.rearrange("p (k c b) -> p k c b", k=4, c=KC) if shift is not None else None
                return g[:, k + shift, :, 2 * t:2 * t + 2].unsqueeze(3).to_broadcast([P, KC, 2, SEQ])

            def by_seq(ap):
                return ap.rearrange("p (c b n) -> p c b n", c=KC, b=2)

            def norm0(it, kind, t):
                n = norm_no(NORMS0, it, kind, t)
                dve.wait_ge(L0.rstd, n + 1)
                nc.vector.tensor_scalar(xn, xa[:, t, :], rstd, float(D) ** 0.5, ALU.mult, ALU.mult).then_inc(L0.xn, 1)
                dve.wait_ge(L0.nt, n + 1)
                dve.wait_ge(L0.tables, 32 * (it + 1))
                nc.vector.tensor_tensor(by_seq(xn), by_seq(ps_c[:]), gain(kind, t), ALU.mult).then_inc(L0.h32, 1)

            def attn0(stage, it, t):
                n = tile(it, t)
                if stage in ("norm1", "norm2"):
                    norm0(it, stage, t)
                if stage == "proj":
                    dve.wait_ge(L0.proj, n + 1)
                    dve.wait_ge(L0.kk, n)
                    dve.wait_ge(L0.tables, 32 * (it + 1))
                    dve.wait_ge(L0.vv, 64 * n)
                    nc.vector.tensor_scalar(v0[:, 0], ps_pq[:, 576:640], INV, None, ALU.mult).then_inc(L0.v_hi, 1)
                    q = ps_pq[:, 0:576].rearrange("p (g s f) -> p g s f", g=9, s=2)
                    r1 = rot.rearrange("p (g s f) -> p g s f", g=9, s=2)
                    r2 = rot2.rearrange("p (g s f) -> p g s f", g=9, s=2)
                    cos = rope[:, t, 0, :].unsqueeze(1).unsqueeze(1).to_broadcast([P, 9, 2, 32])
                    sin = rope[:, t, 1, :].unsqueeze(1).to_broadcast([P, 9, 32])
                    nc.vector.tensor_tensor(r1, q, cos, ALU.mult).then_inc(L0.qk32, 1)
                    nc.vector.tensor_tensor(r2[:, :, 0, :], q[:, :, 1, :], sin, ALU.mult).then_inc(L0.qk32, 1)
                    nc.vector.tensor_tensor(r2[:, :, 1, :], q[:, :, 0, :], sin, ALU.mult).then_inc(L0.qk32, 1)
                    dve.wait_ge(L0.v_hi, n + 1)
                    nc.vector.scalar_tensor_tensor(v0[:, 1], ps_pq[:, 576:640], INV, v0[:, 0], ALU.mult,
                                                   ALU.subtract).then_inc(L0.v16, 1)
                    dve.wait_ge(L0.qk32, 3 * n + 3)
                    nc.vector.tensor_tensor(r1[:, :, 0, :], r1[:, :, 0, :], r2[:, :, 0, :], ALU.subtract).then_inc(L0.sq, 1)
                    nc.vector.tensor_tensor(r1[:, :, 1, :], r1[:, :, 1, :], r2[:, :, 1, :], ALU.add).then_inc(L0.rot, 1)
                if stage == "turn":
                    dve.wait_ge(L0.turned, n + 1)
                    dve.wait_ge(L0.scores, n)
                    nc.vector.tensor_copy(qf0.rearrange("p b g q -> p g b q"),
                                          as16(ps_c[:], 8).rearrange("p g (b q) -> p g b q", b=2)).then_inc(L0.qf, 1)
                if stage == "scores":
                    softmax(L0, e0, ps_d[:], n, n)
                if stage == "mix":
                    dve.wait_ge(L0.c_hi, n + 1)
                    nc.vector.tensor_tensor(ctx0[:, 1], ps_d[:].rearrange("p (c n) -> p c n", c=KC), ctx0[:, 0],
                                            ALU.subtract).then_inc(L0.c_lo, 1)
                if stage == "out":
                    dve.wait_ge(L0.o, n + 1)
                    nc.vector.scalar_tensor_tensor(xa[:, t, :], ps_d[:], INV, xa[:, t, :], ALU.mult,
                                                   ALU.add).then_inc(L0.x1, 1)

            def softmax(L, e, bank, m, n):
                s3 = bank.rearrange("p (g t) -> p g t", g=8)
                dve.wait_ge(L.scores, m + 1)
                dve.wait_ge(L.p_lo, m)
                if L is L1:
                    dve.wait_ge(L.sum, m)
                    nc.vector.tensor_tensor(e, s3, mask_t.unsqueeze(1).to_broadcast([P, 8, SEQ]), ALU.add).then_inc(L.mx0, 1)
                    dve.wait_ge(L.mx0, m + 1)
                    s3 = e
                nc.vector.tensor_reduce(row_max, s3, AX_X, ALU.max).then_inc(L.mx, 1)
                dve.wait_ge(L.mx, m + 1)
                nc.vector.tensor_tensor(e, s3, row_max.unsqueeze(2).to_broadcast([P, 8, SEQ]), ALU.subtract).then_inc(L.shift, 1)
                dve.wait_ge(L.e, m + 1)
                nc.vector.tensor_reduce(row_sum, e, AX_X, ALU.add).then_inc(L.sum, 1)
                dve.wait_ge(L.sum, m + 1)
                nc.vector.reciprocal(row_inv, row_sum).then_inc(L.inv, 1)
                dve.wait_ge(L.inv, m + 1)
                nc.vector.tensor_tensor(e, e, row_inv.unsqueeze(2).to_broadcast([P, 8, SEQ]), ALU.mult).then_inc(L.prob, 1)

            for s in range(SLOTS0):
                if FIRST + s < SETUP:
                    cut_lo(FIRST + s)
                for stage, t in TABLE0[s]:
                    attn0(stage, 0, t)

            def slots0(it, both):
                for s in range(SLOTS0):
                    if s < IC:
                        dve.wait_ge(L0.act, it * IC + s + 1)
                        a = act0[:, s % 2, :]
                        nc.vector.scalar_tensor_tensor(a, a, 1.0, ps_m[2 * (s % 2)][:], ALU.add, ALU.mult).then_inc(L0.gated, 1)
                        dve.wait_ge(L0.gated, it * IC + s + 1)
                        nc.vector.scalar_tensor_tensor(a, a, 0.5 * INV * INV, ps_m[2 * (s % 2) + 1][:], ALU.mult,
                                                       ALU.mult).then_inc(L0.m32, 1)
                    if both:
                        for stage, t in TABLE0[s]:
                            attn0(stage, it + 1, t)
                    elif s >= IC:
                        cut_lo(SETUP + s - IC)
                    if s >= IC and (s - IC) % 2 == 1:
                        t = (s - IC) // 2
                        dve.wait_ge(L0.down, it * 8 + s - IC + 1)
                        dve.wait_ge(L0.hand, 16 * (tile(it, t) + 1))
                        nc.vector.scalar_tensor_tensor(xm[:, t, :], ps_m[t % 2][:], INV, xm[:, t, :], ALU.mult,
                                                       ALU.add).then_inc(L0.y, 1)

            with dve.Fori(0, NBLK - 1) as i:
                slots0(i, True)
            slots0(NBLK - 1, False)

            dve.wait_ge(s_l1c, 16 * 8)
            nc.vector.tensor_scalar(sm_scale, sm_scale, 4.605170185988092, None, ALU.min).then_inc(s_l1s, 1)

            def norm1(it, kind, t):
                n = norm_no(NORMS1, it, kind, t)
                if kind == "norm1":
                    dve.wait_ge(L1.x_in, 16 * (tile(it, t) + 1))
                else:
                    dve.wait_ge(L1.x1, tile(it, t) + 1)
                nc.vector.bn_stats(stats[:, 0:6], xa[:, t, :]).then_inc(L1.stat0, 1)
                dve.wait_ge(L1.stat0, n + 1)
                nc.vector.memset(spare, 0.0)
                nc.vector.bn_aggr(moments, stats[:, 0:6]).then_inc(L1.stat, 1)
                dve.wait_ge(L1.rstd, n + 1)
                dve.wait_ge(L1.h_lo, n)
                dve.wait_ge(L1.stat, n + 1)
                nc.vector.tensor_scalar(xn, xa[:, t, :], moments[:, 0:1], rstd, ALU.subtract, ALU.mult).then_inc(L1.xn, 1)
                dve.wait_ge(L1.nt, n + 1)
                dve.wait_ge(L1.tables, 16 * (it + 1))
                nc.vector.tensor_tensor(by_seq(xn), by_seq(ps_c[:]), gain(kind, t), ALU.mult).then_inc(L1.h_scaled, 1)
                dve.wait_ge(L1.h_scaled, n + 1)
                nc.vector.tensor_tensor(by_seq(xn), by_seq(xn), gain(kind, t, 2), ALU.add).then_inc(L1.h32, 1)

            def attn1(stage, it, t):
                n = tile(it, t)
                if stage in ("norm1", "norm2"):
                    norm1(it, stage, t)
                if stage == "proj":
                    dve.wait_ge(L1.proj, n + 1)
                    dve.wait_ge(L1.q_lo, 4 * n)
                    dve.wait_ge(L1.kk, 4 * n)
                    nc.vector.scalar_tensor_tensor(qk1[:, 0:512], ps_pq[:, 0:512], INV, q_bias_t, ALU.mult,
                                                   ALU.add).then_inc(L1.qk32, 1)
                    dve.wait_ge(L1.v_hi, n + 1)
                    nc.vector.scalar_tensor_tensor(v1[:, 1], ps_d[:], INV, v1[:, 0], ALU.mult,
                                                   ALU.subtract).then_inc(L1.v16, 1)
                    dve.wait_ge(L1.sq, n + 1)
                    nc.vector.tensor_reduce(norm_sq, sq1.rearrange("p (g d) -> p g d", g=32), AX_X, ALU.add).then_inc(L1.nsum, 1)
                    dve.wait_ge(L1.nsum, n + 1)
                    nc.vector.tensor_scalar(norm_sq, norm_sq, 1e-24, None, ALU.max).then_inc(L1.nmax, 1)
                    dve.wait_ge(L1.ninv, n + 1)
                    qk = qk1.rearrange("p (g d) -> p g d", g=32)
                    nc.vector.tensor_tensor(qk, qk, norm_inv.unsqueeze(2).to_broadcast([P, 32, HD1]), ALU.mult).then_inc(L1.normed, 1)
                for h in range(2):
                    if stage == ("turn0", "turn1_scores0")[h]:
                        dve.wait_ge(L1.turned, 2 * n + h + 1)
                        dve.wait_ge(L1.scores, 2 * n + h)
                        nc.vector.tensor_copy(qf1, as16(ps_c[:], HALF)).then_inc(L1.qf, 1)
                    if stage == ("turn1_scores0", "scores1_turn_p0")[h]:
                        softmax(L1, e1, ps_d[:] if h == 0 else ps_pq[:, 512:1024], 2 * n + h, n)
                if stage == "mix1":
                    dve.wait_ge(L1.mixed, 2 * n + 2)
                    dve.wait_ge(L1.x1, n)
                    nc.vector.tensor_tensor(ctx32.rearrange("p (c n) -> p c n", c=KC), ps_d[:].rearrange("p (c n) -> p c n", c=KC),
                                            v_bias_t.unsqueeze(2).to_broadcast([P, KC, P]), ALU.add).then_inc(L1.c32, 1)
                    dve.wait_ge(L1.c_hi, n + 1)
                    nc.vector.tensor_tensor(ctx1[:, 1], ctx32.rearrange("p (c n) -> p c n", c=KC), ctx1[:, 0],
                                            ALU.subtract).then_inc(L1.c_lo, 1)
                if stage == "out":
                    dve.wait_ge(L1.o, n + 1)
                    nc.vector.scalar_tensor_tensor(ctx32, ps_d[:], INV, b_proj_t, ALU.mult, ALU.add).then_inc(L1.o_b, 1)
                    dve.wait_ge(L1.o_b, n + 1)
                    dve.wait_ge(L1.gam_a, 32 * (n + 1))
                    nc.vector.tensor_tensor(ctx32, ctx32, gamma_a, ALU.mult).then_inc(L1.o_g, 1)

            for s in range(SLOTS1):
                if SWAP + s < len(groups):
                    cut_lo(SWAP + s)
                for stage, t in TABLE1[s]:
                    attn1(stage, 0, t)

            C0 = 0.7978845608028654

            def slots1(it, both):
                for s in range(SLOTS1):
                    if s < IC:
                        dve.wait_ge(L1.usq, it * IC + s + 1)
                        g = g1[:, s % 2, :]
                        nc.vector.tensor_scalar(g, g, 0.044715 * C0, C0, ALU.mult, ALU.add).then_inc(L1.poly, 1)
                        dve.wait_ge(L1.act, it * IC + s + 1)
                        u = u1[:, s % 2, :]
                        nc.vector.scalar_tensor_tensor(u, g, 1.0, u, ALU.add, ALU.mult).then_inc(L1.m32, 1)
                    if both:
                        for stage, t in TABLE1[s]:
                            attn1(stage, it + 1, t)
                    if s >= IC and (s - IC) % 4 == 3:
                        t = (s - IC) // 4
                        m = tile(it, t)
                        dve.wait_ge(L1.down, it * 16 + s - IC + 1)
                        dve.wait_ge(L1.m_lo, (it + 1) * IC)
                        dve.wait_ge(L1.y, m)
                        d = u1[:, 0, :]
                        nc.vector.scalar_tensor_tensor(d, ps_m[t % 2][:], 0.5 * INV, b_fc2_t, ALU.mult, ALU.add).then_inc(L1.d_b, 1)
                        dve.wait_ge(L1.d_b, m + 1)
                        dve.wait_ge(L1.gam_m, 32 * (m + 1))
                        nc.vector.tensor_tensor(d, d, gamma_m, ALU.mult).then_inc(L1.d_g, 1)
                        dve.wait_ge(L1.d_g, m + 1)
                        dve.wait_ge(L1.hand, 16 * (m + 1))
                        nc.vector.tensor_tensor(xm[:, t, :], xm[:, t, :], d, ALU.add).then_inc(L1.y, 1)

            with dve.Fori(0, NBLK - 1) as i:
                slots1(i, True)
            slots1(NBLK - 1, False)

        @block.tensor
        def _(pe):
            PASSES = ((0, 0), (0, 1), (1, 0))

            def products(jobs, left, chunks, first=True, last=True):
                ins = None
                for k in chunks:
                    for a, b in PASSES:
                        for o, right in jobs:
                            ins = nc.tensor.matmul(o, left(a, k), right(b, k),
                                                   start=(first and k == chunks[0] and (a, b) == PASSES[0]),
                                                   stop=(last and k == chunks[-1] and (a, b) == PASSES[-1]),
                                                   skip_group_check=True)
                return ins

            def ada(g, n):
                pe.wait_ge(s_wlo, g + 1)
                pe.wait_ge(s_cond, 1)
                if n >= 2:
                    pe.wait_ge(s_ada_out, n - 1)
                bank = ps_m[n % 2]
                c = cond_cut if n < 2 else silu_cut
                if 2 <= n < 4:
                    ins = products([(bank[0:NSEQ, :], lambda b, k: ada_cut[:, b, k, :])],
                                   lambda a, k: c[:, a, k, :], range(KC))
                else:
                    for f in range(KC):
                        ins = products([(bank[:, NSEQ * f:NSEQ * (f + 1)], lambda b, k: c[:, b, k, :])],
                                       lambda a, k: ada_cut[:, a, k, P * f:P * (f + 1)], range(KC))
                ins.then_inc(s_ada, 1)

            def setup_group(g):
                if groups[g][0] == "ada":
                    ada(g, groups[g][1])

            for g in range(FIRST):
                setup_group(g)

            pe.wait_ge(s_const, 5)

            def norm(L, norms, it, kind, t):
                n = norm_no(norms, it, kind, t)
                pe.wait_ge(L.xn, n + 1)
                if L is L0:
                    pe.wait_ge(L.h32, n)
                    done = sum(1 for s, q in order_of(TABLE0, ("norm1", "norm2", "turn"))[:order_of(TABLE0, ("norm1", "norm2", "turn")).index((kind, t))] if s == "turn")
                    pe.wait_ge(L.qf, tile(it, 0) + done)
                else:
                    order = order_of(TABLE1, ("norm1", "norm2", "turn0", "turn1_scores0"))
                    done = sum(1 for s, q in order[:order.index((kind, t))] if s[0:4] == "turn")
                    pe.wait_ge(L.h_scaled, n)
                    pe.wait_ge(L.qf, 2 * tile(it, 0) + done)
                for c in range(KC):
                    ins = nc.tensor.transpose(ps_c[:, P * c:P * (c + 1)], xn[:, P * c:P * (c + 1)], ident32[:])
                ins.then_inc(L.nt, 1)

            def norms_before(table, norms, it, stage, t, stages):
                order = order_of(table, ("norm1", "norm2") + stages)
                done = sum(1 for s, q in order[:order.index((stage, t))] if s in ("norm1", "norm2"))
                return it * len(norms) + done

            def attn0(stage, it, t):
                n = tile(it, t)
                if stage in ("norm1", "norm2"):
                    norm(L0, NORMS0, it, stage, t)
                if stage == "proj":
                    pe.wait_ge(s_wlo, 3)
                    pe.wait_ge(L0.h_lo, norm_no(NORMS0, it, "norm1", t) + 1)
                    pe.wait_ge(L0.kf, n)
                    left = lambda a, k: h_attn[:, t % 2, a, k, :]
                    products([(ps_pq[:, 0:512], lambda b, k: qkv0_w[:, b, k, 0:512]),
                              (ps_pq[:, 512:640], lambda b, k: qkv0_w[:, b, k, 512:640])],
                             left, range(KC)).then_inc(L0.proj, 1)
                if stage == "turn":
                    pe.wait_ge(L0.q_lo, n + 1)
                    pe.wait_ge(L0.kk, n + 1)
                    pe.wait_ge(L0.rot, n + 1)
                    pe.wait_ge(L0.v16, n + 1)
                    pe.wait_ge(L0.h32, norms_before(TABLE0, NORMS0, it, stage, t, ("turn",)))
                    pe.wait_ge(L0.qf, n)
                    for g in range(HEADS0):
                        nc.tensor.transpose(as16(ps_c[:], 8)[:, g, :], qk0[:, g].rearrange("p h d -> p (h d)"), ident16[:])
                    for h in range(2):
                        ins = nc.tensor.transpose(as16(ps_pq[:, 0:128], 2)[:, h, :], kk0[:, h].rearrange("p r d -> p (r d)"), ident16[:])
                    ins.then_inc(L0.turned, 1)
                if stage == "scores":
                    pe.wait_ge(L0.qf, n + 1)
                    pe.wait_ge(L0.kf, n + 1)
                    pe.wait_ge(L0.x1, n)
                    for b in range(2):
                        for hp in range(4):
                            for h in range(2):
                                ins = nc.tensor.matmul(ps_d[:, (4 * b + hp) * SEQ:(4 * b + hp + 1) * SEQ],
                                                       qf0[:, b, 2 * hp:2 * hp + 2, :].rearrange("p g q -> p (g q)"),
                                                       kf0[:, h, SEQ * b:SEQ * (b + 1)], start=(h == 0), stop=(h == 1))
                    ins.then_inc(L0.scores, 1)
                if stage == "turn_p":
                    pe.wait_ge(L0.p_lo, n + 1)
                    pe.wait_ge(L0.shift, n + 1)
                    for g in range(8):
                        ins = nc.tensor.transpose(as16(ps_d[:], 8)[:, g, :], p0[:, g].rearrange("p h t -> p (h t)"), ident16[:])
                    ins.then_inc(L0.p_turned, 1)
                if stage == "mix":
                    pe.wait_ge(L0.pt, n + 1)
                    pe.wait_ge(L0.vv, 64 * (n + 1))
                    o = ps_d[:].rearrange("p (c b q) -> p c b q", c=KC, b=2)
                    for b in range(2):
                        for h in range(2):
                            for par in range(2):
                                ins = nc.tensor.matmul(o[SEQ * par:SEQ * (par + 1), :, b, :], vv0[:, b, h, :],
                                                       pt0[:, 4 * b:4 * b + 4, SEQ * par:SEQ * (par + 1)],
                                                       start=(h == 0), stop=(h == 1))
                    ins.then_inc(L0.mixed, 1)
                if stage == "out":
                    pe.wait_ge(s_wlo, 4)
                    pe.wait_ge(L0.c_lo, n + 1)
                    products([(ps_d[:], lambda b, k: wo0_w[:, b, k, :])],
                             lambda a, k: ctx0[:, a, k, :], range(KC)).then_inc(L0.o, 1)

            for s in range(SLOTS0):
                if FIRST + s < SETUP:
                    setup_group(FIRST + s)
                for stage, t in TABLE0[s]:
                    attn0(stage, 0, t)
            pe.wait_ge(s_wlo, SETUP)

            def slots0(it, both):
                for s in range(SLOTS0):
                    if s < IC:
                        if s == 0:
                            pe.wait_ge(L0.h_lo, (it + 1) * len(NORMS0))
                        if s >= 2:
                            pe.wait_ge(L0.m32, it * IC + s - 1)
                        else:
                            pe.wait_ge(L0.y, tile(it, 0))
                        right = lambda b, k: h_mlp[:, b, k, :]
                        for w, bank in ((gate_w, ps_m[2 * (s % 2)]), (up_w, ps_m[2 * (s % 2) + 1])):
                            ins = products([(bank[:], right)], lambda a, k: w[:, a, k, P * s:P * (s + 1)], range(KC))
                        ins.then_inc(L0.up, 1)
                    else:
                        t, half = (s - IC) // 2, (s - IC) % 2
                        chunks = range(8 * half, 8 * half + 8)
                        pe.wait_ge(L0.m_lo, it * IC + chunks[-1] + 1)
                        if half == 0:
                            pe.wait_ge(L0.m32, (it + 1) * IC)
                            if t >= 2:
                                pe.wait_ge(L0.y, tile(it, t) - 1)
                        products([(ps_m[t % 2][:], lambda b, k: down_w[:, b, k, :])],
                                 lambda a, k: inner[:, a, k, P * t:P * (t + 1)], chunks,
                                 first=(half == 0), last=(half == 1)).then_inc(L0.down, 1)
                    if both:
                        for stage, t in TABLE0[s]:
                            attn0(stage, it + 1, t)

            with pe.Fori(0, NBLK - 1) as i:
                slots0(i, True)
            slots0(NBLK - 1, False)

            def attn1(stage, it, t):
                n = tile(it, t)
                if stage in ("norm1", "norm2"):
                    norm(L1, NORMS1, it, stage, t)
                if stage == "proj":
                    pe.wait_ge(L1.h_lo, norm_no(NORMS1, it, "norm1", t) + 1)
                    pe.wait_ge(L1.kf, 2 * n)
                    pe.wait_ge(L1.pt, 2 * n)
                    left = lambda a, k: h_attn[:, t % 2, a, k, :]
                    products([(ps_pq[:, 512 * q:512 * (q + 1)], lambda b, k, q=q: qkv1_w[:, b, k, 512 * q:512 * (q + 1)])
                              for q in range(2)], left, range(KC)).then_inc(L1.proj, 1)
                    pe.wait_ge(L1.o_b, n)
                    products([(ps_d[:], lambda b, k: qkv1_w[:, b, k, 1024:1536])], left, range(KC)).then_inc(L1.projv, 1)
                for h in range(2):
                    if stage == ("turn0", "turn1_scores0")[h]:
                        pe.wait_ge(L1.q_lo, 4 * n + 2 * h + 2)
                        pe.wait_ge(L1.kk, 4 * n + 2 * h + 2)
                        pe.wait_ge(L1.h_scaled, norms_before(TABLE1, NORMS1, it, stage, t, ("turn0", "turn1_scores0")))
                        pe.wait_ge(L1.qf, 2 * n + h)
                        pe.wait_ge(L1.kf, 2 * n + h)
                        pe.wait_ge(L1.qk32, n + 1)
                        for g in range(HALF):
                            nc.tensor.transpose(as16(ps_c[:], HALF)[:, g, :], q16[:, g].rearrange("p r d -> p (r d)"), ident16[:])
                        for g in range(HALF):
                            ins = nc.tensor.transpose(as16(ps_pq[:, 0:512], HALF)[:, g, :], k16[:, g].rearrange("p r d -> p (r d)"), ident16[:])
                        ins.then_inc(L1.turned, 1)
                for h in range(2):
                    bank = ps_d[:] if h == 0 else ps_pq[:, 512:1024]
                    if stage == ("turn1_scores0", "scores1_turn_p0")[h]:
                        pe.wait_ge(L1.qf, 2 * n + h + 1)
                        pe.wait_ge(L1.kf, 2 * n + h + 1)
                        pe.wait_ge(L1.v16, n + 1)
                        pe.wait_ge(L1.rot, n + 1)
                        for b in range(2):
                            for g in range(HALF):
                                ins = nc.tensor.matmul(bank[SEQ * b:SEQ * (b + 1), SEQ * g:SEQ * (g + 1)],
                                                       qf1[:, g, SEQ * b:SEQ * (b + 1)], kf1[:, g, SEQ * b:SEQ * (b + 1)],
                                                       start=True, stop=True)
                        ins.then_inc(L1.scores, 1)
                for h in range(2):
                    bank = ps_d[:] if h == 0 else ps_pq[:, 512:1024]
                    if stage == ("mix0_turn_p1", "mix1")[h]:
                        pe.wait_ge(L1.pt, 2 * n + h + 1)
                        pe.wait_ge(L1.vv, 64 * (n + 1))
                        o = ps_d[:].rearrange("p (c b q) -> p c b q", c=KC, b=2)
                        for b in range(2):
                            for g in range(HALF):
                                hd = HALF * h + g
                                row = HD1 * (hd % 4)
                                for a in range(2):
                                    ins = nc.tensor.matmul(o[row:row + HD1, hd // 4, b, :], vv1[:, b, a, HD1 * hd:HD1 * (hd + 1)],
                                                           pt1[:, g, SEQ * b:SEQ * (b + 1)], start=(a == 0), stop=(a == 1))
                        ins.then_inc(L1.mixed, 1)
                    if stage == ("scores1_turn_p0", "mix0_turn_p1")[h]:
                        pe.wait_ge(L1.p_lo, 2 * n + h + 1)
                        pe.wait_ge(L1.mx0, 2 * n + h + 1)
                        for g in range(HALF):
                            ins = nc.tensor.transpose(as16(bank, HALF)[:, g, :], p1[:, g].rearrange("p h t -> p (h t)"), ident16[:])
                        ins.then_inc(L1.p_turned, 1)
                if stage == "out":
                    pe.wait_ge(L1.c_lo, n + 1)
                    pe.wait_ge(L1.c32, n + 1)
                    products([(ps_d[:], lambda b, k: proj1_w[:, b, k, :])],
                             lambda a, k: ctx1[:, a, k, :], range(KC)).then_inc(L1.o, 1)

            pe.wait_ge(s_wlo, SETUP + 4)
            for s in range(SLOTS1):
                for stage, t in TABLE1[s]:
                    attn1(stage, 0, t)
            pe.wait_ge(s_wlo, len(groups))

            def slots1(it, both):
                for s in range(SLOTS1):
                    if s < IC:
                        if s == 0:
                            pe.wait_ge(L1.h_lo, (it + 1) * len(NORMS1))
                        if s >= 4:
                            pe.wait_ge(L1.u, it * IC + s - 3)
                        else:
                            pe.wait_ge(L1.d_b, tile(it, 0))
                        products([(ps_m[s % 4][:], lambda b, k: h_mlp[:, b, k, :])],
                                 lambda a, k: fc1_w[:, a, k, P * s:P * (s + 1)], range(KC)).then_inc(L1.up, 1)
                    else:
                        t, part = (s - IC) // 4, (s - IC) % 4
                        chunks = range(4 * part, 4 * part + 4)
                        pe.wait_ge(L1.m_lo, it * IC + chunks[-1] + 1)
                        if part == 0:
                            pe.wait_ge(L1.u, (it + 1) * IC)
                            if t >= 2:
                                pe.wait_ge(L1.d_b, tile(it, t) - 1)
                        products([(ps_m[t % 2][:], lambda b, k: fc2_w[:, b, k, :])],
                                 lambda a, k: inner[:, a, k, P * t:P * (t + 1)], chunks,
                                 first=(part == 0), last=(part == 3)).then_inc(L1.down, 1)
                    if both:
                        for stage, t in TABLE1[s]:
                            attn1(stage, it + 1, t)

            with pe.Fori(0, NBLK - 1) as i:
                slots1(i, True)
            slots1(NBLK - 1, False)


def kernel(**inputs):
    import numpy as np
    import concourse.bacc as bacc
    from concourse.bass_utils import run_bass_kernel_spmd

    a = {k: np.asarray(v) for k, v in inputs.items()}

    def chunked(v, c):
        return np.ascontiguousarray(v.reshape(c, P, *v.shape[1:]).swapaxes(0, 1))

    b_ada = a["L1_cond_bada"]
    host = {
        "x": a["x"].reshape(NSEQ * SEQ, D),
        "pos": np.ascontiguousarray(a["pos_BxS"].reshape(NBLK * TILES, P).T),
        "cond_t": chunked(np.ascontiguousarray(a["cond_2048"].T), KC),
        "mask": a["mask_1x1xSxS_ff0"].reshape(SEQ, SEQ),
        "ln_w": np.concatenate([chunked(a["L0_cond_ln1_w"], KC), chunked(a["L0_cond_ln2_w"], KC)], axis=1),
        "tw_t": np.stack([a["L0_cond_ln1_tw"].T, a["L0_cond_ln2_tw"].T]),
        "wqkv0_t": np.concatenate([a["L0_cond_Wq"].T, a["L0_cond_Wk"].T, a["L0_cond_Wv"].T], axis=1),
        "wo0_t": a["L0_cond_Wo"].T,
        "wg_t": a["L0_cond_Wg"].T,
        "wu_t": a["L0_cond_Wu"].T,
        "wd_t": a["L0_cond_Wd"].T,
        "wqkv1_t": a["L1_cond_Wqkv"].T,
        "q_bias": a["L1_cond_q_bias"].reshape(1, D),
        "v_bias": chunked(a["L1_cond_v_bias"], KC),
        "scale_log": a["L1_cond_scale_mul_log"].reshape(1, HEADS1),
        "wproj_t": a["L1_cond_Wproj"].T,
        "b_proj": a["L1_cond_bproj"].reshape(1, D),
        "wada_t": a["L1_cond_Wada"].T,
        "b_ada": chunked(b_ada, 6 * KC),
        "b_ada_row": b_ada.reshape(6, D),
        "wfc1_t": a["L1_cond_Wfc1"].T,
        "b_fc1": chunked(a["L1_cond_bfc1"], IC),
        "wfc2_t": a["L1_cond_Wfc2"].T,
        "b_fc2": a["L1_cond_bfc2"].reshape(1, D),
    }
    nc = bacc.Bacc("TRN2", target_bir_lowering=False, num_devices=1)
    arrays, args = {}, []
    for name, v in host.items():
        v = np.ascontiguousarray(v)
        arrays[name] = v
        args.append(nc.dram_tensor(name, v.shape, mybir.dt.from_np(v.dtype), kind="ExternalInput").ap())
    out = nc.dram_tensor("out", (NSEQ * SEQ, D), F32, kind="ExternalOutput").ap()
    layers_kernel(nc, *args, out)
    r = run_bass_kernel_spmd(nc, [arrays], core_ids=[0])
    return r.results[0]["out"].reshape(NSEQ, SEQ, D)
```

```python
from contextlib import ExitStack

import concourse.bass as bass
from concourse import mybir

ALU = mybir.AluOpType
ACT = mybir.ActivationFunctionType
F32 = mybir.dt.float32
F16 = mybir.dt.float16
I32 = mybir.dt.int32
AX_X = mybir.AxisListType.X

P = 128
D = 512
KC = D // P
SEQ = 64
NSEQ = 64
BLOCK = 512
TILES = BLOCK // P
NBLK = NSEQ * SEQ // BLOCK
INTER = 2048
IC = INTER // P
HEADS0, HD0 = 8, 64
HEADS1, HD1 = 16, 32
HALF = HEADS1 // 2
QKV0 = D + 2 * HD0
EPS = 1e-6
GELU_C = 0.7978845608028654
WS = 16.0
INV = 1.0 / WS
TWO_PI = 6.283185307179586
PI_HIGH = 6.28125
PI_LOW = TWO_PI - PI_HIGH
ROUND = 12582912.0
PI_IN = 3.1415925

SLOTS0 = 24
SLOTS1 = 34


def slot_table(slots, stages, starts, second_norm):
    table = [[] for _ in range(slots)]
    for t, first in enumerate(starts):
        for n, stage in enumerate(stages):
            table[first + n].insert(0, (stage, t))
    for t, s in enumerate(second_norm):
        table[s + 1].append(("norm2", t))
        table[s].append(("stat2", t))
    return table


TABLE0 = slot_table(SLOTS0, ["stat1", "norm1", "proj", "turn", "scores", "softmax", "turn_p", "mix", "out"],
                    [0, 4, 8, 12], [16, 18, 20, 22])
TABLE1 = slot_table(SLOTS1, ["stat1", "norm1", "proj", "projv", "prep0", "turn0", "scores0", "turn1",
                             "scores1_turn_p0", "mix0", "turn_p1", "mix1", "out"],
                    [0, 6, 12, 18], [20, 22, 27, 31])


def order_of(table, stages):
    return [(s, t) for slot in table for s, t in slot if s in stages]


def count_before(table, it, at, of):
    order = order_of(table, of + (at[0],))
    return it * len(order_of(table, of)) + sum(1 for s, _ in order[:order.index(at)] if s in of)


COST0 = {"norm1": 2, "norm2": 2, "proj": 16, "turn": 3, "scores": 4, "turn_p": 2, "mix": 3, "out": 12}
COST1 = {"norm1": 2, "norm2": 2, "proj": 24, "projv": 12, "turn0": 4, "scores0": 2, "turn1": 4,
         "scores1_turn_p0": 4, "mix0": 4, "turn_p1": 2, "mix1": 4, "out": 12}


def deal(table, cost, jobs):
    total = sum(cost.get(s, 0) for slot in table for s, _ in slot) + sum(job[-1] for job in jobs)
    done, left, dealt = 0, list(jobs), []
    for n, slot in enumerate(table):
        done += sum(cost.get(s, 0) for s, _ in slot)
        dealt.append([])
        while left and (done + left[0][-1] / 2 <= total * (n + 1) / len(table) or n == len(table) - 1):
            done += left[0][-1]
            dealt[-1].append(left.pop(0))
    return dealt


JOBS0 = deal(TABLE0, COST0, [(kind, j, 0, KC, 3 * KC) for j in range(IC) for kind in ("gate", "up")]
             + [("down", t, k, k + 4, 12) for t in range(TILES) for k in range(0, IC, 4)])
JOBS1 = deal(TABLE1, COST1, [("up", j, k, k + 2, 6) for j in range(IC) for k in (0, 2)]
             + [("down", t, k, k + 2, 6) for t in range(TILES) for k in range(0, IC, 2)])


def ending(jobs, kind, last):
    return [[job[1] for job in slot if job[0] == kind and job[3] == last] for slot in jobs]


UPS0, DOWNS0 = ending(JOBS0, "up", KC), ending(JOBS0, "down", IC)
UPS1, DOWNS1 = ending(JOBS1, "up", KC), ending(JOBS1, "down", IC)

NORMS0 = order_of(TABLE0, ("norm1", "norm2"))
NORMS1 = order_of(TABLE1, ("norm1", "norm2"))


def layers_kernel(nc, x, pos, cond_t, mask, ln_w, tw_t, wqkv0_t, wo0_t, wg_t, wu_t, wd_t,
                  wqkv1_t, q_bias, v_bias, scale_log, wproj_t, b_proj, wada_t, b_ada, b_ada_row,
                  wfc1_t, b_fc1, wfc2_t, b_fc2, out):
    with ExitStack() as ctx:
        def sb(name, shape, dt):
            return ctx.enter_context(nc.sbuf_tensor(name, shape, dt))

        def sem(name):
            return ctx.enter_context(nc.semaphore(name))

        x_mid = nc.dram_tensor("x_mid", (NSEQ * SEQ, D), F32, kind="Internal").ap()
        rope_dram = nc.dram_tensor("rope_tables", (P, NBLK * TILES, 2, 32), F32, kind="Internal").ap()
        gain0_dram = nc.dram_tensor("gain0", (NBLK, P, 2, KC, 8), F32, kind="Internal").ap()
        mod1_dram = nc.dram_tensor("mod1", (NBLK, P, 4, KC, 8), F32, kind="Internal").ap()
        gamma_dram = nc.dram_tensor("gamma", (2, NSEQ, D), F32, kind="Internal").ap()

        weights = sb("weights", [P, 58368], F16)
        region_a, region_b, region_c = weights[:, 0:32768], weights[:, 32768:49152], weights[:, 49152:58368]

        def cut(ap, k):
            return ap.rearrange("p (h k n) -> p h k n", h=2, k=k)

        gate_w, up_w = cut(region_a[:, 0:16384], KC), cut(region_a[:, 16384:32768], KC)
        down_w = cut(region_b, IC)
        qkv0_w, wo0_w = cut(region_c[:, 0:5120], KC), cut(region_c[:, 5120:9216], KC)
        qkv1_w, proj1_w = cut(region_a[:, 0:12288], KC), cut(region_a[:, 12288:16384], KC)
        fc1_w, fc2_w = cut(region_a[:, 16384:32768], KC), cut(region_b, IC)

        xa = sb("x_attn", [P, TILES, D], F32)
        xm = sb("x_mlp", [P, TILES, D], F32)
        h_attn = sb("h_attn", [P, 2, 2, KC, P], F16)
        h_mlp = sb("h_mlp", [P, 2, KC, BLOCK], F16)
        inner = sb("inner", [P, 2, IC, BLOCK], F16)
        ident32 = sb("ident32", [P, P], F32)
        ident16 = sb("ident16", [P, P], F16)
        scratch = sb("scratch", [P, 8300], F32)

        taken = {"scratch": 0, "c": 0}

        def carve(n32, where="scratch"):
            at = taken[where]
            taken[where] = at + n32
            if where == "c":
                return region_c[:, 2 * at:2 * (at + n32)].bitcast(F32)
            assert at + n32 <= 8300, at + n32
            return scratch[:, at:at + n32]

        xn = carve(512)
        small = carve(256)
        stats = small[:, 0:8]
        moments = small[:, 8:10]
        rstd = small[:, 10:11]
        var_eps = small[:, 11:12]
        minus_half = small[:, 12:44]
        row_max = small[:, 44:52]
        row_sum = small[:, 52:60]
        row_inv = small[:, 60:68]
        norm_sq = small[:, 68:100]
        norm_inv = small[:, 100:132]
        sm_scale = small[:, 132:148]
        v_bias_t = small[:, 148:152]
        b_fc1_t = small[:, 152:168]
        mask_t = small[:, 168:232]
        spare = small[:, 232:233]
        eps_t = small[:, 233:234]
        eps_t0 = small[:, 234:235]
        gains = carve(128)
        base = taken["scratch"]
        act0 = carve(1024).rearrange("p (a n) -> p a n", a=2)
        qk0 = carve(8 * 2 * 64 // 2).bitcast(F16).rearrange("p (g h d) -> p g h d", g=HEADS0, h=2)
        kk0 = carve(128).bitcast(F16).rearrange("p (h r d) -> p h r d", h=2, r=2)
        rot = carve(576)
        rot2 = carve(576)
        qf0 = carve(512).bitcast(F16).rearrange("p (b g q) -> p b g q", b=2, g=HEADS0)
        kf0 = carve(128).bitcast(F16).rearrange("p (h n) -> p h n", h=2)
        v0 = carve(64).bitcast(F16).rearrange("p (h d) -> p h d", h=2)
        vv0 = carve(128).bitcast(F16).rearrange("p (b h d) -> p b h d", b=2, h=2)
        e0 = carve(512).rearrange("p (g t) -> p g t", g=8)
        p0 = carve(512).bitcast(F16).rearrange("p (g h t) -> p g h t", g=8, h=2)
        pt0 = carve(512).bitcast(F16).rearrange("p (g n) -> p g n", g=8)
        ctx0 = carve(512).bitcast(F16).rearrange("p (h c n) -> p h c n", h=2, c=KC)
        rope = carve(TILES * 64).rearrange("p (t s f) -> p t s f", t=TILES, s=2)
        cond32 = carve(256).rearrange("p (k b) -> p k b", k=KC)
        cond_cut = carve(256).bitcast(F16).rearrange("p (h k b) -> p h k b", h=2, k=KC)
        silu_cut = carve(256).bitcast(F16).rearrange("p (h k b) -> p h k b", h=2, k=KC)
        taken["scratch"] = base
        u1 = carve(1024).rearrange("p (a n) -> p a n", a=2)
        g1 = carve(1024).rearrange("p (a n) -> p a n", a=2)
        q16 = carve(512).bitcast(F16).rearrange("p (g r d) -> p g r d", g=HALF, r=4)
        k16 = carve(512).bitcast(F16).rearrange("p (g r d) -> p g r d", g=HALF, r=4)
        sq1 = carve(1024)
        qf1 = sq1[:, 0:512].bitcast(F16).rearrange("p (g n) -> p g n", g=HALF)
        kf1 = sq1[:, 512:1024].bitcast(F16).rearrange("p (g n) -> p g n", g=HALF)
        e1 = carve(512).rearrange("p (g t) -> p g t", g=HALF)
        ctx32 = carve(512)
        vv1 = carve(1024).bitcast(F16).rearrange("p (b h n) -> p b h n", b=2, h=2)
        v1 = carve(512).bitcast(F16).rearrange("p (h n) -> p h n", h=2)
        p1 = carve(512).bitcast(F16).rearrange("p (g h t) -> p g h t", g=HALF, h=2)
        qk1 = carve(1024, "c")
        pt1 = carve(512, "c").bitcast(F16).rearrange("p (g n) -> p g n", g=HALF)
        ctx1 = carve(512, "c").bitcast(F16).rearrange("p (h c n) -> p h c n", h=2, c=KC)
        gamma_a = carve(512, "c")
        gamma_m = carve(512, "c")
        q_bias_t = carve(512, "c")
        b_proj_t = carve(512, "c")
        b_fc2_t = carve(512, "c")
        stage_inner = [inner[:].rearrange("p h c n -> p (h c n)")[:, 4096 * n:4096 * (n + 1)].bitcast(F32)
                       for n in range(4)]
        stage_c = [region_c[:, 4096 * n:4096 * (n + 1)].bitcast(F32) for n in range(2)]
        ada_cut = xm[:].rearrange("p t n -> p (t n)").bitcast(F16).rearrange("p (h k n) -> p h k n", h=2, k=KC)
        ada_out = act0.rearrange("p a n -> p (a n)")
        hm_words = h_mlp[:].rearrange("p h k n -> p (h k n)").bitcast(F32)
        xm_words = xm[:].rearrange("p t n -> p (t n)")
        ang, turns = hm_words[:, 0:1024], hm_words[:, 1024:2048]
        cos_t, sin_t = xm_words[:, 0:1024], xm_words[:, 1024:2048]
        freq = act0[:, 0, 0:32]
        pos_i = act0[:, 0, 64:96].bitcast(I32)
        pos_f = act0[:, 0, 96:128]
        ln_w_t = act0[:, 0, 128:136]
        b_ada_t = act0[:, 0, 136:160]
        ada_f32 = act0[:, 0, 256:512].rearrange("p (c b) -> p c b", c=KC)
        gamma_row = act0[:, 1, :]
        b_ada_bc = [hm_words[0:NSEQ, 512 * n:512 * (n + 1)] for n in range(2)]

        ps_m = [ctx.enter_context(nc.psum_tensor(f"ps_m{n}", [P, 512], F32)) for n in range(4)]
        ps_pq = ctx.enter_context(nc.psum_tensor("ps_pq", [P, 1024], F32))
        ps_c = ctx.enter_context(nc.psum_tensor("ps_c", [P, 512], F32))
        ps_d = ctx.enter_context(nc.psum_tensor("ps_d", [P, 512], F32))

        def as16(ap, g):
            return ap.bitcast(F16).rearrange("p (g n) -> p g n", g=g)

        s_const = sem("constants_ready")
        s_setup_dma = sem("setup_loads")
        s_setup = sem("setup_chain")
        s_setup_act = sem("setup_chain_act")
        s_cond = sem("cond_cut_ready")
        s_rope_st = sem("rope_stored")
        s_stage = [sem(f"weights_landed{n}") for n in range(6)]
        s_whi = sem("weights_hi_cut")
        s_wlo = sem("weights_lo_cut")
        s_ada = sem("ada_products")
        s_ada_out = sem("ada_out_ready")
        s_ada_st = sem("ada_stored")
        s_l1c = sem("layer1_constants_loaded")
        s_l1s = sem("layer1_scale_ready")

        class Layer:

            def __init__(self, n):
                def s(name):
                    return sem(f"l{n}_{name}")
                self.x_in = s("x_loaded")
                self.tables = s("gains_norm1_loaded")
                self.tables2 = s("gains_norm2_loaded")
                self.stat = s("stat_ready")
                self.var = s("var_eps_ready")
                self.rstd = s("rstd_ready")
                self.xn = s("xn_ready")
                self.nt = s("norm_transposed")
                self.h32 = s("h32_ready")
                self.h_hi = s("h_hi_ready")
                self.h_lo = s("h_lo_ready")
                self.proj = s("projected")
                self.rot = s("rotated")
                self.qk32 = s("qk32_ready")
                self.v_hi = s("v_hi_ready")
                self.v16 = s("v_cut")
                self.vv = s("v_spread")
                self.q_hi = s("q_hi_ready")
                self.k_hi = s("k_hi_ready")
                self.q_lo = s("q_lo_ready")
                self.kk = s("k_lo_ready")
                self.turned = s("qk_transposed")
                self.qf = s("q_feature_major")
                self.kf = s("k_feature_major")
                self.scores = s("scores_ready")
                self.mx = s("row_max_ready")
                self.shift = s("scores_shifted")
                self.e = s("exp_ready")
                self.sum = s("row_sum_ready")
                self.inv = s("row_inverse_ready")
                self.prob = s("probs_ready")
                self.p_hi = s("p_hi_ready")
                self.p_lo = s("p_lo_ready")
                self.p_turned = s("p_transposed")
                self.pt = s("p_key_major")
                self.mixed = s("mixed")
                self.c_hi = s("ctx_hi_ready")
                self.c_lo = s("ctx_lo_ready")
                self.o = s("out_projected")
                self.x1 = s("x_after_attention")
                self.hand = s("x_handed_over")
                self.up = s("up_done")
                self.act = s("act_done")
                self.m32 = s("inner32_ready")
                self.m_hi = s("inner_hi_ready")
                self.m_lo = s("inner_lo_ready")
                self.down = s("down_done")
                self.y = s("y_ready")
                self.y_out = s("y_stored")
                self.sq = s("qk_squared")
                if n == 0:
                    self.gated = s("act_times_gate")
                    self.rope_in = s("rope_loaded")
                else:
                    self.stat0 = s("stat_partial")
                    self.h_scaled = s("h_scaled")
                    self.projv = s("v_projected")
                    self.mx0 = s("masked_ready")
                    self.c32 = s("ctx32_ready")
                    self.o_b = s("out_biased")
                    self.o_g = s("out_gated")
                    self.u = s("u_ready")
                    self.usq = s("u_squared")
                    self.arg = s("tanh_arg_ready")
                    self.d_b = s("down_biased")
                    self.d_g = s("down_gated")
                    self.gam_a = s("gamma_attn_loaded")
                    self.gam_m = s("gamma_mlp_loaded")
                    self.normed = s("qk_normalised")
                    self.nsum = s("qk_norms_summed")
                    self.nmax = s("qk_norms_floored")
                    self.npow = s("qk_norms_inverted")
                    self.ninv = s("qk_norms_ready")

        L0, L1 = Layer(0), Layer(1)

        def first_block(it):
            return isinstance(it, int) and it == 0

        def rows(w, k, c0, n):
            return w[k * P * KC:(k + 1) * P * KC, c0:c0 + n].rearrange("(k p) n -> p k n", p=P)

        groups = [("ada", 0, rows(tw_t[0], 0, 0, D)),
                  ("w", qkv0_w[:, :, :, 0:512], rows(wqkv0_t, 0, 0, 512)),
                  ("w", qkv0_w[:, :, :, 512:640], rows(wqkv0_t, 0, 512, 128)),
                  ("w", wo0_w, rows(wo0_t, 0, 0, D)),
                  ("ada", 1, rows(tw_t[1], 0, 0, D))]
        FIRST = len(groups)
        groups += [("ada", 2 + n, rows(wada_t, 0, n * D, D)) for n in range(6)]
        for n in range(4):
            groups.append(("w", gate_w[:, :, :, 512 * n:512 * (n + 1)], rows(wg_t, 0, 512 * n, 512)))
            groups.append(("w", up_w[:, :, :, 512 * n:512 * (n + 1)], rows(wu_t, 0, 512 * n, 512)))
        groups += [("w", down_w[:, :, 4 * n:4 * (n + 1), :], rows(wd_t, n, 0, D)) for n in range(4)]
        SETUP = len(groups)
        groups += [("w", qkv1_w[:, :, :, 512 * n:512 * (n + 1)], rows(wqkv1_t, 0, 512 * n, 512)) for n in range(3)]
        groups.append(("w", proj1_w, rows(wproj_t, 0, 0, D)))
        groups += [("w", fc1_w[:, :, :, 512 * n:512 * (n + 1)], rows(wfc1_t, 0, 512 * n, 512)) for n in range(4)]
        SWAP = len(groups)
        CUT1 = SLOTS0 - (SWAP - SETUP)
        groups += [("w", fc2_w[:, :, 4 * n:4 * (n + 1), :], rows(wfc2_t, n, 0, D)) for n in range(4)]

        def place(g):
            if g < SETUP:
                n, k = g % 4, g // 4
                return s_stage[n], 16 * (k + 1), stage_inner[n], g - 4
            if g < SWAP:
                n, k = (g - SETUP) % 2, (g - SETUP) // 2
                return s_stage[4 + n], 16 * (k + 1), stage_c[n], g - 2 if g - 2 >= SETUP else -1
            n = g - SWAP
            before = sum(1 for q in range(SETUP) if q % 4 == n)
            return s_stage[n], 16 * (before + 1), stage_inner[n], -1

        def staged(g):
            n = groups[g][2].shape[2]
            return place(g)[2][:, 0:KC * n].rearrange("p (k n) -> p k n", k=KC)

        def dest(g, hl):
            if groups[g][0] == "ada":
                return ada_cut[:, hl]
            return groups[g][1][:, hl]

        def ada_before(g):
            return sum(1 for q in groups[:g] if q[0] == "ada")

        def tile(it, t):
            return it * TILES + t

        def norm_no(norms, it, kind, t):
            return it * len(norms) + norms.index((kind, t))

        block = ctx.enter_context(nc.Block())

        @block.sync
        def _(sp):
            count_registers = [sp.alloc_register("count_first"), sp.alloc_register("count_second")]

            def counts(*values):
                for n, r in zip(values, count_registers):
                    if not isinstance(n, int):
                        sp.reg_mov(r, n)
                return [n if isinstance(n, int) else r for n, r in zip(values, count_registers)]

            def by_block(ap, it, t):
                return ap.rearrange("(n t p) d -> n t p d", n=NBLK, t=TILES)[bass.ds(it, 1), t].rearrange("o p d -> (o p) d")

            def load_group(g):
                s, _, words, reuse = place(g)
                if reuse >= 0:
                    sp.wait_ge(s_wlo, reuse + 1)
                sp.dma_start(staged(g), groups[g][2]).then_inc(s, 16)

            def load_x(L, src, it, t):
                sp.dma_start(xa[:, t, :], by_block(src, it, t)).then_inc(L.x_in, 16)

            def spread(L, v, vv, it, t):
                cut_done, mixed = counts(tile(it, t) + 1, tile(it, t) if L is L0 else 2 * tile(it, t))
                sp.wait_ge(L.v16, cut_done)
                sp.wait_ge(L.mixed, mixed)
                for b in range(2):
                    for half in range(2):
                        sp.dma_start(vv[SEQ * half:SEQ * (half + 1), b], v[SEQ * b:SEQ * (b + 1)]).then_inc(L.vv, 16)

            def store_y(L, dst, it, t):
                sp.wait_ge(L.y, tile(it, t) + 1)
                sp.dma_start(by_block(dst, it, t), xm[:, t, :]).then_inc(L.y_out, 16)

            def hand_over(L, norms, it, t):
                if first_block(it):
                    sp.wait_ge(L.x1, tile(it, t) + 1)
                else:
                    attended, left = counts(tile(it, t) + 1, 16 * (tile(it, t) - TILES + 1))
                    sp.wait_ge(L.x1, attended)
                    sp.wait_ge(L.y_out, left)
                sp.dma_start(xm[:, t, :], xa[:, t, :]).then_inc(L.hand, 16)

            def next_x(L, norms, src, it, t):
                handed, normed = counts(16 * (tile(it, t) + 1), norm_no(norms, it, "norm2", t) + 1)
                sp.wait_ge(L.hand, handed)
                sp.wait_ge(L.xn, normed)
                load_x(L, src, it + 1, t)

            def move_on(L, norms, src, it, t, more):
                hand_over(L, norms, it, t)
                if more:
                    next_x(L, norms, src, it, t)

            def gains_of(L, dram, it, kind):
                n = 1 if L is L0 else 2
                dst = gains.rearrange("p (j k n) -> p j k n", j=2, k=2)[:, 0:n, kind, :]
                src = dram[bass.ds(it, 1)].rearrange("o p (j k) c b -> p (o j) k (c b)", k=2)[:, :, kind, :]
                sp.dma_start(dst, src).then_inc(L.tables if kind == 0 else L.tables2, 16)

            def rope_of(it):
                sp.dma_start(rope.rearrange("p t s f -> p (t s f)"), rope_dram.rearrange("p (n t) s f -> p n t s f", n=NBLK)[:, bass.ds(it, 1)].rearrange("p o t s f -> p (o t s f)")).then_inc(L0.rope_in, 16)

            def next_tables(L, dram, norms, it):
                normed, rotated = counts(norm_no(norms, it, "norm1", TILES - 1) + 1, tile(it, TILES))
                sp.wait_ge(L.h32, normed)
                sp.wait_ge(L.rot, rotated)
                gains_of(L, dram, it + 1, 0)
                if L is L0:
                    rope_of(it + 1)

            def gamma(L, which, dst, s, it, t):
                for b in range(2):
                    row = gamma_dram[which].rearrange("(n s) d -> n s d", n=NBLK)[bass.ds(it, 1), 2 * t + b, :]
                    sp.dma_start(dst[SEQ * b:SEQ * (b + 1), :], row.to_broadcast([SEQ, D])).then_inc(s, 16)

            sp.dma_start(pos_i, pos).then_inc(s_setup_dma, 16)
            sp.dma_start(ln_w_t, ln_w).then_inc(s_setup_dma, 16)
            sp.dma_start(b_ada_t, b_ada).then_inc(s_setup_dma, 16)
            sp.dma_start(cond32, cond_t).then_inc(s_setup_dma, 16)
            for g in range(2):
                load_group(g)
            for t in range(TILES):
                load_x(L0, x, 0, t)
            for g in range(2, FIRST - 1):
                load_group(g)
            sp.wait_ge(s_setup, 13)
            sp.dma_start(rope_dram[:, :, 0, :], cos_t.rearrange("p (t f) -> p t f", f=32)).then_inc(s_rope_st, 16)
            sp.dma_start(rope_dram[:, :, 1, :], sin_t.rearrange("p (t f) -> p t f", f=32)).then_inc(s_rope_st, 16)
            sp.wait_ge(s_rope_st, 32)
            load_group(FIRST - 1)
            for n in range(2):
                sp.dma_start(b_ada_bc[n], b_ada_row[n:n + 1, :].to_broadcast([NSEQ, D])).then_inc(s_setup_dma, 16)

            def store_ada(n):
                sp.wait_ge(s_ada_out, n + 1)
                if n < 2:
                    for blk in range(NBLK):
                        sp.dma_start(gain0_dram[blk, :, n], ada_f32[:, :, 8 * blk:8 * (blk + 1)]).then_inc(s_ada_st, 16)
                elif n < 4:
                    for c in range(NBLK):
                        sp.dma_start(gamma_dram[n - 2, 8 * c:8 * (c + 1), :], gamma_row[8 * c:8 * (c + 1), :]).then_inc(s_ada_st, 16)
                else:
                    for blk in range(NBLK):
                        sp.dma_start(mod1_dram[blk, :, n - 4], ada_f32[:, :, 8 * blk:8 * (blk + 1)]).then_inc(s_ada_st, 16)

            load_group(FIRST)
            store_ada(0)
            load_group(FIRST + 1)
            store_ada(1)
            sp.wait_ge(s_ada_st, 16 * NBLK * 2)
            gains_of(L0, gain0_dram, 0, 0)
            gains_of(L0, gain0_dram, 0, 1)
            rope_of(0)
            for s in range(SLOTS0):
                g = FIRST + s
                if g + 2 < SETUP:
                    load_group(g + 2)
                if g < SETUP and groups[g][0] == "ada":
                    store_ada(groups[g][1])
                for stage, t in TABLE0[s]:
                    if stage == "turn":
                        spread(L0, v0, vv0, 0, t)
                        if t == TILES - 1:
                            next_tables(L0, gain0_dram, NORMS0, 0)
            for t in range(TILES):
                hand_over(L0, NORMS0, 0, t)
                next_x(L0, NORMS0, x, 0, t)

            def slots0(it, more):
                sp.wait_ge(L0.h32, (it + 1) * len(NORMS0))
                gains_of(L0, gain0_dram, it + 1, 1)
                for s in range(SLOTS0):
                    for stage, t in TABLE0[s]:
                        if stage == "turn":
                            spread(L0, v0, vv0, it + 1, t)
                            if t == TILES - 1 and more:
                                next_tables(L0, gain0_dram, NORMS0, it + 1)
                    for t in DOWNS0[s]:
                        store_y(L0, x_mid, it, t)
                        move_on(L0, NORMS0, x, it + 1, t, more)

            with sp.Fori(0, NBLK - 2) as i:
                slots0(i, True)
            slots0(NBLK - 2, False)
            def load_const1():
                for dst, src, n in ((mask_t, mask, 2), (q_bias_t, q_bias, 1), (b_proj_t, b_proj, 1), (b_fc2_t, b_fc2, 1),
                                    (sm_scale, scale_log, 1)):
                    if n == 2:
                        for b in range(2):
                            sp.dma_start(dst[SEQ * b:SEQ * (b + 1), :], src).then_inc(s_l1c, 16)
                    else:
                        sp.dma_start(dst, src.to_broadcast([P, src.shape[1]])).then_inc(s_l1c, 16)
                sp.dma_start(v_bias_t, v_bias).then_inc(s_l1c, 16)
                sp.dma_start(b_fc1_t, b_fc1).then_inc(s_l1c, 16)

            sp.wait_ge(L0.x1, TILES * NBLK)
            for g in range(SETUP, SETUP + 2):
                load_group(g)
            for s in range(SLOTS0):
                g = SETUP + s - CUT1 + 2
                if SETUP + 2 <= g < SWAP:
                    load_group(g)
                for t in DOWNS0[s]:
                    store_y(L0, x_mid, NBLK - 1, t)
            sp.wait_ge(s_wlo, SWAP)
            load_const1()
            sp.wait_ge(s_ada_st, 16 * NBLK * 8)
            for kind in range(2):
                gains_of(L1, mod1_dram, 0, kind)
            sp.wait_ge(L0.y_out, 16 * TILES * NBLK)
            for t in range(TILES):
                load_x(L1, x_mid, 0, t)
            sp.wait_ge(L0.down, NBLK * TILES)
            for g in range(SWAP, len(groups)):
                load_group(g)

            def attn1(stage, it, t, more):
                if stage == "mix0":
                    sp.wait_ge(L1.o_g, tile(it, t))
                    gamma(L1, 0, gamma_a, L1.gam_a, it, t)
                if stage == "scores0":
                    spread(L1, v1, vv1, it, t)
                    if t == TILES - 1 and more:
                        next_tables(L1, mod1_dram, NORMS1, it)

            for s in range(SLOTS1):
                for stage, t in TABLE1[s]:
                    attn1(stage, 0, t, True)
            for t in range(TILES):
                hand_over(L1, NORMS1, 0, t)
                next_x(L1, NORMS1, x_mid, 0, t)

            def slots1(it, both, more):
                if both:
                    sp.wait_ge(L1.h32, (it + 1) * len(NORMS1))
                    gains_of(L1, mod1_dram, it + 1, 1)
                for s in range(SLOTS1):
                    if both:
                        for stage, t in TABLE1[s]:
                            attn1(stage, it + 1, t, more)
                    for kind, t, k, _, _ in JOBS1[s]:
                        if kind == "down" and k == 0:
                            sp.wait_ge(L1.d_g, tile(it, t))
                            gamma(L1, 1, gamma_m, L1.gam_m, it, t)
                    for t in DOWNS1[s]:
                        store_y(L1, out, it, t)
                        if both:
                            move_on(L1, NORMS1, x_mid, it + 1, t, more)

            with sp.Fori(0, NBLK - 2) as i:
                slots1(i, True, True)
            slots1(NBLK - 2, True, False)
            slots1(NBLK - 1, False, False)
            sp.wait_ge(L1.y_out, 16 * TILES * NBLK)

        @block.gpsimd
        def _(pool):
            for n, m in enumerate((ident32, ident16)):
                nc.gpsimd.memset(m[:], 0.0).then_inc(s_const, 1)
                pool.wait_ge(s_const, 2 * n + 1)
                nc.gpsimd.affine_select(out=m[:], in_=m[:], compare_op=ALU.not_equal, fill=1.0, base=0,
                                        pattern=[[-1, P]], channel_multiplier=1).then_inc(s_const, 1)
            nc.gpsimd.memset(minus_half, -0.5).then_inc(s_const, 1)
            nc.gpsimd.memset(eps_t, EPS).then_inc(s_const, 1)
            nc.gpsimd.memset(eps_t0, D * EPS).then_inc(s_const, 1)
            for n in range(32):
                inv_freq = float(1.0 / 10000.0 ** (2.0 * n / HD0))
                nc.gpsimd.memset(freq[:, n:n + 1], inv_freq).then_inc(s_const, 1)

            def norm(L, norms, it, kind, t):
                n = norm_no(norms, it, kind, t)
                pool.wait_ge(L.stat, n + 1)
                value = stats[:, 0:1] if L is L0 else moments[:, 1:2]
                nc.gpsimd.tensor_tensor(var_eps, value, eps_t[:, 0:1] if L is L1 else eps_t0, ALU.add).then_inc(L.var, 1)
                pool.wait_ge(L.var, n + 1)
                nc.gpsimd.tensor_tensor(rstd, var_eps, minus_half[:, 0:1], ALU.pow).then_inc(L.rstd, 1)

            def norm_lo(L, norms, it, kind, t):
                n = norm_no(norms, it, kind, t)
                pool.wait_ge(L.h_hi, n + 1)
                dst = h_attn[:, t % 2, 1] if kind == "norm1" else h_mlp[:, 1, :, t * P:(t + 1) * P]
                hi = h_attn[:, t % 2, 0] if kind == "norm1" else h_mlp[:, 0, :, t * P:(t + 1) * P]
                nc.gpsimd.tensor_tensor(dst, xn.rearrange("p (c n) -> p c n", c=KC), hi, ALU.subtract).then_inc(L.h_lo, 1)

            def attn0(stage, it, t):
                n = tile(it, t)
                if stage in ("stat1", "stat2"):
                    norm(L0, NORMS0, it, "norm" + stage[4], t)
                if stage in ("norm1", "norm2"):
                    norm_lo(L0, NORMS0, it, stage, t)
                if stage == "proj":
                    pool.wait_ge(L0.q_hi, n + 1)
                    nc.gpsimd.tensor_tensor(qk0[:, :, 1, :], rot[:, 0:512].rearrange("p (g d) -> p g d", g=HEADS0),
                                            qk0[:, :, 0, :], ALU.subtract).then_inc(L0.q_lo, 1)
                    pool.wait_ge(L0.k_hi, n + 1)
                    nc.gpsimd.tensor_tensor(kk0[:, 1], rot[:, 512:576].unsqueeze(1).to_broadcast([P, 2, HD0]), kk0[:, 0],
                                            ALU.subtract).then_inc(L0.kk, 1)
                if stage == "softmax":
                    pool.wait_ge(L0.p_hi, n + 1)
                    nc.gpsimd.tensor_tensor(p0[:, :, 1, :], e0, p0[:, :, 0, :], ALU.subtract).then_inc(L0.p_lo, 1)

            def mlp_lo(L, src, it, j):
                pool.wait_ge(L.m_hi, it * IC + j + 1)
                nc.gpsimd.tensor_tensor(inner[:, 1, j, :], src[:, j % 2, :], inner[:, 0, j, :],
                                        ALU.subtract).then_inc(L.m_lo, 1)

            pool.wait_ge(s_const, 39)
            for s in range(SLOTS0):
                for stage, t in TABLE0[s]:
                    attn0(stage, 0, t)

            def slots0(it, both):
                for s in range(SLOTS0):
                    if both:
                        for stage, t in TABLE0[s]:
                            attn0(stage, it + 1, t)
                    for j in UPS0[s]:
                        mlp_lo(L0, act0, it, j)

            with pool.Fori(0, NBLK - 1) as i:
                slots0(i, True)
            slots0(NBLK - 1, False)

            def attn1(stage, it, t):
                n = tile(it, t)
                if stage in ("stat1", "stat2"):
                    norm(L1, NORMS1, it, "norm" + stage[4], t)
                if stage in ("norm1", "norm2"):
                    norm_lo(L1, NORMS1, it, stage, t)
                if stage == "projv":
                    pool.wait_ge(L1.nmax, n + 1)
                    nc.gpsimd.tensor_tensor(norm_inv, norm_sq, minus_half, ALU.pow).then_inc(L1.npow, 1)
                    pool.wait_ge(L1.npow, n + 1)
                    pool.wait_ge(s_l1s, 3)
                    nc.gpsimd.tensor_tensor(norm_inv[:, 0:HEADS1], norm_inv[:, 0:HEADS1], sm_scale,
                                            ALU.mult).then_inc(L1.ninv, 1)
                for h in range(2):
                    if stage == ("prep0", "turn0")[h]:
                        for which, dst, hi_done, lo_done, a, b in ((0, q16, L1.q_hi, L1.q_lo, 0, 1), (1, k16, L1.k_hi, L1.kk, 0, 2)):
                            src = qk1[:, 512 * which + 256 * h:512 * which + 256 * (h + 1)].rearrange("p (g d) -> p g d", g=HALF)
                            pool.wait_ge(hi_done, 4 * n + 2 * h + 2)
                            for r in range(2):
                                lo = dst[:, :, (1 + 2 * r) if which == 0 else (2 + r), :]
                                nc.gpsimd.tensor_tensor(lo, src, dst[:, :, 0, :], ALU.subtract).then_inc(lo_done, 1)
                    if stage == ("turn1", "mix0")[h]:
                        pool.wait_ge(L1.p_hi, 2 * n + h + 1)
                        nc.gpsimd.tensor_tensor(p1[:, :, 1, :], e1, p1[:, :, 0, :], ALU.subtract).then_inc(L1.p_lo, 1)
                if stage == "out":
                    pool.wait_ge(L1.o_g, n + 1)
                    nc.gpsimd.tensor_tensor(xa[:, t, :], xa[:, t, :], ctx32, ALU.add).then_inc(L1.x1, 1)

            for s in range(SLOTS1):
                for stage, t in TABLE1[s]:
                    attn1(stage, 0, t)

            def slots1(it, both):
                for s in range(SLOTS1):
                    for j in UPS1[s][:-1]:
                        mlp_lo(L1, u1, it, j)
                    if both:
                        for stage, t in TABLE1[s]:
                            attn1(stage, it + 1, t)
                    for j in UPS1[s][-1:]:
                        mlp_lo(L1, u1, it, j)

            with pool.Fori(0, NBLK - 1) as i:
                slots1(i, True)
            slots1(NBLK - 1, False)

        @block.scalar
        def _(act):
            act.wait_ge(s_setup_dma, 64)
            act.wait_ge(s_setup, 7)
            nc.scalar.activation(sin_t, ang, ACT.Sin).then_inc(s_setup_act, 1)
            act.wait_ge(s_setup, 11)
            nc.scalar.activation(cos_t, turns, ACT.Sin).then_inc(s_setup_act, 1)
            nc.scalar.copy(cond_cut[:, 0], cond32).then_inc(s_setup_act, 1)
            nc.scalar.activation(xn[:, 0:256].rearrange("p (k b) -> p k b", k=KC), cond32, ACT.Tanh, scale=0.5).then_inc(s_setup_act, 1)

            def cut_hi(g):
                s, n, _, _ = place(g)
                act.wait_ge(s, n)
                if groups[g][0] == "ada":
                    act.wait_ge(s_rope_st, 32)
                    act.wait_ge(s_ada, ada_before(g))
                if SETUP <= g < SWAP:
                    act.wait_ge(L0.up, NBLK * IC)
                if g >= SWAP:
                    act.wait_ge(L0.down, NBLK * TILES)
                nc.scalar.mul(dest(g, 0), staged(g), WS).then_inc(s_whi, 1)

            for g in range(FIRST):
                cut_hi(g)

            def norm_square(it, kind, t):
                n = norm_no(NORMS0, it, kind, t)
                act.wait_ge(L0.h_lo, n)
                if kind == "norm1":
                    act.wait_ge(L0.x_in, 16 * (tile(it, t) + 1))
                else:
                    act.wait_ge(L0.x1, tile(it, t) + 1)
                nc.scalar.activation(xn, xa[:, t, :], ACT.Square, accum_out=stats[:, 0:1]).then_inc(L0.stat, 1)

            def norm_hi(L, norms, it, kind, t):
                n = norm_no(norms, it, kind, t)
                act.wait_ge(L.h32, n + 1)
                if kind == "norm1":
                    if t > 0 or not first_block(it):
                        act.wait_ge(L.proj if L is L0 else L.projv, tile(it, t) - 1)
                    dst = h_attn[:, t % 2, 0]
                else:
                    act.wait_ge(L.up, it * IC)
                    dst = h_mlp[:, 0, :, t * P:(t + 1) * P]
                nc.scalar.copy(dst, xn.rearrange("p (c n) -> p c n", c=KC)).then_inc(L.h_hi, 1)

            def attn0(stage, it, t):
                n = tile(it, t)
                if stage in ("stat1", "stat2"):
                    norm_square(it, "norm" + stage[4], t)
                if stage in ("norm1", "norm2"):
                    norm_hi(L0, NORMS0, it, stage, t)
                if stage == "proj":
                    act.wait_ge(L0.rot, n + 1)
                    act.wait_ge(L0.turned, n)
                    nc.scalar.copy(qk0[:, :, 0, :], rot[:, 0:512].rearrange("p (g d) -> p g d", g=HEADS0)).then_inc(L0.q_hi, 1)
                    nc.scalar.copy(kk0[:, 0], rot[:, 512:576].unsqueeze(1).to_broadcast([P, 2, HD0])).then_inc(L0.k_hi, 1)
                if stage == "turn":
                    act.wait_ge(L0.turned, n + 1)
                    act.wait_ge(L0.scores, n)
                    nc.scalar.copy(kf0, as16(ps_pq[:, 0:128], 2)).then_inc(L0.kf, 1)
                if stage == "scores":
                    act.wait_ge(L0.shift, n + 1)
                    nc.scalar.activation(e0, e0, ACT.Exp, scale=float(HD0) ** -0.5).then_inc(L0.e, 1)
                if stage == "softmax":
                    act.wait_ge(L0.prob, n + 1)
                    act.wait_ge(L0.p_turned, n)
                    nc.scalar.copy(p0[:, :, 0, :], e0).then_inc(L0.p_hi, 1)
                if stage == "turn_p":
                    act.wait_ge(L0.p_turned, n + 1)
                    act.wait_ge(L0.mixed, n)
                    nc.scalar.copy(pt0, as16(ps_d[:], 8)).then_inc(L0.pt, 1)
                if stage == "mix":
                    act.wait_ge(L0.mixed, n + 1)
                    act.wait_ge(L0.o, n)
                    nc.scalar.copy(ctx0[:, 0], ps_d[:].rearrange("p (c n) -> p c n", c=KC)).then_inc(L0.c_hi, 1)

            for s in range(SLOTS0):
                if FIRST + s < SETUP:
                    cut_hi(FIRST + s)
                for stage, t in TABLE0[s]:
                    attn0(stage, 0, t)

            def mlp_hi(L, src, it, j):
                act.wait_ge(L.m32, it * IC + j + 1)
                act.wait_ge(L.down, tile(it, 0))
                nc.scalar.copy(inner[:, 0, j, :], src[:, j % 2, :]).then_inc(L.m_hi, 1)

            def slots0(it, both):
                for s in range(SLOTS0):
                    for j in UPS0[s]:
                        act.wait_ge(L0.up, it * IC + j + 1)
                        act.wait_ge(L0.m_lo, it * IC + (j - 1 if j > 1 else 0))
                        nc.scalar.activation(act0[:, j % 2, :], ps_m[2 * (j % 2)][:], ACT.Tanh,
                                             scale=0.5 * INV).then_inc(L0.act, 1)
                    if both:
                        for stage, t in TABLE0[s]:
                            attn0(stage, it + 1, t)
                    for j in UPS0[s]:
                        mlp_hi(L0, act0, it, j)
                    if not both and s >= CUT1:
                        cut_hi(SETUP + s - CUT1)

            with act.Fori(0, NBLK - 1) as i:
                slots0(i, True)
            slots0(NBLK - 1, False)

            act.wait_ge(s_l1s, 1)
            nc.scalar.activation(sm_scale, sm_scale, ACT.Exp).then_inc(s_l1s, 2)

            def attn1(stage, it, t):
                n = tile(it, t)
                if stage in ("norm1", "norm2"):
                    norm_hi(L1, NORMS1, it, stage, t)
                if stage == "proj":
                    act.wait_ge(L1.proj, n + 1)
                    act.wait_ge(L1.k_hi, 4 * n)
                    act.wait_ge(L1.kk, 4 * n)
                    nc.scalar.mul(qk1[:, 512:1024], ps_pq[:, 512:1024], INV).then_inc(L1.rot, 1)
                    act.wait_ge(L1.qk32, n + 1)
                    act.wait_ge(L1.rot, n + 1)
                    act.wait_ge(L1.scores, 2 * n)
                    nc.scalar.activation(sq1, qk1, ACT.Square).then_inc(L1.sq, 1)
                if stage == "projv":
                    act.wait_ge(L1.projv, n + 1)
                    act.wait_ge(L1.vv, 64 * n)
                    nc.scalar.mul(v1[:, 0], ps_m[2][:], INV).then_inc(L1.v_hi, 1)
                for h in range(2):
                    if stage == ("prep0", "turn0")[h]:
                        act.wait_ge(L1.normed, n + 1)
                        act.wait_ge(L1.turned, 2 * n + h)
                        for r in range(2):
                            nc.scalar.copy(q16[:, :, 2 * r, :], qk1[:, 256 * h:256 * (h + 1)].rearrange("p (g d) -> p g d", g=HALF)).then_inc(L1.q_hi, 1)
                        for r in range(2):
                            nc.scalar.copy(k16[:, :, r, :], qk1[:, 512 + 256 * h:512 + 256 * (h + 1)].rearrange("p (g d) -> p g d", g=HALF)).then_inc(L1.k_hi, 1)
                    if stage == ("turn0", "turn1")[h]:
                        act.wait_ge(L1.turned, 2 * n + h + 1)
                        act.wait_ge(L1.scores, 2 * n + h)
                        nc.scalar.copy(kf1, as16(ps_pq[:, 0:512], HALF)).then_inc(L1.kf, 1)
                    if stage == ("scores0", "scores1_turn_p0")[h]:
                        act.wait_ge(L1.shift, 2 * n + h + 1)
                        nc.scalar.activation(e1, e1, ACT.Exp).then_inc(L1.e, 1)
                    if stage == ("turn1", "mix0")[h]:
                        act.wait_ge(L1.prob, 2 * n + h + 1)
                        act.wait_ge(L1.p_turned, 2 * n + h)
                        nc.scalar.copy(p1[:, :, 0, :], e1).then_inc(L1.p_hi, 1)
                    if stage == ("scores1_turn_p0", "turn_p1")[h]:
                        act.wait_ge(L1.p_turned, 2 * n + h + 1)
                        act.wait_ge(L1.mixed, 2 * n + h)
                        bank = ps_d[:] if h == 0 else ps_m[3][:]
                        nc.scalar.copy(pt1, as16(bank, HALF)).then_inc(L1.pt, 1)
                if stage == "mix1":
                    act.wait_ge(L1.c32, n + 1)
                    act.wait_ge(L1.o, n)
                    nc.scalar.copy(ctx1[:, 0], ctx32.rearrange("p (c n) -> p c n", c=KC)).then_inc(L1.c_hi, 1)

            for s in range(SLOTS1):
                if SWAP + s < len(groups):
                    cut_hi(SWAP + s)
                for stage, t in TABLE1[s]:
                    attn1(stage, 0, t)

            def mlp_tanh(it, j):
                act.wait_ge(L1.arg, it * IC + j + 1)
                nc.scalar.activation(g1[:, j % 2, :], g1[:, j % 2, :], ACT.Tanh).then_inc(L1.act, 1)

            def slots1(it, both):
                for s in range(SLOTS1):
                    for j in UPS1[s]:
                        act.wait_ge(L1.up, it * IC + j + 1)
                        act.wait_ge(L1.m_lo, it * IC + (j - 1 if j > 1 else 0))
                        if j == 0:
                            act.wait_ge(L1.y, tile(it, 0))
                        nc.scalar.activation(u1[:, j % 2, :], ps_m[j % 2][:], ACT.Identity, bias=b_fc1_t[:, j:j + 1],
                                             scale=INV).then_inc(L1.u, 1)
                        act.wait_ge(L1.u, it * IC + j + 1)
                        nc.scalar.activation(g1[:, j % 2, :], u1[:, j % 2, :], ACT.Square,
                                             scale=(0.044715 * GELU_C) ** 0.5).then_inc(L1.usq, 1)
                        if j != UPS1[s][-1]:
                            mlp_tanh(it, j)
                            mlp_hi(L1, u1, it, j)
                    if both:
                        for stage, t in TABLE1[s]:
                            attn1(stage, it + 1, t)
                    for j in UPS1[s][-1:]:
                        mlp_tanh(it, j)
                        mlp_hi(L1, u1, it, j)

            with act.Fori(0, NBLK - 1) as i:
                slots1(i, True)
            slots1(NBLK - 1, False)

        @block.vector
        def _(dve):
            steps = [0]

            def link(ins):
                steps[0] += 1
                ins.then_inc(s_setup, 1)
                dve.wait_ge(s_setup, steps[0])

            dve.wait_ge(s_setup_dma, 64)
            dve.wait_ge(s_const, 39)
            a3, t3 = ang.rearrange("p (t f) -> p t f", f=32), turns.rearrange("p (t f) -> p t f", f=32)
            link(nc.vector.tensor_copy(pos_f, pos_i))
            link(nc.vector.tensor_tensor(a3, pos_f.unsqueeze(2).to_broadcast([P, 32, 32]),
                                         freq.unsqueeze(1).to_broadcast([P, 32, 32]), ALU.mult))
            link(nc.vector.tensor_scalar(turns, ang, 1.0 / TWO_PI, ROUND, ALU.mult, ALU.add))
            link(nc.vector.tensor_scalar(turns, turns, ROUND, None, ALU.subtract))
            link(nc.vector.scalar_tensor_tensor(ang, turns, -PI_HIGH, ang, ALU.mult, ALU.add))
            link(nc.vector.scalar_tensor_tensor(ang, turns, -PI_LOW, ang, ALU.mult, ALU.add))
            link(nc.vector.tensor_scalar(ang, ang, PI_IN, -PI_IN, ALU.min, ALU.max))
            link(nc.vector.tensor_scalar(turns, ang, TWO_PI / 4, PI_IN, ALU.add, ALU.is_gt))
            link(nc.vector.scalar_tensor_tensor(turns, turns, -TWO_PI, ang, ALU.mult, ALU.add))
            link(nc.vector.tensor_scalar(turns, turns, TWO_PI / 4, PI_IN, ALU.add, ALU.min))
            link(nc.vector.tensor_scalar(turns, turns, -PI_IN, None, ALU.max))
            dve.wait_ge(s_setup_act, 2)
            link(nc.vector.tensor_scalar(sin_t, sin_t, INV, None, ALU.mult))
            link(nc.vector.tensor_scalar(cos_t, cos_t, INV, None, ALU.mult))
            dve.wait_ge(s_setup_act, 4)
            half_silu = xn[:, 0:256].rearrange("p (k b) -> p k b", k=KC)
            link(nc.vector.tensor_tensor(cond_cut[:, 1], cond32, cond_cut[:, 0], ALU.subtract))
            link(nc.vector.scalar_tensor_tensor(half_silu, half_silu, 1.0, cond32, ALU.add, ALU.mult))
            link(nc.vector.tensor_scalar(half_silu, half_silu, 0.5, None, ALU.mult))
            link(nc.vector.tensor_copy(silu_cut[:, 0], half_silu))
            nc.vector.tensor_tensor(silu_cut[:, 1], half_silu, silu_cut[:, 0], ALU.subtract).then_inc(s_cond, 1)

            def cut_lo(g):
                dve.wait_ge(s_whi, g + 1)
                nc.vector.scalar_tensor_tensor(dest(g, 1), staged(g), WS, dest(g, 0), ALU.mult,
                                               ALU.subtract).then_inc(s_wlo, 1)
                if groups[g][0] == "ada":
                    ada(groups[g][1])

            def ada(n):
                dve.wait_ge(s_ada, n + 1)
                dve.wait_ge(s_ada_st, 16 * NBLK * n)
                bank = ps_m[n % 2]
                feat = bank[:, 0:256].rearrange("p (c b) -> p c b", c=KC)
                if n < 2:
                    link(nc.vector.tensor_scalar(ada_f32, feat, INV, 1.0, ALU.mult, ALU.add))
                    w = ln_w_t[:, 4 * n:4 * (n + 1)].unsqueeze(2).to_broadcast([P, KC, NSEQ])
                    nc.vector.tensor_tensor(ada_f32, ada_f32, w, ALU.mult).then_inc(s_ada_out, 1)
                elif n < 4:
                    dve.wait_ge(s_setup_dma, 64 + 32)
                    nc.vector.scalar_tensor_tensor(gamma_row[0:NSEQ, :], bank[0:NSEQ, :], INV, b_ada_bc[n - 2], ALU.mult,
                                                   ALU.add).then_inc(s_ada_out, 1)
                else:
                    b = b_ada_t[:, 4 * (n - 2):4 * (n - 1)].unsqueeze(2).to_broadcast([P, KC, NSEQ])
                    ins = nc.vector.scalar_tensor_tensor(ada_f32, feat, INV, b, ALU.mult, ALU.add)
                    if n < 6:
                        link(ins)
                        ins = nc.vector.tensor_scalar(ada_f32, ada_f32, 1.0, None, ALU.add)
                    ins.then_inc(s_ada_out, 1)

            for g in range(FIRST):
                cut_lo(g)

            def gain(kind, t, shift=0):
                k = 0 if kind == "norm1" else 1
                g = gains.rearrange("p (k c b) -> p k c b", k=4, c=KC) if shift is not None else None
                return g[:, k + shift, :, 2 * t:2 * t + 2].unsqueeze(3).to_broadcast([P, KC, 2, SEQ])

            def by_seq(ap):
                return ap.rearrange("p (c b n) -> p c b n", c=KC, b=2)

            def stat0(it, kind, t):
                n = norm_no(NORMS0, it, kind, t)
                dve.wait_ge(L0.rstd, n + 1)
                nc.vector.tensor_scalar(xn, xa[:, t, :], rstd, float(D) ** 0.5, ALU.mult, ALU.mult).then_inc(L0.xn, 1)

            def norm0(it, kind, t):
                n = norm_no(NORMS0, it, kind, t)
                dve.wait_ge(L0.nt, n + 1)
                dve.wait_ge(L0.tables if kind == "norm1" else L0.tables2, 16 * (it + 1))
                nc.vector.tensor_tensor(by_seq(xn), by_seq(ps_c[:]), gain(kind, t), ALU.mult).then_inc(L0.h32, 1)

            def attn0(stage, it, t):
                n = tile(it, t)
                if stage in ("stat1", "stat2"):
                    stat0(it, "norm" + stage[4], t)
                if stage in ("norm1", "norm2"):
                    norm0(it, stage, t)
                if stage == "proj":
                    dve.wait_ge(L0.proj, n + 1)
                    dve.wait_ge(L0.kk, n)
                    dve.wait_ge(L0.rope_in, 16 * (it + 1))
                    dve.wait_ge(L0.vv, 64 * n)
                    nc.vector.tensor_scalar(v0[:, 0], ps_pq[:, 576:640], INV, None, ALU.mult).then_inc(L0.v_hi, 1)
                    q = ps_pq[:, 0:576].rearrange("p (g s f) -> p g s f", g=9, s=2)
                    r1 = rot.rearrange("p (g s f) -> p g s f", g=9, s=2)
                    r2 = rot2.rearrange("p (g s f) -> p g s f", g=9, s=2)
                    cos = rope[:, t, 0, :].unsqueeze(1).unsqueeze(1).to_broadcast([P, 9, 2, 32])
                    sin = rope[:, t, 1, :].unsqueeze(1).to_broadcast([P, 9, 32])
                    nc.vector.tensor_tensor(r1, q, cos, ALU.mult).then_inc(L0.qk32, 1)
                    nc.vector.tensor_tensor(r2[:, :, 0, :], q[:, :, 1, :], sin, ALU.mult).then_inc(L0.qk32, 1)
                    nc.vector.tensor_tensor(r2[:, :, 1, :], q[:, :, 0, :], sin, ALU.mult).then_inc(L0.qk32, 1)
                    dve.wait_ge(L0.v_hi, n + 1)
                    nc.vector.scalar_tensor_tensor(v0[:, 1], ps_pq[:, 576:640], INV, v0[:, 0], ALU.mult,
                                                   ALU.subtract).then_inc(L0.v16, 1)
                    dve.wait_ge(L0.qk32, 3 * n + 3)
                    nc.vector.tensor_tensor(r1[:, :, 0, :], r1[:, :, 0, :], r2[:, :, 0, :], ALU.subtract).then_inc(L0.sq, 1)
                    nc.vector.tensor_tensor(r1[:, :, 1, :], r1[:, :, 1, :], r2[:, :, 1, :], ALU.add).then_inc(L0.rot, 1)
                if stage == "turn":
                    dve.wait_ge(L0.turned, n + 1)
                    dve.wait_ge(L0.scores, n)
                    nc.vector.tensor_copy(qf0.rearrange("p b g q -> p g b q"),
                                          as16(ps_c[:], 8).rearrange("p g (b q) -> p g b q", b=2)).then_inc(L0.qf, 1)
                if stage == "scores":
                    exponents(L0, e0, ps_d[:], n)
                if stage == "softmax":
                    probabilities(L0, e0, n)
                if stage == "mix":
                    dve.wait_ge(L0.c_hi, n + 1)
                    nc.vector.tensor_tensor(ctx0[:, 1], ps_d[:].rearrange("p (c n) -> p c n", c=KC), ctx0[:, 0],
                                            ALU.subtract).then_inc(L0.c_lo, 1)
                if stage == "out":
                    dve.wait_ge(L0.o, n + 1)
                    nc.vector.scalar_tensor_tensor(xa[:, t, :], ps_pq[:, 0:512], INV, xa[:, t, :], ALU.mult,
                                                   ALU.add).then_inc(L0.x1, 1)

            def exponents(L, e, bank, m):
                s3 = bank.rearrange("p (g t) -> p g t", g=8)
                dve.wait_ge(L.scores, m + 1)
                dve.wait_ge(L.p_lo, m)
                if L is L1:
                    dve.wait_ge(L.sum, m)
                    nc.vector.tensor_tensor(e, s3, mask_t.unsqueeze(1).to_broadcast([P, 8, SEQ]), ALU.add).then_inc(L.mx0, 1)
                    dve.wait_ge(L.mx0, m + 1)
                    s3 = e
                nc.vector.tensor_reduce(row_max, s3, AX_X, ALU.max).then_inc(L.mx, 1)
                dve.wait_ge(L.mx, m + 1)
                nc.vector.tensor_tensor(e, s3, row_max.unsqueeze(2).to_broadcast([P, 8, SEQ]), ALU.subtract).then_inc(L.shift, 1)

            def probabilities(L, e, m):
                dve.wait_ge(L.e, m + 1)
                nc.vector.tensor_reduce(row_sum, e, AX_X, ALU.add).then_inc(L.sum, 1)
                dve.wait_ge(L.sum, m + 1)
                nc.vector.reciprocal(row_inv, row_sum).then_inc(L.inv, 1)
                dve.wait_ge(L.inv, m + 1)
                nc.vector.tensor_tensor(e, e, row_inv.unsqueeze(2).to_broadcast([P, 8, SEQ]), ALU.mult).then_inc(L.prob, 1)

            for s in range(SLOTS0):
                if FIRST + s < SETUP:
                    cut_lo(FIRST + s)
                for stage, t in TABLE0[s]:
                    attn0(stage, 0, t)

            def slots0(it, both):
                for s in range(SLOTS0):
                    for j in UPS0[s]:
                        dve.wait_ge(L0.act, it * IC + j + 1)
                        a = act0[:, j % 2, :]
                        nc.vector.scalar_tensor_tensor(a, a, 1.0, ps_m[2 * (j % 2)][:], ALU.add, ALU.mult).then_inc(L0.gated, 1)
                        dve.wait_ge(L0.gated, it * IC + j + 1)
                        nc.vector.scalar_tensor_tensor(a, a, 0.5 * INV * INV, ps_m[2 * (j % 2) + 1][:], ALU.mult,
                                                       ALU.mult).then_inc(L0.m32, 1)
                    if both:
                        for stage, t in TABLE0[s]:
                            attn0(stage, it + 1, t)
                    for t in DOWNS0[s]:
                        dve.wait_ge(L0.down, tile(it, t) + 1)
                        dve.wait_ge(L0.hand, 16 * (tile(it, t) + 1))
                        nc.vector.scalar_tensor_tensor(xm[:, t, :], ps_m[t % 2][:], INV, xm[:, t, :], ALU.mult,
                                                       ALU.add).then_inc(L0.y, 1)
                    if not both and s >= CUT1:
                        cut_lo(SETUP + s - CUT1)

            with dve.Fori(0, NBLK - 1) as i:
                slots0(i, True)
            slots0(NBLK - 1, False)

            dve.wait_ge(s_l1c, 16 * 8)
            nc.vector.tensor_scalar(sm_scale, sm_scale, 4.605170185988092, None, ALU.min).then_inc(s_l1s, 1)

            def stat1(it, kind, t):
                n = norm_no(NORMS1, it, kind, t)
                if kind == "norm1":
                    dve.wait_ge(L1.x_in, 16 * (tile(it, t) + 1))
                else:
                    dve.wait_ge(L1.x1, tile(it, t) + 1)
                nc.vector.bn_stats(stats[:, 0:6], xa[:, t, :]).then_inc(L1.stat0, 1)
                dve.wait_ge(L1.stat0, n + 1)
                nc.vector.memset(spare, 0.0)
                nc.vector.bn_aggr(moments, stats[:, 0:6]).then_inc(L1.stat, 1)
                dve.wait_ge(L1.rstd, n + 1)
                dve.wait_ge(L1.h_lo, n)
                dve.wait_ge(L1.stat, n + 1)
                nc.vector.tensor_scalar(xn, xa[:, t, :], moments[:, 0:1], rstd, ALU.subtract, ALU.mult).then_inc(L1.xn, 1)

            def norm1(it, kind, t):
                n = norm_no(NORMS1, it, kind, t)
                dve.wait_ge(L1.nt, n + 1)
                dve.wait_ge(L1.tables if kind == "norm1" else L1.tables2, 16 * (it + 1))
                nc.vector.tensor_tensor(by_seq(xn), by_seq(ps_pq[:, 512:1024]), gain(kind, t), ALU.mult).then_inc(L1.h_scaled, 1)
                dve.wait_ge(L1.h_scaled, n + 1)
                nc.vector.tensor_tensor(by_seq(xn), by_seq(xn), gain(kind, t, 2), ALU.add).then_inc(L1.h32, 1)

            def attn1(stage, it, t):
                n = tile(it, t)
                if stage in ("stat1", "stat2"):
                    stat1(it, "norm" + stage[4], t)
                if stage in ("norm1", "norm2"):
                    norm1(it, stage, t)
                if stage == "proj":
                    dve.wait_ge(L1.proj, n + 1)
                    dve.wait_ge(L1.q_lo, 4 * n)
                    dve.wait_ge(L1.kk, 4 * n)
                    nc.vector.scalar_tensor_tensor(qk1[:, 0:512], ps_pq[:, 0:512], INV, q_bias_t, ALU.mult,
                                                   ALU.add).then_inc(L1.qk32, 1)
                if stage == "projv":
                    dve.wait_ge(L1.sq, n + 1)
                    nc.vector.tensor_reduce(norm_sq, sq1.rearrange("p (g d) -> p g d", g=32), AX_X, ALU.add).then_inc(L1.nsum, 1)
                    dve.wait_ge(L1.nsum, n + 1)
                    nc.vector.tensor_scalar(norm_sq, norm_sq, 1e-24, None, ALU.max).then_inc(L1.nmax, 1)
                    dve.wait_ge(L1.ninv, n + 1)
                    qk = qk1.rearrange("p (g d) -> p g d", g=32)
                    nc.vector.tensor_tensor(qk, qk, norm_inv.unsqueeze(2).to_broadcast([P, 32, HD1]), ALU.mult).then_inc(L1.normed, 1)
                    dve.wait_ge(L1.v_hi, n + 1)
                    nc.vector.scalar_tensor_tensor(v1[:, 1], ps_m[2][:], INV, v1[:, 0], ALU.mult,
                                                   ALU.subtract).then_inc(L1.v16, 1)
                for h in range(2):
                    if stage == ("turn0", "turn1")[h]:
                        dve.wait_ge(L1.turned, 2 * n + h + 1)
                        dve.wait_ge(L1.scores, 2 * n + h)
                        nc.vector.tensor_copy(qf1, as16(ps_c[:], HALF)).then_inc(L1.qf, 1)
                    if stage == ("scores0", "scores1_turn_p0")[h]:
                        exponents(L1, e1, ps_d[:] if h == 0 else ps_m[3][:], 2 * n + h)
                    if stage == ("turn1", "mix0")[h]:
                        probabilities(L1, e1, 2 * n + h)
                if stage == "mix1":
                    dve.wait_ge(L1.mixed, 2 * n + 2)
                    dve.wait_ge(L1.x1, n)
                    nc.vector.tensor_tensor(ctx32.rearrange("p (c n) -> p c n", c=KC), ps_d[:].rearrange("p (c n) -> p c n", c=KC),
                                            v_bias_t.unsqueeze(2).to_broadcast([P, KC, P]), ALU.add).then_inc(L1.c32, 1)
                    dve.wait_ge(L1.c_hi, n + 1)
                    nc.vector.tensor_tensor(ctx1[:, 1], ctx32.rearrange("p (c n) -> p c n", c=KC), ctx1[:, 0],
                                            ALU.subtract).then_inc(L1.c_lo, 1)
                if stage == "out":
                    dve.wait_ge(L1.o, n + 1)
                    nc.vector.scalar_tensor_tensor(ctx32, ps_pq[:, 512:1024], INV, b_proj_t, ALU.mult, ALU.add).then_inc(L1.o_b, 1)
                    dve.wait_ge(L1.o_b, n + 1)
                    dve.wait_ge(L1.gam_a, 32 * (n + 1))
                    nc.vector.tensor_tensor(ctx32, ctx32, gamma_a, ALU.mult).then_inc(L1.o_g, 1)

            for s in range(SLOTS1):
                if SWAP + s < len(groups):
                    cut_lo(SWAP + s)
                for stage, t in TABLE1[s]:
                    attn1(stage, 0, t)

            def gelu(it, j):
                dve.wait_ge(L1.act, it * IC + j + 1)
                u = u1[:, j % 2, :]
                nc.vector.scalar_tensor_tensor(u, g1[:, j % 2, :], 1.0, u, ALU.add, ALU.mult).then_inc(L1.m32, 1)

            def slots1(it, both):
                for s in range(SLOTS1):
                    for j in UPS1[s]:
                        dve.wait_ge(L1.usq, it * IC + j + 1)
                        g = g1[:, j % 2, :]
                        nc.vector.scalar_tensor_tensor(g, g, GELU_C, u1[:, j % 2, :], ALU.add, ALU.mult).then_inc(L1.arg, 1)
                        if j != UPS1[s][-1]:
                            gelu(it, j)
                    if both:
                        for stage, t in TABLE1[s]:
                            attn1(stage, it + 1, t)
                    for j in UPS1[s][-1:]:
                        gelu(it, j)
                    for t in DOWNS1[s]:
                        m = tile(it, t)
                        dve.wait_ge(L1.down, m + 1)
                        dve.wait_ge(L1.m_lo, (it + 1) * IC)
                        dve.wait_ge(L1.y, m)
                        d = u1[:, 0, :]
                        nc.vector.scalar_tensor_tensor(d, ps_m[t % 2][:], 0.5 * INV, b_fc2_t, ALU.mult, ALU.add).then_inc(L1.d_b, 1)
                        dve.wait_ge(L1.d_b, m + 1)
                        dve.wait_ge(L1.gam_m, 32 * (m + 1))
                        nc.vector.tensor_tensor(d, d, gamma_m, ALU.mult).then_inc(L1.d_g, 1)
                        dve.wait_ge(L1.d_g, m + 1)
                        dve.wait_ge(L1.hand, 16 * (m + 1))
                        nc.vector.tensor_tensor(xm[:, t, :], xm[:, t, :], d, ALU.add).then_inc(L1.y, 1)

            with dve.Fori(0, NBLK - 1) as i:
                slots1(i, True)
            slots1(NBLK - 1, False)

        @block.tensor
        def _(pe):
            PASSES = ((0, 0), (0, 1), (1, 0))

            def products(jobs, left, chunks, first=True, last=True, late=None, ready=None):
                early = [p for p in PASSES if late is None or p[late] == 0]
                order = [(k, p) for k in chunks for p in early]
                order += [(k, p) for k in chunks for p in PASSES if p not in early]
                ins = None
                for n, (k, (a, b)) in enumerate(order):
                    if late is not None and n == len(early) * len(chunks):
                        pe.wait_ge(ready[0], ready[1])
                    for o, right in jobs:
                        ins = nc.tensor.matmul(o, left(a, k), right(b, k), start=(first and n == 0),
                                               stop=(last and n == len(order) - 1), skip_group_check=True)
                return ins

            def ada(g, n):
                pe.wait_ge(s_wlo, g + 1)
                pe.wait_ge(s_cond, 1)
                if n >= 2:
                    pe.wait_ge(s_ada_out, n - 1)
                bank = ps_m[n % 2]
                c = cond_cut if n < 2 else silu_cut
                if 2 <= n < 4:
                    ins = products([(bank[0:NSEQ, :], lambda b, k: ada_cut[:, b, k, :])],
                                   lambda a, k: c[:, a, k, :], range(KC))
                else:
                    for f in range(KC):
                        ins = products([(bank[:, NSEQ * f:NSEQ * (f + 1)], lambda b, k: c[:, b, k, :])],
                                       lambda a, k: ada_cut[:, a, k, P * f:P * (f + 1)], range(KC))
                ins.then_inc(s_ada, 1)

            def setup_group(g):
                if groups[g][0] == "ada":
                    ada(g, groups[g][1])

            for g in range(FIRST):
                setup_group(g)

            pe.wait_ge(s_const, 5)

            def norm(L, norms, it, kind, t):
                n = norm_no(norms, it, kind, t)
                pe.wait_ge(L.xn, n + 1)
                if L is L0:
                    pe.wait_ge(L.h32, n)
                    pe.wait_ge(L.qf, count_before(TABLE0, it, (kind, t), ("turn",)))
                    bank = ps_c[:]
                else:
                    pe.wait_ge(L.h_scaled, n)
                    pe.wait_ge(L.rot, count_before(TABLE1, it, (kind, t), ("proj",)))
                    pe.wait_ge(L.o_b, count_before(TABLE1, it, (kind, t), ("out",)))
                    bank = ps_pq[:, 512:1024]
                for c in range(KC):
                    ins = nc.tensor.transpose(bank[:, P * c:P * (c + 1)], xn[:, P * c:P * (c + 1)], ident32[:])
                ins.then_inc(L.nt, 1)

            def attn0(stage, it, t):
                n = tile(it, t)
                if stage in ("norm1", "norm2"):
                    norm(L0, NORMS0, it, stage, t)
                if stage == "proj":
                    pe.wait_ge(s_wlo, 3)
                    normed = norm_no(NORMS0, it, "norm1", t) + 1
                    pe.wait_ge(L0.h_hi, normed)
                    pe.wait_ge(L0.kf, n)
                    pe.wait_ge(L0.x1, count_before(TABLE0, it, (stage, t), ("out",)))
                    left = lambda a, k: h_attn[:, t % 2, a, k, :]
                    products([(ps_pq[:, 0:512], lambda b, k: qkv0_w[:, b, k, 0:512]),
                              (ps_pq[:, 512:640], lambda b, k: qkv0_w[:, b, k, 512:640])],
                             left, range(KC), late=0, ready=(L0.h_lo, normed)).then_inc(L0.proj, 1)
                if stage == "turn":
                    pe.wait_ge(L0.q_lo, n + 1)
                    pe.wait_ge(L0.kk, n + 1)
                    pe.wait_ge(L0.rot, n + 1)
                    pe.wait_ge(L0.v16, n + 1)
                    pe.wait_ge(L0.h32, count_before(TABLE0, it, (stage, t), ("norm1", "norm2")))
                    pe.wait_ge(L0.qf, n)
                    for g in range(HEADS0):
                        nc.tensor.transpose(as16(ps_c[:], 8)[:, g, :], qk0[:, g].rearrange("p h d -> p (h d)"), ident16[:])
                    for h in range(2):
                        ins = nc.tensor.transpose(as16(ps_pq[:, 0:128], 2)[:, h, :], kk0[:, h].rearrange("p r d -> p (r d)"), ident16[:])
                    ins.then_inc(L0.turned, 1)
                if stage == "scores":
                    pe.wait_ge(L0.qf, n + 1)
                    pe.wait_ge(L0.kf, n + 1)
                    pe.wait_ge(L0.c_lo, n)
                    for b in range(2):
                        for hp in range(4):
                            for h in range(2):
                                ins = nc.tensor.matmul(ps_d[:, (4 * b + hp) * SEQ:(4 * b + hp + 1) * SEQ],
                                                       qf0[:, b, 2 * hp:2 * hp + 2, :].rearrange("p g q -> p (g q)"),
                                                       kf0[:, h, SEQ * b:SEQ * (b + 1)], start=(h == 0), stop=(h == 1))
                    ins.then_inc(L0.scores, 1)
                if stage == "turn_p":
                    pe.wait_ge(L0.p_lo, n + 1)
                    pe.wait_ge(L0.shift, n + 1)
                    for g in range(8):
                        ins = nc.tensor.transpose(as16(ps_d[:], 8)[:, g, :], p0[:, g].rearrange("p h t -> p (h t)"), ident16[:])
                    ins.then_inc(L0.p_turned, 1)
                if stage == "mix":
                    pe.wait_ge(L0.pt, n + 1)
                    pe.wait_ge(L0.vv, 64 * (n + 1))
                    o = ps_d[:].rearrange("p (c b q) -> p c b q", c=KC, b=2)
                    for b in range(2):
                        for h in range(2):
                            for par in range(2):
                                ins = nc.tensor.matmul(o[SEQ * par:SEQ * (par + 1), :, b, :], vv0[:, b, h, :],
                                                       pt0[:, 4 * b:4 * b + 4, SEQ * par:SEQ * (par + 1)],
                                                       start=(h == 0), stop=(h == 1))
                    ins.then_inc(L0.mixed, 1)
                if stage == "out":
                    pe.wait_ge(s_wlo, 4)
                    pe.wait_ge(L0.c_hi, n + 1)
                    pe.wait_ge(L0.kf, count_before(TABLE0, it, (stage, t), ("turn",)))
                    products([(ps_pq[:, 0:512], lambda b, k: wo0_w[:, b, k, :])],
                             lambda a, k: ctx0[:, a, k, :], range(KC), late=0, ready=(L0.c_lo, n + 1)).then_inc(L0.o, 1)

            for s in range(SLOTS0):
                if FIRST + s < SETUP:
                    setup_group(FIRST + s)
                for stage, t in TABLE0[s]:
                    attn0(stage, 0, t)
            pe.wait_ge(s_wlo, SETUP)

            def slots0(it, both):
                for s in range(SLOTS0):
                    for kind, j, first, last, _ in JOBS0[s]:
                        if kind == "gate":
                            if j == 0:
                                pe.wait_ge(L0.h_lo, (it + 1) * len(NORMS0))
                            if j >= 2:
                                pe.wait_ge(L0.m32, it * IC + j - 1)
                            else:
                                pe.wait_ge(L0.y, tile(it, 0))
                        if kind == "down":
                            pe.wait_ge(L0.m_lo, it * IC + last)
                            if first == 0:
                                pe.wait_ge(L0.m32, (it + 1) * IC)
                                if j >= 2:
                                    pe.wait_ge(L0.y, tile(it, j) - 1)
                            ins = products([(ps_m[j % 2][:], lambda b, k: down_w[:, b, k, :])],
                                           lambda a, k: inner[:, a, k, P * j:P * (j + 1)], range(first, last),
                                           first=(first == 0), last=(last == IC))
                            if last == IC:
                                ins.then_inc(L0.down, 1)
                        else:
                            w, bank = (gate_w, ps_m[2 * (j % 2)]) if kind == "gate" else (up_w, ps_m[2 * (j % 2) + 1])
                            ins = products([(bank[:], lambda b, k: h_mlp[:, b, k, :])],
                                           lambda a, k: w[:, a, k, P * j:P * (j + 1)], range(first, last))
                            if kind == "up":
                                ins.then_inc(L0.up, 1)
                    if both:
                        for stage, t in TABLE0[s]:
                            attn0(stage, it + 1, t)

            with pe.Fori(0, NBLK - 1) as i:
                slots0(i, True)
            slots0(NBLK - 1, False)

            def attn1(stage, it, t):
                n = tile(it, t)
                if stage in ("norm1", "norm2"):
                    norm(L1, NORMS1, it, stage, t)
                if stage == "proj":
                    normed = norm_no(NORMS1, it, "norm1", t) + 1
                    pe.wait_ge(L1.h_hi, normed)
                    pe.wait_ge(L1.kf, 2 * n)
                    pe.wait_ge(L1.rot, n)
                    pe.wait_ge(L1.o_b, count_before(TABLE1, it, (stage, t), ("out",)))
                    pe.wait_ge(L1.h_scaled, count_before(TABLE1, it, (stage, t), ("norm1", "norm2")))
                    left = lambda a, k: h_attn[:, t % 2, a, k, :]
                    products([(ps_pq[:, 512 * q:512 * (q + 1)], lambda b, k, q=q: qkv1_w[:, b, k, 512 * q:512 * (q + 1)])
                              for q in range(2)], left, range(KC), late=0, ready=(L1.h_lo, normed)).then_inc(L1.proj, 1)
                if stage == "projv":
                    left = lambda a, k: h_attn[:, t % 2, a, k, :]
                    pe.wait_ge(L1.v16, n)
                    products([(ps_m[2][:], lambda b, k: qkv1_w[:, b, k, 1024:1536])], left, range(KC)).then_inc(L1.projv, 1)
                for h in range(2):
                    if stage == ("turn0", "turn1")[h]:
                        pe.wait_ge(L1.q_lo, 4 * n + 2 * h + 2)
                        pe.wait_ge(L1.kk, 4 * n + 2 * h + 2)
                        pe.wait_ge(L1.qf, 2 * n + h)
                        pe.wait_ge(L1.kf, 2 * n + h)
                        pe.wait_ge(L1.qk32, n + 1)
                        for g in range(HALF):
                            nc.tensor.transpose(as16(ps_c[:], HALF)[:, g, :], q16[:, g].rearrange("p r d -> p (r d)"), ident16[:])
                        for g in range(HALF):
                            ins = nc.tensor.transpose(as16(ps_pq[:, 0:512], HALF)[:, g, :], k16[:, g].rearrange("p r d -> p (r d)"), ident16[:])
                        ins.then_inc(L1.turned, 1)
                for h in range(2):
                    bank = ps_d[:] if h == 0 else ps_m[3][:]
                    if stage == ("scores0", "scores1_turn_p0")[h]:
                        pe.wait_ge(L1.qf, 2 * n + h + 1)
                        pe.wait_ge(L1.kf, 2 * n + h + 1)
                        if h == 0:
                            pe.wait_ge(L1.c32, n)
                        else:
                            pe.wait_ge(L1.pt, 2 * n)
                        for b in range(2):
                            for g in range(HALF):
                                ins = nc.tensor.matmul(bank[SEQ * b:SEQ * (b + 1), SEQ * g:SEQ * (g + 1)],
                                                       qf1[:, g, SEQ * b:SEQ * (b + 1)], kf1[:, g, SEQ * b:SEQ * (b + 1)],
                                                       start=True, stop=True)
                        ins.then_inc(L1.scores, 1)
                for h in range(2):
                    bank = ps_d[:] if h == 0 else ps_m[3][:]
                    if stage == ("mix0", "mix1")[h]:
                        pe.wait_ge(L1.pt, 2 * n + h + 1)
                        pe.wait_ge(L1.vv, 64 * (n + 1))
                        o = ps_d[:].rearrange("p (c b q) -> p c b q", c=KC, b=2)
                        for b in range(2):
                            for g in range(HALF):
                                hd = HALF * h + g
                                row = HD1 * (hd % 4)
                                for a in range(2):
                                    ins = nc.tensor.matmul(o[row:row + HD1, hd // 4, b, :], vv1[:, b, a, HD1 * hd:HD1 * (hd + 1)],
                                                           pt1[:, g, SEQ * b:SEQ * (b + 1)], start=(a == 0), stop=(a == 1))
                        ins.then_inc(L1.mixed, 1)
                    if stage == ("scores1_turn_p0", "turn_p1")[h]:
                        pe.wait_ge(L1.p_lo, 2 * n + h + 1)
                        pe.wait_ge(L1.mx0, 2 * n + h + 1)
                        for g in range(HALF):
                            ins = nc.tensor.transpose(as16(bank, HALF)[:, g, :], p1[:, g].rearrange("p h t -> p (h t)"), ident16[:])
                        ins.then_inc(L1.p_turned, 1)
                if stage == "out":
                    pe.wait_ge(L1.c_hi, n + 1)
                    pe.wait_ge(L1.rot, count_before(TABLE1, it, (stage, t), ("proj",)))
                    pe.wait_ge(L1.h_scaled, count_before(TABLE1, it, (stage, t), ("norm1", "norm2")))
                    products([(ps_pq[:, 512:1024], lambda b, k: proj1_w[:, b, k, :])],
                             lambda a, k: ctx1[:, a, k, :], range(KC), late=0, ready=(L1.c_lo, n + 1)).then_inc(L1.o, 1)

            pe.wait_ge(s_wlo, SETUP + 4)
            for s in range(SLOTS1):
                for stage, t in TABLE1[s]:
                    attn1(stage, 0, t)
            pe.wait_ge(s_wlo, len(groups))

            def slots1(it, both):
                for s in range(SLOTS1):
                    for kind, j, first, last, _ in JOBS1[s]:
                        if kind == "up":
                            if j == 0 and first == 0:
                                pe.wait_ge(L1.h_lo, (it + 1) * len(NORMS1))
                            if j >= 2:
                                pe.wait_ge(L1.u, it * IC + j - 1)
                            else:
                                pe.wait_ge(L1.d_b, tile(it, 0))
                            ins = products([(ps_m[j % 2][:], lambda b, k: h_mlp[:, b, k, :])],
                                           lambda a, k: fc1_w[:, a, k, P * j:P * (j + 1)], range(first, last),
                                           first=(first == 0), last=(last == KC))
                            if last == KC:
                                ins.then_inc(L1.up, 1)
                        else:
                            pe.wait_ge(L1.m_lo, it * IC + last)
                            if first == 0:
                                pe.wait_ge(L1.u, (it + 1) * IC)
                                if j >= 2:
                                    pe.wait_ge(L1.d_b, tile(it, j) - 1)
                            ins = products([(ps_m[j % 2][:], lambda b, k: fc2_w[:, b, k, :])],
                                           lambda a, k: inner[:, a, k, P * j:P * (j + 1)], range(first, last),
                                           first=(first == 0), last=(last == IC))
                            if last == IC:
                                ins.then_inc(L1.down, 1)
                    if both:
                        for stage, t in TABLE1[s]:
                            attn1(stage, it + 1, t)

            with pe.Fori(0, NBLK - 1) as i:
                slots1(i, True)
            slots1(NBLK - 1, False)


def kernel(**inputs):
    import numpy as np
    import concourse.bacc as bacc
    from concourse.bass_utils import run_bass_kernel_spmd

    a = {k: np.asarray(v) for k, v in inputs.items()}

    def chunked(v, c):
        return np.ascontiguousarray(v.reshape(c, P, *v.shape[1:]).swapaxes(0, 1))

    b_ada = a["L1_cond_bada"]
    host = {
        "x": a["x"].reshape(NSEQ * SEQ, D),
        "pos": np.ascontiguousarray(a["pos_BxS"].reshape(NBLK * TILES, P).T),
        "cond_t": chunked(np.ascontiguousarray(a["cond_2048"].T), KC),
        "mask": a["mask_1x1xSxS_ff0"].reshape(SEQ, SEQ),
        "ln_w": np.concatenate([chunked(a["L0_cond_ln1_w"], KC), chunked(a["L0_cond_ln2_w"], KC)], axis=1),
        "tw_t": np.stack([a["L0_cond_ln1_tw"].T, a["L0_cond_ln2_tw"].T]),
        "wqkv0_t": np.concatenate([a["L0_cond_Wq"].T, a["L0_cond_Wk"].T, a["L0_cond_Wv"].T], axis=1),
        "wo0_t": a["L0_cond_Wo"].T,
        "wg_t": a["L0_cond_Wg"].T,
        "wu_t": a["L0_cond_Wu"].T,
        "wd_t": a["L0_cond_Wd"].T,
        "wqkv1_t": a["L1_cond_Wqkv"].T,
        "q_bias": a["L1_cond_q_bias"].reshape(1, D),
        "v_bias": chunked(a["L1_cond_v_bias"], KC),
        "scale_log": a["L1_cond_scale_mul_log"].reshape(1, HEADS1),
        "wproj_t": a["L1_cond_Wproj"].T,
        "b_proj": a["L1_cond_bproj"].reshape(1, D),
        "wada_t": a["L1_cond_Wada"].T,
        "b_ada": chunked(b_ada, 6 * KC),
        "b_ada_row": b_ada.reshape(6, D),
        "wfc1_t": a["L1_cond_Wfc1"].T,
        "b_fc1": chunked(a["L1_cond_bfc1"], IC),
        "wfc2_t": a["L1_cond_Wfc2"].T,
        "b_fc2": a["L1_cond_bfc2"].reshape(1, D),
    }
    nc = bacc.Bacc("TRN2", target_bir_lowering=False, num_devices=1)
    arrays, args = {}, []
    for name, v in host.items():
        v = np.ascontiguousarray(v)
        arrays[name] = v
        args.append(nc.dram_tensor(name, v.shape, mybir.dt.from_np(v.dtype), kind="ExternalInput").ap())
    out = nc.dram_tensor("out", (NSEQ * SEQ, D), F32, kind="ExternalOutput").ap()
    layers_kernel(nc, *args, out)
    r = run_bass_kernel_spmd(nc, [arrays], core_ids=[0])
    return r.results[0]["out"].reshape(NSEQ, SEQ, D)
```

```python
from contextlib import ExitStack

import concourse.bass as bass
from concourse import mybir

ALU = mybir.AluOpType
ACT = mybir.ActivationFunctionType
F32 = mybir.dt.float32
F16 = mybir.dt.float16
I32 = mybir.dt.int32
AX_X = mybir.AxisListType.X

P = 128
D = 512
KC = D // P
SEQ = 64
NSEQ = 64
BLOCK = 512
TILES = BLOCK // P
NBLK = NSEQ * SEQ // BLOCK
INTER = 2048
IC = INTER // P
HEADS0, HD0 = 8, 64
HEADS1, HD1 = 16, 32
HALF = HEADS1 // 2
QKV0 = D + 2 * HD0
EPS = 1e-6
GELU_C = 0.7978845608028654
WS = 16.0
INV = 1.0 / WS
TWO_PI = 6.283185307179586
PI_HIGH = 6.28125
PI_LOW = TWO_PI - PI_HIGH
ROUND = 12582912.0
PI_IN = 3.1415925

SLOTS0 = 24
SLOTS1 = 35


def slot_table(slots, stages, starts, stat1, norm1, stat2, norm2):
    table = [[] for _ in range(slots)]
    for t, first in enumerate(starts):
        for n, stage in enumerate(stages):
            table[first + n].append((stage, t))
    for name, at in (("norm1", norm1), ("norm2", norm2), ("stat1", stat1), ("stat2", stat2)):
        for t, s in enumerate(at):
            table[s].append((name, t))
    return table


TABLE0 = slot_table(SLOTS0, ["proj", "turn", "scores", "softmax", "turn_p", "mix", "out"],
                    [2, 6, 10, 14], [0, 4, 8, 12], [1, 5, 9, 13], [16, 18, 20, 22], [17, 19, 21, 23])
TABLE1 = slot_table(SLOTS1, ["proj", "projv", "prep0", "rest", "turn0", "scores0", "turn1",
                             "scores1_turn_p0", "mix0", "turn_p1", "mix1", "out"],
                    [2, 8, 14, 20], [0, 4, 11, 16], [1, 6, 12, 18], [21, 24, 27, 32], [23, 25, 28, 33])


def order_of(table, stages):
    return [(s, t) for slot in table for s, t in slot if s in stages]


def count_before(table, it, at, of):
    order = order_of(table, of + (at[0],))
    return it * len(order_of(table, of)) + sum(1 for s, _ in order[:order.index(at)] if s in of)


COST0 = {"norm1": 2, "norm2": 2, "proj": 14, "turn": 3, "scores": 4,
         "turn_p": -4, "mix": 3, "out": 14, "stat2": 4}
COST1 = {"norm1": 4, "norm2": 2, "proj": 24, "projv": 12, "turn0": 3, "scores0": 2,
         "scores1_turn_p0": 4, "mix0": 4, "turn_p1": 2, "mix1": 8, "out": 12, "rest": -3}


def deal(table, cost, jobs):
    total = sum(cost.get(s, 0) for slot in table for s, _ in slot) + sum(job[-1] for job in jobs)
    done, left, dealt = 0, list(jobs), []
    for n, slot in enumerate(table):
        done += sum(cost.get(s, 0) for s, _ in slot)
        dealt.append([])
        while left and (not dealt[-1] or done + left[0][-1] / 2 <= total * (n + 1) / len(table) or n == len(table) - 1):
            done += left[0][-1]
            dealt[-1].append(left.pop(0))
    return dealt


JOBS0 = deal(TABLE0, COST0, [(kind, j, 0, KC, 3 * KC) for j in range(IC) for kind in ("gate", "up")]
             + [("down", t, k, k + 4, 12) for t in range(TILES) for k in range(0, IC, 4)])
JOBS1 = deal(TABLE1, COST1, [("up", j, k, k + 2, 6) for j in range(IC) for k in (0, 2)]
             + [("down", t, k, k + 2, 6) for t in range(TILES) for k in range(0, IC, 2)])


def reading(slot):
    return sorted(slot, key=lambda at: at[0] == "projv")


def scales(slot):
    return [("scale" + s[4], t) for s, t in slot if s in ("norm1", "norm2")]


def ending(jobs, kind, last):
    return [[job[1] for job in slot if job[0] == kind and job[3] == last] for slot in jobs]


UPS0, DOWNS0 = ending(JOBS0, "up", KC), ending(JOBS0, "down", IC)
UPS1, DOWNS1 = ending(JOBS1, "up", KC), ending(JOBS1, "down", IC)

NORMS0 = order_of(TABLE0, ("norm1", "norm2"))
NORMS1 = order_of(TABLE1, ("norm1", "norm2"))


def layers_kernel(nc, x, pos, cond_t, mask, ln_w, tw_t, wqkv0_t, wo0_t, wg_t, wu_t, wd_t,
                  wqkv1_t, q_bias, v_bias, scale_log, wproj_t, b_proj, wada_t, b_ada, b_ada_row,
                  wfc1_t, b_fc1, wfc2_t, b_fc2, out):
    with ExitStack() as ctx:
        def sb(name, shape, dt):
            return ctx.enter_context(nc.sbuf_tensor(name, shape, dt))

        def sem(name):
            return ctx.enter_context(nc.semaphore(name))

        x_mid = nc.dram_tensor("x_mid", (NSEQ * SEQ, D), F32, kind="Internal").ap()
        rope_dram = nc.dram_tensor("rope_tables", (P, NBLK * TILES, 2, 32), F32, kind="Internal").ap()
        gain0_dram = nc.dram_tensor("gain0", (P, 2, KC, NSEQ), F32, kind="Internal").ap()
        mod1_dram = nc.dram_tensor("mod1", (P, 4, KC, NSEQ), F32, kind="Internal").ap()
        gamma_dram = nc.dram_tensor("gamma", (2, NSEQ, D), F32, kind="Internal").ap()

        weights = sb("weights", [P, 58368], F16)
        region_a, region_b, region_c = weights[:, 0:32768], weights[:, 32768:49152], weights[:, 49152:58368]

        def cut(ap, k):
            return ap.rearrange("p (h k n) -> p h k n", h=2, k=k)

        gate_w, up_w = cut(region_a[:, 0:16384], KC), cut(region_a[:, 16384:32768], KC)
        down_w = cut(region_b, IC)
        qkv0_w, wo0_w = cut(region_c[:, 0:5120], KC), cut(region_c[:, 5120:9216], KC)
        qkv1_w, proj1_w = cut(region_a[:, 0:12288], KC), cut(region_a[:, 12288:16384], KC)
        fc1_w, fc2_w = cut(region_a[:, 16384:32768], KC), cut(region_b, IC)

        xa = sb("x_attn", [P, TILES, D], F32)
        xm = sb("x_mlp", [P, TILES, D], F32)
        h_attn = sb("h_attn", [P, 2, 2, KC, P], F16)
        h_mlp = sb("h_mlp", [P, 2, KC, BLOCK], F16)
        inner = sb("inner", [P, 2, IC, BLOCK], F16)
        ident32 = sb("ident32", [P, P], F32)
        ident16 = sb("ident16", [P, P], F16)
        scratch = sb("scratch", [P, 8300], F32)

        taken = {"scratch": 0, "c": 0}

        def carve(n32, where="scratch"):
            at = taken[where]
            taken[where] = at + n32
            if where == "c":
                return region_c[:, 2 * at:2 * (at + n32)].bitcast(F32)
            assert at + n32 <= 8300, at + n32
            return scratch[:, at:at + n32]

        xn = carve(512)
        small = carve(256)
        stats = small[:, 0:8]
        moments = small[:, 8:10]
        rstd = small[:, 10:11]
        var_eps = small[:, 11:12]
        minus_half = small[:, 12:44]
        row_max = small[:, 44:52]
        row_sum = small[:, 52:60]
        row_inv = small[:, 60:68]
        norm_sq = small[:, 68:100]
        norm_inv = small[:, 100:132]
        sm_scale = small[:, 132:148]
        v_bias_t = small[:, 148:152]
        b_fc1_t = small[:, 152:168]
        mask_t = small[:, 168:232]
        wait_carrier = small[:, 232:233]
        eps_t = small[:, 233:234]
        eps_t0 = small[:, 234:235]
        gains = carve(128)
        base = taken["scratch"]
        act0 = carve(1024).rearrange("p (a n) -> p a n", a=2)
        qk0 = carve(8 * 2 * 64 // 2).bitcast(F16).rearrange("p (g h d) -> p g h d", g=HEADS0, h=2)
        kk0 = carve(128).bitcast(F16).rearrange("p (h r d) -> p h r d", h=2, r=2)
        rot = carve(576)
        rot2 = carve(576)
        qf0 = carve(512).bitcast(F16).rearrange("p (b g q) -> p b g q", b=2, g=HEADS0)
        kf0 = carve(128).bitcast(F16).rearrange("p (h n) -> p h n", h=2)
        v0 = carve(64).bitcast(F16).rearrange("p (h d) -> p h d", h=2)
        vv0 = carve(128).bitcast(F16).rearrange("p (b h d) -> p b h d", b=2, h=2)
        e0 = carve(512).rearrange("p (g t) -> p g t", g=8)
        p0 = carve(512).bitcast(F16).rearrange("p (g h t) -> p g h t", g=8, h=2)
        pt0 = carve(512).bitcast(F16).rearrange("p (g n) -> p g n", g=8)
        ctx0 = carve(512).bitcast(F16).rearrange("p (h c n) -> p h c n", h=2, c=KC)
        rope = carve(TILES * 64).rearrange("p (t s f) -> p t s f", t=TILES, s=2)
        cond32 = carve(256).rearrange("p (k b) -> p k b", k=KC)
        cond_cut = carve(256).bitcast(F16).rearrange("p (h k b) -> p h k b", h=2, k=KC)
        silu_cut = carve(256).bitcast(F16).rearrange("p (h k b) -> p h k b", h=2, k=KC)
        taken["scratch"] = base
        u1 = carve(1024).rearrange("p (a n) -> p a n", a=2)
        g1 = carve(1024).rearrange("p (a n) -> p a n", a=2)
        q16 = carve(512).bitcast(F16).rearrange("p (g r d) -> p g r d", g=HALF, r=4)
        k16 = carve(512).bitcast(F16).rearrange("p (g r d) -> p g r d", g=HALF, r=4)
        qf1 = carve(512).bitcast(F16).rearrange("p (g n) -> p g n", g=HALF)
        kf1 = carve(512).bitcast(F16).rearrange("p (g n) -> p g n", g=HALF)
        e1 = carve(512).rearrange("p (g t) -> p g t", g=HALF)
        ctx32 = carve(512)
        vv1 = carve(1024).bitcast(F16).rearrange("p (b h n) -> p b h n", b=2, h=2)
        v1 = carve(512).bitcast(F16).rearrange("p (h n) -> p h n", h=2)
        p1 = carve(512).bitcast(F16).rearrange("p (g h t) -> p g h t", g=HALF, h=2)
        qk1 = carve(1024, "c")
        pt1 = carve(512, "c").bitcast(F16).rearrange("p (g n) -> p g n", g=HALF)
        ctx1 = carve(512, "c").bitcast(F16).rearrange("p (h c n) -> p h c n", h=2, c=KC)
        gamma_a = carve(512, "c")
        gamma_m = carve(512, "c")
        q_bias_t = carve(512, "c")
        b_proj_t = carve(512, "c")
        b_fc2_t = carve(512, "c")
        stage_inner = [inner[:].rearrange("p h c n -> p (h c n)")[:, 4096 * n:4096 * (n + 1)].bitcast(F32)
                       for n in range(4)]
        stage_c = [region_c[:, 4096 * n:4096 * (n + 1)].bitcast(F32) for n in range(2)]
        ada_cut = xm[:].rearrange("p t n -> p (t n)").bitcast(F16).rearrange("p (h k n) -> p h k n", h=2, k=KC)
        hm_words = h_mlp[:].rearrange("p h k n -> p (h k n)").bitcast(F32)
        ang, turns = hm_words[:, 0:1024], hm_words[:, 1024:2048]
        cos_t, sin_t = turns, ang
        freq = act0[:, 0, 0:32]
        pos_i = act0[:, 0, 64:96].bitcast(I32)
        pos_f = act0[:, 0, 96:128]
        ln_w_t = act0[:, 0, 128:136]
        b_ada_t = act0[:, 0, 136:160]
        ada_f32 = act0[:, 0, 256:512].rearrange("p (c b) -> p c b", c=KC)
        gamma_row = act0[:, 1, :]
        b_ada_bc = [hm_words[0:NSEQ, 512 * n:512 * (n + 1)] for n in range(2)]

        ps_m = [ctx.enter_context(nc.psum_tensor(f"ps_m{n}", [P, 512], F32)) for n in range(4)]
        ps_pq = ctx.enter_context(nc.psum_tensor("ps_pq", [P, 1024], F32))
        ps_c = ctx.enter_context(nc.psum_tensor("ps_c", [P, 512], F32))
        ps_d = ctx.enter_context(nc.psum_tensor("ps_d", [P, 512], F32))

        def as16(ap, g):
            return ap.bitcast(F16).rearrange("p (g n) -> p g n", g=g)

        s_const = sem("constants_ready")
        s_setup_dma = sem("setup_loads")
        s_setup = sem("setup_chain")
        s_setup_act = sem("setup_chain_act")
        s_cond = sem("cond_cut_ready")
        s_rope_st = sem("rope_stored")
        s_stage = [sem(f"weights_landed{n}") for n in range(6)]
        s_whi = sem("weights_hi_cut")
        s_wlo = sem("weights_lo_cut")
        s_ada = sem("ada_products")
        s_ada_out = sem("ada_out_ready")
        s_ada_st = sem("ada_stored")
        s_l1c = sem("layer1_constants_loaded")
        s_l1b = sem("layer1_bias_rows_loaded")
        s_l1s = sem("layer1_scale_ready")

        class Layer:

            def __init__(self, n):
                def s(name):
                    return sem(f"l{n}_{name}")
                self.x_in = s("x_loaded")
                self.tables = s("gains_norm1_loaded")
                self.tables2 = s("gains_norm2_loaded")
                self.stat = s("stat_ready")
                self.var = s("var_eps_ready")
                self.rstd = s("rstd_ready")
                self.xn = s("xn_ready")
                self.nt = s("norm_transposed")
                self.h32 = s("h32_ready")
                self.h_hi = s("h_hi_ready")
                self.h_lo = s("h_lo_ready")
                self.proj = s("projected")
                self.rot = s("rotated")
                self.qk32 = s("qk32_ready")
                self.v_hi = s("v_hi_ready")
                self.v16 = s("v_cut")
                self.vv = s("v_spread")
                self.q_hi = s("q_hi_ready")
                self.k_hi = s("k_hi_ready")
                self.q_lo = s("q_lo_ready")
                self.kk = s("k_lo_ready")
                self.turned = s("qk_transposed")
                self.qf = s("q_feature_major")
                self.kf = s("k_feature_major")
                self.scores = s("scores_ready")
                self.mx = s("row_max_ready")
                self.shift = s("scores_shifted")
                self.e = s("exp_ready")
                self.sum = s("row_sum_ready")
                self.inv = s("row_inverse_ready")
                self.prob = s("probs_ready")
                self.p_hi = s("p_hi_ready")
                self.p_lo = s("p_lo_ready")
                self.p_turned = s("p_transposed")
                self.pt = s("p_key_major")
                self.mixed = s("mixed")
                self.c_hi = s("ctx_hi_ready")
                self.c_lo = s("ctx_lo_ready")
                self.o = s("out_projected")
                self.x1 = s("x_after_attention")
                self.hand = s("x_handed_over")
                self.up = s("up_done")
                self.act = s("act_done")
                self.m32 = s("inner32_ready")
                self.m_hi = s("inner_hi_ready")
                self.m_lo = s("inner_lo_ready")
                self.down = s("down_done")
                self.y = s("y_ready")
                self.y_out = s("y_stored")
                self.sq = s("qk_squared")
                if n == 0:
                    self.gated = s("act_times_gate")
                    self.rope_in = s("rope_loaded")
                else:
                    self.stat0 = s("stat_partial")
                    self.h_scaled = s("h_scaled")
                    self.projv = s("v_projected")
                    self.mx0 = s("masked_ready")
                    self.c32 = s("ctx32_ready")
                    self.o_b = s("out_biased")
                    self.o_g = s("out_gated")
                    self.u = s("u_ready")
                    self.usq = s("u_squared")
                    self.arg = s("tanh_arg_ready")
                    self.d_b = s("down_biased")
                    self.d_g = s("down_gated")
                    self.gam_a = s("gamma_attn_loaded")
                    self.gam_m = s("gamma_mlp_loaded")
                    self.normed = s("qk_normalised")
                    self.nsum = s("qk_norms_summed")
                    self.nmax = s("qk_norms_floored")
                    self.npow = s("q_norms_inverted")
                    self.npow_k = s("k_norms_inverted")
                    self.ninv = s("qk_norms_ready")

        L0, L1 = Layer(0), Layer(1)

        def first_block(it):
            return isinstance(it, int) and it == 0

        def rows(w, k, c0, n):
            return w[k * P * KC:(k + 1) * P * KC, c0:c0 + n].rearrange("(k p) n -> p k n", p=P)

        groups = [("ada", 0, rows(tw_t[0], 0, 0, D)),
                  ("ada", 1, rows(tw_t[1], 0, 0, D)),
                  ("w", qkv0_w[:, :, :, 0:512], rows(wqkv0_t, 0, 0, 512)),
                  ("w", qkv0_w[:, :, :, 512:640], rows(wqkv0_t, 0, 512, 128)),
                  ("w", wo0_w, rows(wo0_t, 0, 0, D))]
        FIRST = len(groups)
        gate_up = []
        for n in range(4):
            gate_up.append(("w", gate_w[:, :, :, 512 * n:512 * (n + 1)], rows(wg_t, 0, 512 * n, 512)))
            gate_up.append(("w", up_w[:, :, :, 512 * n:512 * (n + 1)], rows(wu_t, 0, 512 * n, 512)))
        for n, group in enumerate(gate_up):
            if n < 6:
                groups.append(("ada", 2 + n, rows(wada_t, 0, n * D, D)))
            groups.append(group)
        groups += [("w", down_w[:, :, 4 * n:4 * (n + 1), :], rows(wd_t, n, 0, D)) for n in range(4)]
        SETUP = len(groups)
        groups += [("w", qkv1_w[:, :, :, 512 * n:512 * (n + 1)], rows(wqkv1_t, 0, 512 * n, 512)) for n in range(3)]
        groups.append(("w", proj1_w, rows(wproj_t, 0, 0, D)))
        groups += [("w", fc1_w[:, :, :, 512 * n:512 * (n + 1)], rows(wfc1_t, 0, 512 * n, 512)) for n in range(4)]
        SWAP = len(groups)
        FC2_AT = 4
        CUT1 = SLOTS0 - (SWAP - SETUP)
        groups += [("w", fc2_w[:, :, 4 * n:4 * (n + 1), :], rows(wfc2_t, n, 0, D)) for n in range(4)]

        def place(g):
            if g < SETUP:
                n, k = g % 4, g // 4
                return s_stage[n], 16 * (k + 1), stage_inner[n], g - 4
            if g < SWAP:
                n, k = (g - SETUP) % 2, (g - SETUP) // 2
                return s_stage[4 + n], 16 * (k + 1), stage_c[n], g - 2 if g - 2 >= SETUP else -1
            n = g - SWAP
            before = sum(1 for q in range(SETUP) if q % 4 == n)
            return s_stage[n], 16 * (before + 1), stage_inner[n], -1

        def staged(g):
            n = groups[g][2].shape[2]
            return place(g)[2][:, 0:KC * n].rearrange("p (k n) -> p k n", k=KC)

        def dest(g, hl):
            if groups[g][0] == "ada":
                return ada_cut[:, hl]
            return groups[g][1][:, hl]

        def ada_before(g):
            return sum(1 for q in groups[:g] if q[0] == "ada")

        def tile(it, t):
            return it * TILES + t

        def norm_no(norms, it, kind, t):
            return it * len(norms) + norms.index((kind, t))

        block = ctx.enter_context(nc.Block())

        @block.sync
        def _(sp):
            count_registers = [sp.alloc_register("count_first"), sp.alloc_register("count_second")]

            def counts(*values):
                for n, r in zip(values, count_registers):
                    if not isinstance(n, int):
                        sp.reg_mov(r, n)
                return [n if isinstance(n, int) else r for n, r in zip(values, count_registers)]

            def by_block(ap, it, t):
                return ap.rearrange("(n t p) d -> n t p d", n=NBLK, t=TILES)[bass.ds(it, 1), t].rearrange("o p d -> (o p) d")

            def load_group(g):
                s, _, words, reuse = place(g)
                if reuse >= 0:
                    sp.wait_ge(s_wlo, reuse + 1)
                sp.dma_start(staged(g), groups[g][2]).then_inc(s, 16)

            def load_x(L, src, it, t):
                sp.dma_start(xa[:, t, :], by_block(src, it, t)).then_inc(L.x_in, 16)

            def spread(L, v, vv, it, t):
                cut_done, mixed = counts(tile(it, t) + 1, tile(it, t) if L is L0 else 2 * tile(it, t))
                sp.wait_ge(L.v16, cut_done)
                sp.wait_ge(L.mixed, mixed)
                for b in range(2):
                    for half in range(2):
                        sp.dma_start(vv[SEQ * half:SEQ * (half + 1), b], v[SEQ * b:SEQ * (b + 1)]).then_inc(L.vv, 16)

            def store_y(L, dst, it, t):
                sp.wait_ge(L.y, tile(it, t) + 1)
                sp.dma_start(by_block(dst, it, t), xm[:, t, :]).then_inc(L.y_out, 16)

            def hand_over(L, norms, it, t):
                if first_block(it):
                    sp.wait_ge(L.x1, tile(it, t) + 1)
                else:
                    attended, left = counts(tile(it, t) + 1, 16 * (tile(it, t) - TILES + 1))
                    sp.wait_ge(L.x1, attended)
                    sp.wait_ge(L.y_out, left)
                sp.dma_start(xm[:, t, :], xa[:, t, :]).then_inc(L.hand, 16)

            def next_x(L, norms, src, it, t):
                handed, normed = counts(16 * (tile(it, t) + 1), norm_no(norms, it, "norm2", t) + 1)
                sp.wait_ge(L.hand, handed)
                sp.wait_ge(L.xn, normed)
                load_x(L, src, it + 1, t)

            def move_on(L, norms, src, it, t, more):
                hand_over(L, norms, it, t)
                if more:
                    next_x(L, norms, src, it, t)

            def gains_of(L, dram, it, kind):
                for j in range(1 if L is L0 else 2):
                    dst = gains.rearrange("p (k c b) -> p k c b", k=4, c=KC)[:, 2 * j + kind]
                    src = dram[:, 2 * j + kind].rearrange("p c (n b) -> n p c b", n=NBLK)[bass.ds(it, 1)]
                    sp.dma_start(dst, src.rearrange("o p c b -> (o p) c b")).then_inc(L.tables if kind == 0 else L.tables2, 16)

            def rope_of(it):
                sp.dma_start(rope.rearrange("p t s f -> p (t s f)"), rope_dram.rearrange("p (n t) s f -> p n t s f", n=NBLK)[:, bass.ds(it, 1)].rearrange("p o t s f -> p (o t s f)")).then_inc(L0.rope_in, 16)

            def next_tables(L, dram, norms, it):
                normed, rotated = counts(norm_no(norms, it, "norm1", TILES - 1) + 1, tile(it, TILES))
                sp.wait_ge(L.h32, normed)
                sp.wait_ge(L.rot, rotated)
                gains_of(L, dram, it + 1, 0)
                if L is L0:
                    rope_of(it + 1)

            def gamma(L, which, dst, s, it, t):
                for b in range(2):
                    row = gamma_dram[which].rearrange("(n s) d -> n s d", n=NBLK)[bass.ds(it, 1), 2 * t + b, :]
                    sp.dma_start(dst[SEQ * b:SEQ * (b + 1), :], row.to_broadcast([SEQ, D])).then_inc(s, 16)

            sp.dma_start(pos_i, pos).then_inc(s_setup_dma, 16)
            sp.dma_start(ln_w_t, ln_w).then_inc(s_setup_dma, 16)
            sp.dma_start(b_ada_t, b_ada).then_inc(s_setup_dma, 16)
            sp.dma_start(cond32, cond_t).then_inc(s_setup_dma, 16)
            for g in range(2):
                load_group(g)
            for t in range(TILES):
                load_x(L0, x, 0, t)
            for g in range(2, FIRST):
                load_group(g)
            sp.wait_ge(s_setup, 17)
            sp.dma_start(rope_dram[:, :, 0, :], cos_t.rearrange("p (t f) -> p t f", f=32)).then_inc(s_rope_st, 16)
            sp.dma_start(rope_dram[:, :, 1, :], sin_t.rearrange("p (t f) -> p t f", f=32)).then_inc(s_rope_st, 16)
            sp.wait_ge(s_rope_st, 32)
            for n in range(2):
                sp.dma_start(b_ada_bc[n], b_ada_row[n:n + 1, :].to_broadcast([NSEQ, D])).then_inc(s_setup_dma, 16)

            def store_ada(n):
                sp.wait_ge(s_ada_out, n + 1)
                if n < 2:
                    sp.dma_start(gain0_dram[:, n], ada_f32).then_inc(s_ada_st, 16)
                elif n < 4:
                    sp.dma_start(gamma_dram[n - 2], gamma_row[0:NSEQ, :]).then_inc(s_ada_st, 16)
                else:
                    sp.dma_start(mod1_dram[:, n - 4], ada_f32).then_inc(s_ada_st, 16)

            load_group(FIRST)
            store_ada(0)
            store_ada(1)
            load_group(FIRST + 1)
            sp.wait_ge(s_ada_st, 16 * 2)
            gains_of(L0, gain0_dram, 0, 0)
            gains_of(L0, gain0_dram, 0, 1)
            rope_of(0)
            for s in range(SLOTS0):
                g = FIRST + s
                if g + 2 < SETUP:
                    load_group(g + 2)
                if s > 0 and g - 1 < SETUP and groups[g - 1][0] == "ada":
                    store_ada(groups[g - 1][1])
                for stage, t in TABLE0[s]:
                    if stage == "turn":
                        spread(L0, v0, vv0, 0, t)
                        if t == TILES - 1:
                            next_tables(L0, gain0_dram, NORMS0, 0)
            for t in range(TILES):
                hand_over(L0, NORMS0, 0, t)
                next_x(L0, NORMS0, x, 0, t)

            def slots0(it, more):
                sp.wait_ge(L0.h32, (it + 1) * len(NORMS0))
                gains_of(L0, gain0_dram, it + 1, 1)
                for s in range(SLOTS0):
                    for stage, t in TABLE0[s]:
                        if stage == "turn":
                            spread(L0, v0, vv0, it + 1, t)
                            if t == TILES - 1 and more:
                                next_tables(L0, gain0_dram, NORMS0, it + 1)
                    for t in DOWNS0[s]:
                        store_y(L0, x_mid, it, t)
                        move_on(L0, NORMS0, x, it + 1, t, more)

            slots0(0, True)
            with sp.Fori(1, NBLK - 2) as i:
                slots0(i, True)
            slots0(NBLK - 2, False)
            for b in range(2):
                sp.dma_start(mask_t[SEQ * b:SEQ * (b + 1), :], mask).then_inc(s_l1c, 16)
            sp.dma_start(sm_scale, scale_log.to_broadcast([P, HEADS1])).then_inc(s_l1c, 16)
            sp.dma_start(v_bias_t, v_bias).then_inc(s_l1c, 16)
            sp.dma_start(b_fc1_t, b_fc1).then_inc(s_l1c, 16)

            sp.wait_ge(L0.x1, TILES * NBLK)
            for g in range(SETUP, SETUP + 2):
                load_group(g)
            sp.wait_ge(L0.hand, 16 * TILES * NBLK)
            sp.wait_ge(L0.xn, len(NORMS0) * NBLK)
            sp.wait_ge(L0.y_out, 16 * TILES)
            for t in range(TILES):
                load_x(L1, x_mid, 0, t)
            sp.wait_ge(L0.h32, len(NORMS0) * NBLK)
            sp.wait_ge(s_ada_st, 16 * 8)
            for kind in range(2):
                gains_of(L1, mod1_dram, 0, kind)
            for s in range(SLOTS0):
                g = SETUP + s - CUT1 + 2
                if SETUP + 2 <= g < SWAP:
                    load_group(g)
                for t in DOWNS0[s]:
                    store_y(L0, x_mid, NBLK - 1, t)
            sp.wait_ge(s_wlo, SWAP)
            for dst, src in ((q_bias_t, q_bias), (b_proj_t, b_proj), (b_fc2_t, b_fc2)):
                sp.dma_start(dst, src.to_broadcast([P, D])).then_inc(s_l1b, 16)
            sp.wait_ge(L0.y_out, 16 * TILES * NBLK)
            sp.wait_ge(L0.down, NBLK * TILES)
            for g in range(SWAP, len(groups)):
                load_group(g)

            def attn1(stage, it, t, more):
                if stage == "mix0":
                    sp.wait_ge(L1.o_g, tile(it, t))
                    gamma(L1, 0, gamma_a, L1.gam_a, it, t)
                if stage == "scores0":
                    spread(L1, v1, vv1, it, t)
                    if t == TILES - 1 and more:
                        next_tables(L1, mod1_dram, NORMS1, it)

            for s in range(SLOTS1):
                for stage, t in reading(TABLE1[s]):
                    attn1(stage, 0, t, True)
            for t in range(TILES):
                hand_over(L1, NORMS1, 0, t)
                next_x(L1, NORMS1, x_mid, 0, t)

            def slots1(it, both, more):
                if both:
                    sp.wait_ge(L1.h32, (it + 1) * len(NORMS1))
                    gains_of(L1, mod1_dram, it + 1, 1)
                for s in range(SLOTS1):
                    if both:
                        for stage, t in reading(TABLE1[s]):
                            attn1(stage, it + 1, t, more)
                    for kind, t, k, _, _ in JOBS1[s]:
                        if kind == "down" and k == 0:
                            sp.wait_ge(L1.d_g, tile(it, t))
                            gamma(L1, 1, gamma_m, L1.gam_m, it, t)
                    for t in DOWNS1[s]:
                        store_y(L1, out, it, t)
                        if both:
                            move_on(L1, NORMS1, x_mid, it + 1, t, more)

            slots1(0, True, True)
            with sp.Fori(1, NBLK - 2) as i:
                slots1(i, True, True)
            slots1(NBLK - 2, True, False)
            slots1(NBLK - 1, False, False)
            sp.wait_ge(L1.y_out, 16 * TILES * NBLK)

        @block.gpsimd
        def _(pool):
            for n, m in enumerate((ident32, ident16)):
                nc.gpsimd.memset(m[:], 0.0).then_inc(s_const, 1)
                pool.wait_ge(s_const, 2 * n + 1)
                nc.gpsimd.affine_select(out=m[:], in_=m[:], compare_op=ALU.not_equal, fill=1.0, base=0,
                                        pattern=[[-1, P]], channel_multiplier=1).then_inc(s_const, 1)
            nc.gpsimd.memset(minus_half, -0.5).then_inc(s_const, 1)
            nc.gpsimd.memset(eps_t, EPS).then_inc(s_const, 1)
            nc.gpsimd.memset(eps_t0, D * EPS).then_inc(s_const, 1)
            for n in range(32):
                inv_freq = float(1.0 / 10000.0 ** (2.0 * n / HD0))
                nc.gpsimd.memset(freq[:, n:n + 1], inv_freq).then_inc(s_const, 1)

            def norm(L, norms, it, kind, t):
                n = norm_no(norms, it, kind, t)
                pool.wait_ge(L.stat, n + 1)
                value = stats[:, 0:1] if L is L0 else moments[:, 1:2]
                nc.gpsimd.tensor_tensor(var_eps, value, eps_t[:, 0:1] if L is L1 else eps_t0, ALU.add).then_inc(L.var, 1)
                pool.wait_ge(L.var, n + 1)
                nc.gpsimd.tensor_tensor(rstd, var_eps, minus_half[:, 0:1], ALU.pow).then_inc(L.rstd, 1)

            def norm_lo(L, norms, it, kind, t):
                n = norm_no(norms, it, kind, t)
                pool.wait_ge(L.h_hi, n + 1)
                dst = h_attn[:, t % 2, 1] if kind == "norm1" else h_mlp[:, 1, :, t * P:(t + 1) * P]
                hi = h_attn[:, t % 2, 0] if kind == "norm1" else h_mlp[:, 0, :, t * P:(t + 1) * P]
                nc.gpsimd.tensor_tensor(dst, xn.rearrange("p (c n) -> p c n", c=KC), hi, ALU.subtract).then_inc(L.h_lo, 1)

            def attn0(stage, it, t):
                n = tile(it, t)
                if stage in ("stat1", "stat2"):
                    norm(L0, NORMS0, it, "norm" + stage[4], t)
                if stage in ("norm1", "norm2"):
                    norm_lo(L0, NORMS0, it, stage, t)
                if stage == "proj":
                    pool.wait_ge(L0.q_hi, n + 1)
                    nc.gpsimd.tensor_tensor(qk0[:, :, 1, :], rot[:, 0:512].rearrange("p (g d) -> p g d", g=HEADS0),
                                            qk0[:, :, 0, :], ALU.subtract).then_inc(L0.q_lo, 1)
                    pool.wait_ge(L0.k_hi, n + 1)
                    nc.gpsimd.tensor_tensor(kk0[:, 1], rot[:, 512:576].unsqueeze(1).to_broadcast([P, 2, HD0]), kk0[:, 0],
                                            ALU.subtract).then_inc(L0.kk, 1)
                if stage == "softmax":
                    pool.wait_ge(L0.p_hi, n + 1)
                    nc.gpsimd.tensor_tensor(p0[:, :, 1, :], e0, p0[:, :, 0, :], ALU.subtract).then_inc(L0.p_lo, 1)

            def mlp_lo(L, src, it, j):
                pool.wait_ge(L.m_hi, it * IC + j + 1)
                nc.gpsimd.tensor_tensor(inner[:, 1, j, :], src[:, j % 2, :], inner[:, 0, j, :],
                                        ALU.subtract).then_inc(L.m_lo, 1)

            pool.wait_ge(s_const, 39)
            for s in range(SLOTS0):
                for stage, t in TABLE0[s]:
                    attn0(stage, 0, t)

            def slots0(it, both):
                for s in range(SLOTS0):
                    if both:
                        for stage, t in TABLE0[s]:
                            attn0(stage, it + 1, t)
                    for j in UPS0[s]:
                        mlp_lo(L0, act0, it, j)

            slots0(0, True)
            with pool.Fori(1, NBLK - 1) as i:
                slots0(i, True)
            slots0(NBLK - 1, False)

            def attn1(stage, it, t):
                n = tile(it, t)
                if stage in ("stat1", "stat2"):
                    norm(L1, NORMS1, it, "norm" + stage[4], t)
                if stage in ("norm1", "norm2"):
                    norm_lo(L1, NORMS1, it, stage, t)
                if stage == "proj":
                    pool.wait_ge(L1.nmax, 2 * n + 1)
                    nc.gpsimd.tensor_tensor(norm_inv[:, 0:HEADS1], norm_sq[:, 0:HEADS1], minus_half[:, 0:HEADS1],
                                            ALU.pow).then_inc(L1.npow, 1)
                    pool.wait_ge(L1.nmax, 2 * n + 2)
                    nc.gpsimd.tensor_tensor(norm_inv[:, HEADS1:], norm_sq[:, HEADS1:], minus_half[:, HEADS1:],
                                            ALU.pow).then_inc(L1.npow_k, 1)
                    pool.wait_ge(L1.npow, n + 1)
                    pool.wait_ge(s_l1s, 3)
                    nc.gpsimd.tensor_tensor(norm_inv[:, 0:HEADS1], norm_inv[:, 0:HEADS1], sm_scale,
                                            ALU.mult).then_inc(L1.ninv, 1)
                for h in range(2):
                    if stage == ("prep0", "turn0")[h]:
                        by_head = lambda at: qk1[:, at:at + 256].rearrange("p (g d) -> p g d", g=HALF).unsqueeze(2).to_broadcast([P, HALF, 2, HD1])
                        pool.wait_ge(L1.q_hi, 2 * n + h + 1)
                        nc.gpsimd.tensor_tensor(q16[:, :, 1:4:2, :], by_head(256 * h), q16[:, :, 0:4:2, :], ALU.subtract).then_inc(L1.q_lo, 1)
                        pool.wait_ge(L1.k_hi, 2 * n + h + 1)
                        nc.gpsimd.tensor_tensor(k16[:, :, 2:4, :], by_head(512 + 256 * h), k16[:, :, 0:2, :], ALU.subtract).then_inc(L1.kk, 1)
                    if stage == ("turn1", "mix0")[h]:
                        pool.wait_ge(L1.p_hi, 2 * n + h + 1)
                        nc.gpsimd.tensor_tensor(p1[:, :, 1, :], e1, p1[:, :, 0, :], ALU.subtract).then_inc(L1.p_lo, 1)
                if stage == "out":
                    pool.wait_ge(L1.o_g, n + 1)
                    nc.gpsimd.tensor_tensor(xa[:, t, :], xa[:, t, :], ctx32, ALU.add).then_inc(L1.x1, 1)

            for s in range(SLOTS1):
                for stage, t in reading(TABLE1[s]):
                    attn1(stage, 0, t)

            def slots1(it, both):
                for s in range(SLOTS1):
                    if both:
                        for stage, t in reading(TABLE1[s]):
                            attn1(stage, it + 1, t)
                    for j in UPS1[s]:
                        mlp_lo(L1, u1, it, j)

            slots1(0, True)
            with pool.Fori(1, NBLK - 1) as i:
                slots1(i, True)
            slots1(NBLK - 1, False)

        @block.scalar
        def _(act):
            act.wait_ge(s_setup_dma, 64)
            nc.scalar.copy(cond_cut[:, 0], cond32).then_inc(s_setup_act, 1)
            nc.scalar.activation(xn[:, 0:256].rearrange("p (k b) -> p k b", k=KC), cond32, ACT.Tanh, scale=0.5).then_inc(s_setup_act, 1)

            def cut_hi(g):
                s, n, _, _ = place(g)
                act.wait_ge(s, n)
                if groups[g][0] == "ada":
                    act.wait_ge(s_ada, ada_before(g))
                if SETUP <= g < SWAP:
                    act.wait_ge(L0.up, NBLK * IC)
                if g >= SWAP:
                    act.wait_ge(L0.down, NBLK * TILES)
                nc.scalar.mul(dest(g, 0), staged(g), WS).then_inc(s_whi, 1)

            cut_hi(0)
            act.wait_ge(s_setup, 15)
            nc.scalar.activation(sin_t, ang, ACT.Sin).then_inc(s_setup_act, 1)
            nc.scalar.activation(cos_t, turns, ACT.Sin).then_inc(s_setup_act, 1)
            for g in range(1, FIRST):
                cut_hi(g)

            def norm_square(it, kind, t):
                n = norm_no(NORMS0, it, kind, t)
                act.wait_ge(L0.h_lo, n)
                if kind == "norm1":
                    act.wait_ge(L0.x_in, 16 * (tile(it, t) + 1))
                else:
                    act.wait_ge(L0.x1, tile(it, t) + 1)
                nc.scalar.activation(xn, xa[:, t, :], ACT.Square, accum_out=stats[:, 0:1]).then_inc(L0.stat, 1)

            def norm_hi(L, norms, it, kind, t):
                n = norm_no(norms, it, kind, t)
                act.wait_ge(L.h32, n + 1)
                if kind == "norm1":
                    if t > 0 or not first_block(it):
                        act.wait_ge(L.proj if L is L0 else L.projv, tile(it, t) - 1)
                    dst = h_attn[:, t % 2, 0]
                else:
                    act.wait_ge(L.up, it * IC)
                    dst = h_mlp[:, 0, :, t * P:(t + 1) * P]
                nc.scalar.copy(dst, xn.rearrange("p (c n) -> p c n", c=KC)).then_inc(L.h_hi, 1)

            def attn0(stage, it, t):
                n = tile(it, t)
                if stage in ("stat1", "stat2"):
                    norm_square(it, "norm" + stage[4], t)
                if stage in ("norm1", "norm2"):
                    norm_hi(L0, NORMS0, it, stage, t)
                if stage == "proj":
                    act.wait_ge(L0.rot, n + 1)
                    act.wait_ge(L0.turned, n)
                    nc.scalar.copy(qk0[:, :, 0, :], rot[:, 0:512].rearrange("p (g d) -> p g d", g=HEADS0)).then_inc(L0.q_hi, 1)
                    nc.scalar.copy(kk0[:, 0], rot[:, 512:576].unsqueeze(1).to_broadcast([P, 2, HD0])).then_inc(L0.k_hi, 1)
                if stage == "turn":
                    act.wait_ge(L0.turned, n + 1)
                    act.wait_ge(L0.scores, n)
                    nc.scalar.copy(kf0, as16(ps_pq[:, 0:128], 2)).then_inc(L0.kf, 1)
                if stage == "scores":
                    act.wait_ge(L0.shift, n + 1)
                    nc.scalar.activation(e0, e0, ACT.Exp, scale=float(HD0) ** -0.5).then_inc(L0.e, 1)
                if stage == "softmax":
                    act.wait_ge(L0.prob, n + 1)
                    act.wait_ge(L0.p_turned, n)
                    nc.scalar.copy(p0[:, :, 0, :], e0).then_inc(L0.p_hi, 1)
                if stage == "turn_p":
                    act.wait_ge(L0.p_turned, n + 1)
                    act.wait_ge(L0.mixed, n)
                    nc.scalar.copy(pt0, as16(ps_d[:], 8)).then_inc(L0.pt, 1)
                if stage == "mix":
                    act.wait_ge(L0.mixed, n + 1)
                    act.wait_ge(L0.o, n)
                    nc.scalar.copy(ctx0[:, 0], ps_d[:].rearrange("p (c n) -> p c n", c=KC)).then_inc(L0.c_hi, 1)

            for s in range(SLOTS0):
                for stage, t in TABLE0[s]:
                    attn0(stage, 0, t)
                if FIRST + s < SETUP:
                    cut_hi(FIRST + s)

            def mlp_hi(L, src, it, j):
                act.wait_ge(L.m32, it * IC + j + 1)
                act.wait_ge(L.down, tile(it, 0))
                nc.scalar.copy(inner[:, 0, j, :], src[:, j % 2, :]).then_inc(L.m_hi, 1)

            def slots0(it, both):
                for s in range(SLOTS0):
                    for j in UPS0[s]:
                        act.wait_ge(L0.up, it * IC + j + 1)
                        act.wait_ge(L0.m_lo, it * IC + (j - 1 if j > 1 else 0))
                        nc.scalar.activation(act0[:, j % 2, :], ps_m[2 * (j % 2)][:], ACT.Tanh,
                                             scale=0.5 * INV).then_inc(L0.act, 1)
                    if both:
                        for stage, t in TABLE0[s]:
                            attn0(stage, it + 1, t)
                    for j in UPS0[s]:
                        mlp_hi(L0, act0, it, j)
                    if not both and s >= CUT1:
                        cut_hi(SETUP + s - CUT1)

            slots0(0, True)
            with act.Fori(1, NBLK - 1) as i:
                slots0(i, True)
            slots0(NBLK - 1, False)

            act.wait_ge(s_l1s, 1)
            nc.scalar.activation(sm_scale, sm_scale, ACT.Exp).then_inc(s_l1s, 2)

            def attn1(stage, it, t):
                n = tile(it, t)
                if stage in ("norm1", "norm2"):
                    norm_hi(L1, NORMS1, it, stage, t)
                if stage == "proj":
                    act.wait_ge(L1.proj, n + 1)
                    act.wait_ge(L1.k_hi, 2 * n)
                    act.wait_ge(L1.kk, 2 * n)
                    nc.scalar.mul(qk1[:, 512:1024], ps_pq[:, 512:1024], INV).then_inc(L1.rot, 1)
                    act.wait_ge(L1.qk32, n + 1)
                    act.wait_ge(L1.h_lo, count_before(TABLE1, it, (stage, t), ("norm1", "norm2")))
                    nc.scalar.activation(xn, qk1[:, 0:512], ACT.Square).then_inc(L1.sq, 1)
                    act.wait_ge(L1.rot, n + 1)
                    act.wait_ge(L1.nsum, 2 * n + 1)
                    nc.scalar.activation(xn, qk1[:, 512:1024], ACT.Square).then_inc(L1.sq, 1)
                if stage == "projv":
                    act.wait_ge(L1.projv, n + 1)
                    act.wait_ge(L1.vv, 64 * n)
                    nc.scalar.mul(v1[:, 0], ps_m[2][:], INV).then_inc(L1.v_hi, 1)
                for h in range(2):
                    if stage == ("turn0", "turn1")[h]:
                        act.wait_ge(L1.turned, 2 * n + h + 1)
                        act.wait_ge(L1.scores, 2 * n + h)
                        nc.scalar.copy(kf1, as16(ps_m[2][:], HALF)).then_inc(L1.kf, 1)
                for h in range(2):
                    if stage == ("prep0", "turn0")[h]:
                        act.wait_ge(L1.normed, n + 1)
                        act.wait_ge(L1.turned, 2 * n + h)
                        by_head = lambda at: qk1[:, at:at + 256].rearrange("p (g d) -> p g d", g=HALF).unsqueeze(2).to_broadcast([P, HALF, 2, HD1])
                        nc.scalar.copy(q16[:, :, 0:4:2, :], by_head(256 * h)).then_inc(L1.q_hi, 1)
                        nc.scalar.copy(k16[:, :, 0:2, :], by_head(512 + 256 * h)).then_inc(L1.k_hi, 1)
                    if stage == ("scores0", "scores1_turn_p0")[h]:
                        act.wait_ge(L1.shift, 2 * n + h + 1)
                        nc.scalar.activation(e1, e1, ACT.Exp).then_inc(L1.e, 1)
                    if stage == ("turn1", "mix0")[h]:
                        act.wait_ge(L1.prob, 2 * n + h + 1)
                        act.wait_ge(L1.p_turned, 2 * n + h)
                        nc.scalar.copy(p1[:, :, 0, :], e1).then_inc(L1.p_hi, 1)
                    if stage == ("scores1_turn_p0", "turn_p1")[h]:
                        act.wait_ge(L1.p_turned, 2 * n + h + 1)
                        act.wait_ge(L1.mixed, 2 * n + h)
                        bank = ps_d[:] if h == 0 else ps_m[3][:]
                        nc.scalar.copy(pt1, as16(bank, HALF)).then_inc(L1.pt, 1)
                if stage == "mix1":
                    act.wait_ge(L1.c32, n + 1)
                    act.wait_ge(L1.o, n)
                    nc.scalar.copy(ctx1[:, 0], ctx32.rearrange("p (c n) -> p c n", c=KC)).then_inc(L1.c_hi, 1)

            for s in range(SLOTS1):
                for stage, t in reading(TABLE1[s]):
                    attn1(stage, 0, t)
                if FC2_AT <= s < FC2_AT + 4:
                    cut_hi(SWAP + s - FC2_AT)

            def mlp_tanh(it, j):
                act.wait_ge(L1.arg, it * IC + j + 1)
                nc.scalar.activation(g1[:, j % 2, :], g1[:, j % 2, :], ACT.Tanh).then_inc(L1.act, 1)

            def slots1(it, both):
                for s in range(SLOTS1):
                    for j in UPS1[s]:
                        act.wait_ge(L1.up, it * IC + j + 1)
                        act.wait_ge(L1.m_lo, it * IC + (j - 1 if j > 1 else 0))
                        if j == 0:
                            act.wait_ge(L1.y, tile(it, 0))
                        nc.scalar.activation(u1[:, j % 2, :], ps_m[j % 2][:], ACT.Identity, bias=b_fc1_t[:, j:j + 1],
                                             scale=INV).then_inc(L1.u, 1)
                        act.wait_ge(L1.u, it * IC + j + 1)
                        nc.scalar.activation(g1[:, j % 2, :], u1[:, j % 2, :], ACT.Square,
                                             scale=(0.044715 * GELU_C) ** 0.5).then_inc(L1.usq, 1)
                    if both:
                        for stage, t in reading(TABLE1[s]):
                            attn1(stage, it + 1, t)
                    for j in UPS1[s]:
                        mlp_tanh(it, j)
                        mlp_hi(L1, u1, it, j)

            slots1(0, True)
            with act.Fori(1, NBLK - 1) as i:
                slots1(i, True)
            slots1(NBLK - 1, False)

        @block.vector
        def _(dve):
            steps = [0]

            def link(ins):
                steps[0] += 1
                ins.then_inc(s_setup, 1)
                dve.wait_ge(s_setup, steps[0])

            dve.wait_ge(s_setup_dma, 64)
            dve.wait_ge(s_setup_act, 2)
            half_silu = xn[:, 0:256].rearrange("p (k b) -> p k b", k=KC)
            link(nc.vector.tensor_tensor(cond_cut[:, 1], cond32, cond_cut[:, 0], ALU.subtract))
            link(nc.vector.scalar_tensor_tensor(half_silu, half_silu, 1.0, cond32, ALU.add, ALU.mult))
            link(nc.vector.tensor_scalar(half_silu, half_silu, 0.5, None, ALU.mult))
            link(nc.vector.tensor_copy(silu_cut[:, 0], half_silu))
            nc.vector.tensor_tensor(silu_cut[:, 1], half_silu, silu_cut[:, 0], ALU.subtract).then_inc(s_cond, 1)

            def cut_lo(g):
                dve.wait_ge(s_whi, g + 1)
                nc.vector.scalar_tensor_tensor(dest(g, 1), staged(g), WS, dest(g, 0), ALU.mult,
                                               ALU.subtract).then_inc(s_wlo, 1)

            def ada_of(g):
                if g < SETUP and groups[g][0] == "ada":
                    ada(groups[g][1])

            def ada(n):
                dve.wait_ge(s_ada, n + 1)
                dve.wait_ge(s_ada_st, 16 * n)
                bank = ps_m[n % 2]
                feat = bank[:, 0:256].rearrange("p (c b) -> p c b", c=KC)
                if n < 2:
                    link(nc.vector.tensor_scalar(ada_f32, feat, INV, 1.0, ALU.mult, ALU.add))
                    w = ln_w_t[:, 4 * n:4 * (n + 1)].unsqueeze(2).to_broadcast([P, KC, NSEQ])
                    nc.vector.tensor_tensor(ada_f32, ada_f32, w, ALU.mult).then_inc(s_ada_out, 1)
                elif n < 4:
                    dve.wait_ge(s_setup_dma, 64 + 32)
                    nc.vector.scalar_tensor_tensor(gamma_row[0:NSEQ, :], bank[0:NSEQ, :], INV, b_ada_bc[n - 2], ALU.mult,
                                                   ALU.add).then_inc(s_ada_out, 1)
                else:
                    b = b_ada_t[:, 4 * (n - 2):4 * (n - 1)].unsqueeze(2).to_broadcast([P, KC, NSEQ])
                    ins = nc.vector.scalar_tensor_tensor(ada_f32, feat, INV, b, ALU.mult, ALU.add)
                    if n < 6:
                        link(ins)
                        ins = nc.vector.tensor_scalar(ada_f32, ada_f32, 1.0, None, ALU.add)
                    ins.then_inc(s_ada_out, 1)

            cut_lo(0)
            dve.wait_ge(s_const, 39)
            a3, t3 = ang.rearrange("p (t f) -> p t f", f=32), turns.rearrange("p (t f) -> p t f", f=32)
            link(nc.vector.tensor_copy(pos_f, pos_i))
            link(nc.vector.tensor_tensor(a3, pos_f.unsqueeze(2).to_broadcast([P, 32, 32]),
                                         freq.unsqueeze(1).to_broadcast([P, 32, 32]), ALU.mult))
            link(nc.vector.tensor_scalar(turns, ang, 1.0 / TWO_PI, ROUND, ALU.mult, ALU.add))
            link(nc.vector.tensor_scalar(turns, turns, ROUND, None, ALU.subtract))
            link(nc.vector.scalar_tensor_tensor(ang, turns, -PI_HIGH, ang, ALU.mult, ALU.add))
            link(nc.vector.scalar_tensor_tensor(ang, turns, -PI_LOW, ang, ALU.mult, ALU.add))
            link(nc.vector.tensor_scalar(ang, ang, PI_IN, -PI_IN, ALU.min, ALU.max))
            link(nc.vector.tensor_scalar(turns, ang, TWO_PI / 4, PI_IN, ALU.add, ALU.is_gt))
            link(nc.vector.scalar_tensor_tensor(turns, turns, -TWO_PI, ang, ALU.mult, ALU.add))
            link(nc.vector.tensor_scalar(turns, turns, TWO_PI / 4, PI_IN, ALU.add, ALU.min))
            link(nc.vector.tensor_scalar(turns, turns, -PI_IN, None, ALU.max))
            dve.wait_ge(s_setup_act, 4)
            link(nc.vector.tensor_scalar(sin_t, sin_t, INV, None, ALU.mult))
            link(nc.vector.tensor_scalar(cos_t, cos_t, INV, None, ALU.mult))
            ada_of(0)
            for g in range(1, FIRST - 1):
                cut_lo(g)
            ada_of(1)
            cut_lo(FIRST - 1)

            def gain(kind, t, shift=0):
                k = 0 if kind == "norm1" else 1
                g = gains.rearrange("p (k c b) -> p k c b", k=4, c=KC)
                return g[:, k + shift, :, 2 * t:2 * t + 2].unsqueeze(3).to_broadcast([P, KC, 2, SEQ])

            def by_seq(ap):
                return ap.rearrange("p (c b n) -> p c b n", c=KC, b=2)

            def stat0(it, kind, t):
                n = norm_no(NORMS0, it, kind, t)
                dve.wait_ge(L0.rstd, n + 1)
                nc.vector.tensor_scalar(xn, xa[:, t, :], rstd, float(D) ** 0.5, ALU.mult, ALU.mult).then_inc(L0.xn, 1)

            def norm0(it, kind, t):
                n = norm_no(NORMS0, it, kind, t)
                dve.wait_ge(L0.nt, n + 1)
                dve.wait_ge(L0.tables if kind == "norm1" else L0.tables2, 16 * (it + 1))
                nc.vector.tensor_tensor(by_seq(xn), by_seq(ps_c[:]), gain(kind, t), ALU.mult).then_inc(L0.h32, 1)

            def attn0(stage, it, t):
                n = tile(it, t)
                if stage in ("stat1", "stat2"):
                    stat0(it, "norm" + stage[4], t)
                if stage in ("norm1", "norm2"):
                    norm0(it, stage, t)
                if stage == "proj":
                    dve.wait_ge(L0.proj, n + 1)
                    dve.wait_ge(L0.kk, n)
                    dve.wait_ge(L0.rope_in, 16 * (it + 1))
                    dve.wait_ge(L0.vv, 64 * n)
                    nc.vector.tensor_scalar(v0[:, 0], ps_pq[:, 576:640], INV, None, ALU.mult).then_inc(L0.v_hi, 1)
                    q = ps_pq[:, 0:576].rearrange("p (g s f) -> p g s f", g=9, s=2)
                    r1 = rot.rearrange("p (g s f) -> p g s f", g=9, s=2)
                    r2 = rot2.rearrange("p (g s f) -> p g s f", g=9, s=2)
                    cos = rope[:, t, 0, :].unsqueeze(1).unsqueeze(1).to_broadcast([P, 9, 2, 32])
                    sin = rope[:, t, 1, :].unsqueeze(1).to_broadcast([P, 9, 32])
                    nc.vector.tensor_tensor(r1, q, cos, ALU.mult).then_inc(L0.qk32, 1)
                    nc.vector.tensor_tensor(r2[:, :, 0, :], q[:, :, 1, :], sin, ALU.mult).then_inc(L0.qk32, 1)
                    nc.vector.tensor_tensor(r2[:, :, 1, :], q[:, :, 0, :], sin, ALU.mult).then_inc(L0.qk32, 1)
                    dve.wait_ge(L0.v_hi, n + 1)
                    nc.vector.scalar_tensor_tensor(v0[:, 1], ps_pq[:, 576:640], INV, v0[:, 0], ALU.mult,
                                                   ALU.subtract).then_inc(L0.v16, 1)
                    dve.wait_ge(L0.qk32, 3 * n + 3)
                    nc.vector.tensor_tensor(r1[:, :, 0, :], r1[:, :, 0, :], r2[:, :, 0, :], ALU.subtract).then_inc(L0.sq, 1)
                    nc.vector.tensor_tensor(r1[:, :, 1, :], r1[:, :, 1, :], r2[:, :, 1, :], ALU.add).then_inc(L0.rot, 1)
                if stage == "turn":
                    dve.wait_ge(L0.turned, n + 1)
                    dve.wait_ge(L0.scores, n)
                    nc.vector.tensor_copy(qf0.rearrange("p b g q -> p g b q"),
                                          as16(ps_c[:], 8).rearrange("p g (b q) -> p g b q", b=2)).then_inc(L0.qf, 1)
                if stage == "scores":
                    exponents(L0, e0, ps_d[:], n)
                if stage == "softmax":
                    probabilities(L0, e0, n)
                if stage == "mix":
                    dve.wait_ge(L0.c_hi, n + 1)
                    nc.vector.tensor_tensor(ctx0[:, 1], ps_d[:].rearrange("p (c n) -> p c n", c=KC), ctx0[:, 0],
                                            ALU.subtract).then_inc(L0.c_lo, 1)
                if stage == "out":
                    dve.wait_ge(L0.o, n + 1)
                    nc.vector.scalar_tensor_tensor(xa[:, t, :], ps_pq[:, 0:512], INV, xa[:, t, :], ALU.mult,
                                                   ALU.add).then_inc(L0.x1, 1)

            def exponents(L, e, bank, m):
                s3 = bank.rearrange("p (g t) -> p g t", g=8)
                dve.wait_ge(L.scores, m + 1)
                dve.wait_ge(L.p_lo, m)
                if L is L1:
                    dve.wait_ge(L.sum, m)
                    nc.vector.tensor_tensor(e, s3, mask_t.unsqueeze(1).to_broadcast([P, 8, SEQ]), ALU.add).then_inc(L.mx0, 1)
                    dve.wait_ge(L.mx0, m + 1)
                    s3 = e
                nc.vector.tensor_reduce(row_max, s3, AX_X, ALU.max).then_inc(L.mx, 1)
                dve.wait_ge(L.mx, m + 1)
                nc.vector.tensor_tensor(e, s3, row_max.unsqueeze(2).to_broadcast([P, 8, SEQ]), ALU.subtract).then_inc(L.shift, 1)

            def probabilities(L, e, m):
                dve.wait_ge(L.e, m + 1)
                nc.vector.tensor_reduce(row_sum, e, AX_X, ALU.add).then_inc(L.sum, 1)
                dve.wait_ge(L.sum, m + 1)
                nc.vector.reciprocal(row_inv, row_sum).then_inc(L.inv, 1)
                dve.wait_ge(L.inv, m + 1)
                nc.vector.tensor_tensor(e, e, row_inv.unsqueeze(2).to_broadcast([P, 8, SEQ]), ALU.mult).then_inc(L.prob, 1)

            for s in range(SLOTS0):
                if s > 0:
                    ada_of(FIRST + s - 1)
                for stage, t in TABLE0[s]:
                    attn0(stage, 0, t)
                if FIRST + s < SETUP:
                    cut_lo(FIRST + s)

            def slots0(it, both):
                for s in range(SLOTS0):
                    for j in UPS0[s]:
                        dve.wait_ge(L0.act, it * IC + j + 1)
                        a = act0[:, j % 2, :]
                        nc.vector.scalar_tensor_tensor(a, a, 1.0, ps_m[2 * (j % 2)][:], ALU.add, ALU.mult).then_inc(L0.gated, 1)
                        dve.wait_ge(L0.gated, it * IC + j + 1)
                        nc.vector.scalar_tensor_tensor(a, a, 0.5 * INV * INV, ps_m[2 * (j % 2) + 1][:], ALU.mult,
                                                       ALU.mult).then_inc(L0.m32, 1)
                    if both:
                        for stage, t in TABLE0[s]:
                            attn0(stage, it + 1, t)
                    if not both and s >= CUT1:
                        cut_lo(SETUP + s - CUT1)
                    for t in DOWNS0[s]:
                        dve.wait_ge(L0.down, tile(it, t) + 1)
                        dve.wait_ge(L0.hand, 16 * (tile(it, t) + 1))
                        nc.vector.scalar_tensor_tensor(xm[:, t, :], ps_m[t % 2][:], INV, xm[:, t, :], ALU.mult,
                                                       ALU.add).then_inc(L0.y, 1)

            slots0(0, True)
            with dve.Fori(1, NBLK - 1) as i:
                slots0(i, True)
            slots0(NBLK - 1, False)

            dve.wait_ge(s_l1c, 16 * 5)
            nc.vector.tensor_scalar(sm_scale, sm_scale, 4.605170185988092, None, ALU.min).then_inc(s_l1s, 1)

            def stat1(it, kind, t):
                n = norm_no(NORMS1, it, kind, t)
                if kind == "norm1":
                    dve.wait_ge(L1.x_in, 16 * (tile(it, t) + 1))
                else:
                    dve.wait_ge(L1.x1, tile(it, t) + 1)
                nc.vector.bn_stats(stats[:, 0:6], xa[:, t, :]).then_inc(L1.stat0, 1)
                dve.wait_ge(L1.stat0, n + 1)
                nc.vector.memset(wait_carrier, 0.0)
                nc.vector.bn_aggr(moments, stats[:, 0:6]).then_inc(L1.stat, 1)

            def scale1(it, kind, t):
                n = norm_no(NORMS1, it, kind, t)
                dve.wait_ge(L1.rstd, n + 1)
                dve.wait_ge(L1.h_lo, n)
                dve.wait_ge(L1.stat, n + 1)
                nc.vector.tensor_scalar(xn, xa[:, t, :], moments[:, 0:1], rstd, ALU.subtract, ALU.mult).then_inc(L1.xn, 1)

            def norm1(it, kind, t):
                n = norm_no(NORMS1, it, kind, t)
                dve.wait_ge(L1.nt, n + 1)
                dve.wait_ge(L1.tables if kind == "norm1" else L1.tables2, 32 * (it + 1))
                nc.vector.tensor_tensor(by_seq(xn), by_seq(ps_pq[:, 0:512]), gain(kind, t), ALU.mult).then_inc(L1.h_scaled, 1)
                dve.wait_ge(L1.h_scaled, n + 1)
                nc.vector.tensor_tensor(by_seq(xn), by_seq(xn), gain(kind, t, 2), ALU.add).then_inc(L1.h32, 1)

            def attn1(stage, it, t):
                n = tile(it, t)
                if stage in ("stat1", "stat2"):
                    stat1(it, "norm" + stage[4], t)
                if stage in ("scale1", "scale2"):
                    scale1(it, "norm" + stage[5], t)
                if stage in ("norm1", "norm2"):
                    norm1(it, stage, t)
                if stage == "proj":
                    dve.wait_ge(L1.proj, n + 1)
                    dve.wait_ge(L1.q_lo, 2 * n)
                    dve.wait_ge(L1.kk, 2 * n)
                    dve.wait_ge(s_l1b, 16 * 3)
                    nc.vector.scalar_tensor_tensor(qk1[:, 0:512], ps_pq[:, 0:512], INV, q_bias_t, ALU.mult,
                                                   ALU.add).then_inc(L1.qk32, 1)
                    for which in range(2):
                        m = 2 * n + which
                        some = norm_sq[:, HEADS1 * which:HEADS1 * (which + 1)]
                        dve.wait_ge(L1.sq, m + 1)
                        nc.vector.tensor_reduce(some, xn.rearrange("p (g d) -> p g d", g=HEADS1), AX_X, ALU.add).then_inc(L1.nsum, 1)
                        dve.wait_ge(L1.nsum, m + 1)
                        nc.vector.tensor_scalar(some, some, 1e-24, None, ALU.max).then_inc(L1.nmax, 1)
                if stage == "prep0":
                    dve.wait_ge(L1.ninv, n + 1)
                    dve.wait_ge(L1.npow_k, n + 1)
                    qk = qk1.rearrange("p (g d) -> p g d", g=32)
                    nc.vector.tensor_tensor(qk, qk, norm_inv.unsqueeze(2).to_broadcast([P, 32, HD1]), ALU.mult).then_inc(L1.normed, 1)
                if stage == "projv":
                    dve.wait_ge(L1.v_hi, n + 1)
                    nc.vector.scalar_tensor_tensor(v1[:, 1], ps_m[2][:], INV, v1[:, 0], ALU.mult,
                                                   ALU.subtract).then_inc(L1.v16, 1)
                for h in range(2):
                    if stage == ("turn0", "turn1")[h]:
                        dve.wait_ge(L1.turned, 2 * n + h + 1)
                        dve.wait_ge(L1.scores, 2 * n + h)
                        nc.vector.tensor_copy(qf1, as16(ps_c[:], HALF)).then_inc(L1.qf, 1)
                    if stage == ("scores0", "scores1_turn_p0")[h]:
                        exponents(L1, e1, ps_d[:] if h == 0 else ps_m[3][:], 2 * n + h)
                    if stage == ("turn1", "mix0")[h]:
                        probabilities(L1, e1, 2 * n + h)
                if stage == "mix1":
                    dve.wait_ge(L1.mixed, 2 * n + 2)
                    dve.wait_ge(L1.x1, n)
                    nc.vector.tensor_tensor(ctx32.rearrange("p (c n) -> p c n", c=KC), ps_d[:].rearrange("p (c n) -> p c n", c=KC),
                                            v_bias_t.unsqueeze(2).to_broadcast([P, KC, P]), ALU.add).then_inc(L1.c32, 1)
                    dve.wait_ge(L1.c_hi, n + 1)
                    nc.vector.tensor_tensor(ctx1[:, 1], ctx32.rearrange("p (c n) -> p c n", c=KC), ctx1[:, 0],
                                            ALU.subtract).then_inc(L1.c_lo, 1)
                if stage == "out":
                    dve.wait_ge(L1.o, n + 1)
                    nc.vector.scalar_tensor_tensor(ctx32, ps_pq[:, 512:1024], INV, b_proj_t, ALU.mult, ALU.add).then_inc(L1.o_b, 1)
                    dve.wait_ge(L1.o_b, n + 1)
                    dve.wait_ge(L1.gam_a, 32 * (n + 1))
                    nc.vector.tensor_tensor(ctx32, ctx32, gamma_a, ALU.mult).then_inc(L1.o_g, 1)

            for s in range(SLOTS1):
                for stage, t in scales(TABLE1[s]) + reading(TABLE1[s]):
                    attn1(stage, 0, t)
                if FC2_AT <= s < FC2_AT + 4:
                    cut_lo(SWAP + s - FC2_AT)

            def gelu(it, j):
                dve.wait_ge(L1.act, it * IC + j + 1)
                u = u1[:, j % 2, :]
                nc.vector.scalar_tensor_tensor(u, g1[:, j % 2, :], 1.0, u, ALU.add, ALU.mult).then_inc(L1.m32, 1)

            def slots1(it, both):
                for s in range(SLOTS1):
                    if both:
                        for stage, t in scales(TABLE1[s]):
                            attn1(stage, it + 1, t)
                    for j in UPS1[s]:
                        dve.wait_ge(L1.usq, it * IC + j + 1)
                        g = g1[:, j % 2, :]
                        nc.vector.scalar_tensor_tensor(g, g, GELU_C, u1[:, j % 2, :], ALU.add, ALU.mult).then_inc(L1.arg, 1)
                    if both:
                        for stage, t in reading(TABLE1[s]):
                            attn1(stage, it + 1, t)
                    for j in UPS1[s]:
                        gelu(it, j)
                    for t in DOWNS1[s]:
                        m = tile(it, t)
                        dve.wait_ge(L1.down, m + 1)
                        dve.wait_ge(L1.m_lo, (it + 1) * IC)
                        dve.wait_ge(L1.y, m)
                        d = u1[:, 0, :]
                        nc.vector.scalar_tensor_tensor(d, ps_m[t % 2][:], 0.5 * INV, b_fc2_t, ALU.mult, ALU.add).then_inc(L1.d_b, 1)
                        dve.wait_ge(L1.d_b, m + 1)
                        dve.wait_ge(L1.gam_m, 32 * (m + 1))
                        nc.vector.tensor_tensor(d, d, gamma_m, ALU.mult).then_inc(L1.d_g, 1)
                        dve.wait_ge(L1.d_g, m + 1)
                        dve.wait_ge(L1.hand, 16 * (m + 1))
                        nc.vector.tensor_tensor(xm[:, t, :], xm[:, t, :], d, ALU.add).then_inc(L1.y, 1)

            slots1(0, True)
            with dve.Fori(1, NBLK - 1) as i:
                slots1(i, True)
            slots1(NBLK - 1, False)

        @block.tensor
        def _(pe):
            PASSES = ((0, 0), (0, 1), (1, 0))

            def products(jobs, left, chunks, first=True, last=True, late=None, ready=None):
                early = [p for p in PASSES if late is None or p[late] == 0]
                order = [(k, p) for k in chunks for p in early]
                order += [(k, p) for k in chunks for p in PASSES if p not in early]
                ins = None
                for n, (k, (a, b)) in enumerate(order):
                    if late is not None and n == len(early) * len(chunks):
                        pe.wait_ge(ready[0], ready[1])
                    for o, right in jobs:
                        ins = nc.tensor.matmul(o, left(a, k), right(b, k), start=(first and n == 0),
                                               stop=(last and n == len(order) - 1), skip_group_check=True)
                return ins

            def ada(g, n):
                pe.wait_ge(s_wlo, g + 1)
                pe.wait_ge(s_cond, 1)
                if n >= 2:
                    pe.wait_ge(s_ada_out, n - 1)
                bank = ps_m[n % 2]
                c = cond_cut if n < 2 else silu_cut
                if 2 <= n < 4:
                    ins = products([(bank[0:NSEQ, :], lambda b, k: ada_cut[:, b, k, :])],
                                   lambda a, k: c[:, a, k, :], range(KC))
                else:
                    for f in range(KC):
                        ins = products([(bank[:, NSEQ * f:NSEQ * (f + 1)], lambda b, k: c[:, b, k, :])],
                                       lambda a, k: ada_cut[:, a, k, P * f:P * (f + 1)], range(KC))
                ins.then_inc(s_ada, 1)

            def setup_group(g):
                if groups[g][0] == "ada":
                    ada(g, groups[g][1])

            for g in range(FIRST):
                setup_group(g)

            pe.wait_ge(s_const, 5)

            def norm(L, norms, it, kind, t):
                n = norm_no(norms, it, kind, t)
                pe.wait_ge(L.xn, n + 1)
                if L is L0:
                    pe.wait_ge(L.h32, n)
                    pe.wait_ge(L.qf, count_before(TABLE0, it, (kind, t), ("turn",)))
                    bank = ps_c[:]
                else:
                    pe.wait_ge(L.h_scaled, n)
                    pe.wait_ge(L.qk32, count_before(TABLE1, it, (kind, t), ("proj",)))
                    bank = ps_pq[:, 0:512]
                for c in range(KC):
                    ins = nc.tensor.transpose(bank[:, P * c:P * (c + 1)], xn[:, P * c:P * (c + 1)], ident32[:])
                ins.then_inc(L.nt, 1)

            def attn0(stage, it, t):
                n = tile(it, t)
                if stage in ("norm1", "norm2"):
                    norm(L0, NORMS0, it, stage, t)
                if stage == "proj":
                    pe.wait_ge(s_wlo, 4)
                    normed = norm_no(NORMS0, it, "norm1", t) + 1
                    pe.wait_ge(L0.h_hi, normed)
                    pe.wait_ge(L0.kf, n)
                    pe.wait_ge(L0.x1, count_before(TABLE0, it, (stage, t), ("out",)))
                    left = lambda a, k: h_attn[:, t % 2, a, k, :]
                    products([(ps_pq[:, 0:512], lambda b, k: qkv0_w[:, b, k, 0:512]),
                              (ps_pq[:, 512:640], lambda b, k: qkv0_w[:, b, k, 512:640])],
                             left, range(KC), late=0, ready=(L0.h_lo, normed)).then_inc(L0.proj, 1)
                if stage == "turn":
                    pe.wait_ge(L0.q_lo, n + 1)
                    pe.wait_ge(L0.kk, n + 1)
                    pe.wait_ge(L0.rot, n + 1)
                    pe.wait_ge(L0.v16, n + 1)
                    pe.wait_ge(L0.h32, count_before(TABLE0, it, (stage, t), ("norm1", "norm2")))
                    pe.wait_ge(L0.qf, n)
                    for g in range(HEADS0):
                        nc.tensor.transpose(as16(ps_c[:], 8)[:, g, :], qk0[:, g].rearrange("p h d -> p (h d)"), ident16[:])
                    for h in range(2):
                        ins = nc.tensor.transpose(as16(ps_pq[:, 0:128], 2)[:, h, :], kk0[:, h].rearrange("p r d -> p (r d)"), ident16[:])
                    ins.then_inc(L0.turned, 1)
                if stage == "scores":
                    pe.wait_ge(L0.qf, n + 1)
                    pe.wait_ge(L0.kf, n + 1)
                    pe.wait_ge(L0.c_lo, n)
                    for b in range(2):
                        for hp in range(4):
                            for h in range(2):
                                ins = nc.tensor.matmul(ps_d[:, (4 * b + hp) * SEQ:(4 * b + hp + 1) * SEQ],
                                                       qf0[:, b, 2 * hp:2 * hp + 2, :].rearrange("p g q -> p (g q)"),
                                                       kf0[:, h, SEQ * b:SEQ * (b + 1)], start=(h == 0), stop=(h == 1))
                    ins.then_inc(L0.scores, 1)
                if stage == "turn_p":
                    pe.wait_ge(L0.p_lo, n + 1)
                    pe.wait_ge(L0.shift, n + 1)
                    for g in range(8):
                        ins = nc.tensor.transpose(as16(ps_d[:], 8)[:, g, :], p0[:, g].rearrange("p h t -> p (h t)"), ident16[:])
                    ins.then_inc(L0.p_turned, 1)
                if stage == "mix":
                    pe.wait_ge(L0.pt, n + 1)
                    pe.wait_ge(L0.vv, 64 * (n + 1))
                    o = ps_d[:].rearrange("p (c b q) -> p c b q", c=KC, b=2)
                    for b in range(2):
                        for h in range(2):
                            for par in range(2):
                                ins = nc.tensor.matmul(o[SEQ * par:SEQ * (par + 1), :, b, :], vv0[:, b, h, :],
                                                       pt0[:, 4 * b:4 * b + 4, SEQ * par:SEQ * (par + 1)],
                                                       start=(h == 0), stop=(h == 1))
                    ins.then_inc(L0.mixed, 1)
                if stage == "out":
                    pe.wait_ge(s_wlo, FIRST)
                    pe.wait_ge(L0.c_hi, n + 1)
                    pe.wait_ge(L0.kf, count_before(TABLE0, it, (stage, t), ("turn",)))
                    products([(ps_pq[:, 0:512], lambda b, k: wo0_w[:, b, k, :])],
                             lambda a, k: ctx0[:, a, k, :], range(KC), late=0, ready=(L0.c_lo, n + 1)).then_inc(L0.o, 1)

            for s in range(SLOTS0):
                for stage, t in TABLE0[s]:
                    attn0(stage, 0, t)
                if FIRST + s < SETUP:
                    setup_group(FIRST + s)
            pe.wait_ge(s_wlo, SETUP)

            def slots0(it, both):
                for s in range(SLOTS0):
                    for kind, j, first, last, _ in JOBS0[s]:
                        if kind == "gate":
                            if j == 0:
                                pe.wait_ge(L0.h_lo, (it + 1) * len(NORMS0))
                            if j >= 2:
                                pe.wait_ge(L0.m32, it * IC + j - 1)
                            else:
                                pe.wait_ge(L0.y, tile(it, 0))
                        if kind == "down":
                            pe.wait_ge(L0.m_lo, it * IC + last)
                            if first == 0:
                                pe.wait_ge(L0.m32, (it + 1) * IC)
                                if j >= 2:
                                    pe.wait_ge(L0.y, tile(it, j) - 1)
                            ins = products([(ps_m[j % 2][:], lambda b, k: down_w[:, b, k, :])],
                                           lambda a, k: inner[:, a, k, P * j:P * (j + 1)], range(first, last),
                                           first=(first == 0), last=(last == IC))
                            if last == IC:
                                ins.then_inc(L0.down, 1)
                        else:
                            w, bank = (gate_w, ps_m[2 * (j % 2)]) if kind == "gate" else (up_w, ps_m[2 * (j % 2) + 1])
                            ins = products([(bank[:], lambda b, k: h_mlp[:, b, k, :])],
                                           lambda a, k: w[:, a, k, P * j:P * (j + 1)], range(first, last))
                            if kind == "up":
                                ins.then_inc(L0.up, 1)
                    if both:
                        for stage, t in TABLE0[s]:
                            attn0(stage, it + 1, t)

            slots0(0, True)
            with pe.Fori(1, NBLK - 1) as i:
                slots0(i, True)
            slots0(NBLK - 1, False)

            def attn1(stage, it, t):
                n = tile(it, t)
                if stage in ("norm1", "norm2"):
                    norm(L1, NORMS1, it, stage, t)
                if stage == "proj":
                    normed = norm_no(NORMS1, it, "norm1", t) + 1
                    pe.wait_ge(L1.h_hi, normed)
                    pe.wait_ge(L1.qk32, n)
                    pe.wait_ge(L1.h_scaled, count_before(TABLE1, it, (stage, t), ("norm1", "norm2")))
                    pe.wait_ge(L1.rot, n)
                    pe.wait_ge(L1.o_b, count_before(TABLE1, it, (stage, t), ("out",)))
                    left = lambda a, k: h_attn[:, t % 2, a, k, :]
                    products([(ps_pq[:, 512 * q:512 * (q + 1)], lambda b, k, q=q: qkv1_w[:, b, k, 512 * q:512 * (q + 1)])
                              for q in range(2)], left, range(KC), late=0, ready=(L1.h_lo, normed)).then_inc(L1.proj, 1)
                if stage == "projv":
                    left = lambda a, k: h_attn[:, t % 2, a, k, :]
                    pe.wait_ge(L1.v16, n)
                    pe.wait_ge(L1.kf, count_before(TABLE1, it, (stage, t), ("turn0", "turn1")))
                    products([(ps_m[2][:], lambda b, k: qkv1_w[:, b, k, 1024:1536])], left, range(KC)).then_inc(L1.projv, 1)
                for h in range(2):
                    if stage == ("turn0", "turn1")[h]:
                        pe.wait_ge(L1.q_lo, 2 * n + h + 1)
                        pe.wait_ge(L1.kk, 2 * n + h + 1)
                        pe.wait_ge(L1.qf, 2 * n + h)
                        pe.wait_ge(L1.kf, 2 * n + h)
                        pe.wait_ge(L1.v16, count_before(TABLE1, it, (stage, t), ("projv",)))
                        for g in range(HALF):
                            nc.tensor.transpose(as16(ps_c[:], HALF)[:, g, :], q16[:, g].rearrange("p r d -> p (r d)"), ident16[:])
                        for g in range(HALF):
                            ins = nc.tensor.transpose(as16(ps_m[2][:], HALF)[:, g, :], k16[:, g].rearrange("p r d -> p (r d)"), ident16[:])
                        ins.then_inc(L1.turned, 1)
                for h in range(2):
                    bank = ps_d[:] if h == 0 else ps_m[3][:]
                    if stage == ("scores0", "scores1_turn_p0")[h]:
                        pe.wait_ge(L1.qf, 2 * n + h + 1)
                        pe.wait_ge(L1.kf, 2 * n + h + 1)
                        if h == 0:
                            pe.wait_ge(L1.c32, n)
                        else:
                            pe.wait_ge(L1.pt, 2 * n)
                        for b in range(2):
                            for g in range(HALF):
                                ins = nc.tensor.matmul(bank[SEQ * b:SEQ * (b + 1), SEQ * g:SEQ * (g + 1)],
                                                       qf1[:, g, SEQ * b:SEQ * (b + 1)], kf1[:, g, SEQ * b:SEQ * (b + 1)],
                                                       start=True, stop=True)
                        ins.then_inc(L1.scores, 1)
                for h in range(2):
                    bank = ps_d[:] if h == 0 else ps_m[3][:]
                    if stage == ("mix0", "mix1")[h]:
                        pe.wait_ge(L1.pt, 2 * n + h + 1)
                        pe.wait_ge(L1.vv, 64 * (n + 1))
                        o = ps_d[:].rearrange("p (c b q) -> p c b q", c=KC, b=2)
                        for b in range(2):
                            for g in range(HALF):
                                hd = HALF * h + g
                                row = HD1 * (hd % 4)
                                for a in range(2):
                                    ins = nc.tensor.matmul(o[row:row + HD1, hd // 4, b, :], vv1[:, b, a, HD1 * hd:HD1 * (hd + 1)],
                                                           pt1[:, g, SEQ * b:SEQ * (b + 1)], start=(a == 0), stop=(a == 1))
                        ins.then_inc(L1.mixed, 1)
                    if stage == ("scores1_turn_p0", "turn_p1")[h]:
                        pe.wait_ge(L1.p_lo, 2 * n + h + 1)
                        pe.wait_ge(L1.mx0, 2 * n + h + 1)
                        for g in range(HALF):
                            ins = nc.tensor.transpose(as16(bank, HALF)[:, g, :], p1[:, g].rearrange("p h t -> p (h t)"), ident16[:])
                        ins.then_inc(L1.p_turned, 1)
                if stage == "out":
                    pe.wait_ge(L1.c_hi, n + 1)
                    pe.wait_ge(L1.rot, count_before(TABLE1, it, (stage, t), ("proj",)))
                    products([(ps_pq[:, 512:1024], lambda b, k: proj1_w[:, b, k, :])],
                             lambda a, k: ctx1[:, a, k, :], range(KC), late=0, ready=(L1.c_lo, n + 1)).then_inc(L1.o, 1)

            pe.wait_ge(s_wlo, SETUP + 4)
            for s in range(SLOTS1):
                for stage, t in TABLE1[s]:
                    attn1(stage, 0, t)
            pe.wait_ge(s_wlo, len(groups))

            def slots1(it, both):
                for s in range(SLOTS1):
                    for kind, j, first, last, _ in JOBS1[s]:
                        if kind == "up":
                            if j == 0 and first == 0:
                                pe.wait_ge(L1.h_lo, (it + 1) * len(NORMS1))
                            if j >= 2:
                                pe.wait_ge(L1.u, it * IC + j - 1)
                            else:
                                pe.wait_ge(L1.d_b, tile(it, 0))
                            ins = products([(ps_m[j % 2][:], lambda b, k: h_mlp[:, b, k, :])],
                                           lambda a, k: fc1_w[:, a, k, P * j:P * (j + 1)], range(first, last),
                                           first=(first == 0), last=(last == KC))
                            if last == KC:
                                ins.then_inc(L1.up, 1)
                        else:
                            pe.wait_ge(L1.m_lo, it * IC + last)
                            if first == 0:
                                pe.wait_ge(L1.u, (it + 1) * IC)
                                if j >= 2:
                                    pe.wait_ge(L1.d_b, tile(it, j) - 1)
                            ins = products([(ps_m[j % 2][:], lambda b, k: fc2_w[:, b, k, :])],
                                           lambda a, k: inner[:, a, k, P * j:P * (j + 1)], range(first, last),
                                           first=(first == 0), last=(last == IC))
                            if last == IC:
                                ins.then_inc(L1.down, 1)
                    if both:
                        for stage, t in TABLE1[s]:
                            attn1(stage, it + 1, t)

            slots1(0, True)
            with pe.Fori(1, NBLK - 1) as i:
                slots1(i, True)
            slots1(NBLK - 1, False)


def kernel(**inputs):
    import numpy as np
    import concourse.bacc as bacc
    from concourse.bass_utils import run_bass_kernel_spmd

    a = {k: np.asarray(v) for k, v in inputs.items()}

    def chunked(v, c):
        return np.ascontiguousarray(v.reshape(c, P, *v.shape[1:]).swapaxes(0, 1))

    b_ada = a["L1_cond_bada"]
    host = {
        "x": a["x"].reshape(NSEQ * SEQ, D),
        "pos": np.ascontiguousarray(a["pos_BxS"].reshape(NBLK * TILES, P).T),
        "cond_t": chunked(np.ascontiguousarray(a["cond_2048"].T), KC),
        "mask": a["mask_1x1xSxS_ff0"].reshape(SEQ, SEQ),
        "ln_w": np.concatenate([chunked(a["L0_cond_ln1_w"], KC), chunked(a["L0_cond_ln2_w"], KC)], axis=1),
        "tw_t": np.stack([a["L0_cond_ln1_tw"].T, a["L0_cond_ln2_tw"].T]),
        "wqkv0_t": np.concatenate([a["L0_cond_Wq"].T, a["L0_cond_Wk"].T, a["L0_cond_Wv"].T], axis=1),
        "wo0_t": a["L0_cond_Wo"].T,
        "wg_t": a["L0_cond_Wg"].T,
        "wu_t": a["L0_cond_Wu"].T,
        "wd_t": a["L0_cond_Wd"].T,
        "wqkv1_t": a["L1_cond_Wqkv"].T,
        "q_bias": a["L1_cond_q_bias"].reshape(1, D),
        "v_bias": chunked(a["L1_cond_v_bias"], KC),
        "scale_log": a["L1_cond_scale_mul_log"].reshape(1, HEADS1),
        "wproj_t": a["L1_cond_Wproj"].T,
        "b_proj": a["L1_cond_bproj"].reshape(1, D),
        "wada_t": a["L1_cond_Wada"].T,
        "b_ada": chunked(b_ada, 6 * KC),
        "b_ada_row": b_ada.reshape(6, D),
        "wfc1_t": a["L1_cond_Wfc1"].T,
        "b_fc1": chunked(a["L1_cond_bfc1"], IC),
        "wfc2_t": a["L1_cond_Wfc2"].T,
        "b_fc2": a["L1_cond_bfc2"].reshape(1, D),
    }
    nc = bacc.Bacc("TRN2", target_bir_lowering=False, num_devices=1)
    arrays, args = {}, []
    for name, v in host.items():
        v = np.ascontiguousarray(v)
        arrays[name] = v
        args.append(nc.dram_tensor(name, v.shape, mybir.dt.from_np(v.dtype), kind="ExternalInput").ap())
    out = nc.dram_tensor("out", (NSEQ * SEQ, D), F32, kind="ExternalOutput").ap()
    layers_kernel(nc, *args, out)
    r = run_bass_kernel_spmd(nc, [arrays], core_ids=[0])
    return r.results[0]["out"].reshape(NSEQ, SEQ, D)
```
